# Optimizing a Trainium2 kernel written in Bass

```python
import numpy as np
import jax
import jax.numpy as jnp

def _softmax(x, axis=-1):
    return jax.nn.softmax(x, axis=axis)

def _gelu(x):
    return jax.nn.gelu(x, approximate=True)

def _silu(x):
    return jax.nn.silu(x)

def _sigmoid(x):
    return jax.nn.sigmoid(x)

def _layernorm(x, axis=-1, eps=1e-05):
    m = jnp.mean(x, axis=axis, keepdims=True)
    v = jnp.var(x, axis=axis, keepdims=True)
    return (x - m) / jnp.sqrt(v + eps)

def _scatter_add(tgt, idx, src, axis=0):
    return tgt.at[idx].add(src)

def _segment_sum(src, seg, n):
    return jax.ops.segment_sum(src, seg, n)
kernel_name = 'mk_decoder_postln_d1_seqx_r2_c5ebb8'

def setup_inputs(seed: int=0):
    np.random.seed(seed)
    _w = jnp.asarray

    def _rec_inputs():
        import jax
        import jax.numpy as jnp
        _rk = jax.random.key(seed)
        x = -0.0005207 + 1.001 * jax.random.normal(jax.random.fold_in(_rk, 1), (16, 512, 512), jnp.float32)
        _lenS = 512 - jax.random.randint(jax.random.fold_in(_rk, 7), (16,), 0, max(1, 512 // 4) + 1, jnp.int32)
        _lenS2 = 77 - jax.random.randint(jax.random.fold_in(_rk, 8), (16,), 0, max(1, 77 // 4) + 1, jnp.int32)
        _ctx_1024P = jax.random.normal(jax.random.fold_in(_rk, 11), (16, 16, 512), jnp.float32)
        _ctx_1024c = jax.random.dirichlet(jax.random.fold_in(_rk, 511), 0.3 * jnp.ones((16,), jnp.float32), (16, 77))
        _ctx_1024t = jnp.einsum('bsk,bkd->bsd', _ctx_1024c, _ctx_1024P)
        _ctx_1024t = _ctx_1024t * jax.lax.rsqrt(jnp.mean(jnp.square(_ctx_1024t)) + 1e-12) * 0.953939
        ctx_1024 = 2.81802e-05 + 1.00001 * (_ctx_1024t + 0.3 * jax.random.normal(jax.random.fold_in(_rk, 611), (16, 77, 512), jnp.float32))
        _validS = jnp.arange(512)[None, :] < _lenS[:, None]
        _validS2 = jnp.arange(77)[None, :] < _lenS2[:, None]
        _causal = jnp.tril(jnp.ones((512, 512), dtype=bool))
        mask_BxSxS2_bk0 = jnp.logical_not(jnp.broadcast_to(_validS2[:, None, :], (16, 512, 77)))
        return (x, ctx_1024, mask_BxSxS2_bk0)
    x, ctx_1024, mask_BxSxS2_bk0 = _rec_inputs()

    def _L0_attn_setup():
        import jax, jax.numpy as jnp
        import numpy as np
        N_HEADS = 16
        SEG = 64
        EPS = 1e-06

        def _sigma(x):
            return jax.nn.elu(x) + 1.0

        def _infini_attention(x, W_q, W_k, W_v, W_o, beta_param):
            B, T, D = x.shape
            H = N_HEADS
            dk = D // H
            assert T % SEG == 0
            S = T // SEG

            def proj(W):
                y = (x @ W.T).reshape(B, T, H, dk).transpose(0, 2, 1, 3)
                return y.reshape(B, H, S, SEG, dk).transpose(2, 0, 1, 3, 4)
            Qs, Ks, Vs = (proj(W_q), proj(W_k), proj(W_v))
            beta = jax.nn.sigmoid(beta_param).reshape(1, H, 1, 1)
            causal = jnp.triu(jnp.ones((SEG, SEG), dtype=bool), k=1)
            inv_sqrt_dk = 1.0 / jnp.sqrt(jnp.asarray(dk, x.dtype))
            M0 = jnp.zeros((B, H, dk, dk), dtype=x.dtype)
            z0 = jnp.zeros((B, H, dk), dtype=x.dtype)

            def step(carry, qkv):
                M, z = carry
                q, k, v = qkv
                sq = _sigma(q)
                denom_q = jnp.sum(sq * z[:, :, None, :], axis=-1, keepdims=True) + EPS
                A_mem = jnp.matmul(sq, M) / denom_q
                scores = jnp.matmul(q, jnp.swapaxes(k, -2, -1)) * inv_sqrt_dk
                scores = jnp.where(causal, -jnp.inf, scores)
                A_dot = jnp.matmul(jax.nn.softmax(scores, axis=-1), v)
                A_s = beta * A_mem + (1.0 - beta) * A_dot
                sk = _sigma(k)
                denom_k = jnp.sum(sk * z[:, :, None, :], axis=-1, keepdims=True) + EPS
                V_prev = jnp.matmul(sk, M) / denom_k
                M_new = M + jnp.einsum('bhtk,bhtv->bhkv', sk, v - V_prev)
                z_new = z + jnp.sum(sk, axis=-2)
                return ((M_new, z_new), A_s)
            (M, z), outs = jax.lax.scan(step, (M0, z0), (Qs, Ks, Vs))
            out = outs.transpose(1, 3, 0, 2, 4).reshape(B, S * SEG, H, dk)
            out = outs.transpose(1, 2, 0, 3, 4).reshape(B, H, T, dk)
            out = out.transpose(0, 2, 1, 3).reshape(B, T, D)
            out = out @ W_o.T
            return (out, M.mean(0), z.mean(0))

        def _reference_tuple_inner(x, W_q, W_k, W_v, W_o, beta_param):
            return _infini_attention(x, W_q, W_k, W_v, W_o, beta_param)
        key = jax.random.key(seed)
        kx, kq, kk, kv, ko = jax.random.split(key, 5)
        B, T, D = (4, 2048, 512)
        scale = D ** (-0.5)
        return {'x': jax.random.normal(kx, (B, T, D), dtype=jnp.float32), 'W_q': jax.random.normal(kq, (D, D), dtype=jnp.float32) * scale, 'W_k': jax.random.normal(kk, (D, D), dtype=jnp.float32) * scale, 'W_v': jax.random.normal(kv, (D, D), dtype=jnp.float32) * scale, 'W_o': jax.random.normal(ko, (D, D), dtype=jnp.float32) * scale, 'beta_param': jnp.zeros((N_HEADS,), dtype=jnp.float32)}
    _L0_attn_all = _L0_attn_setup()
    _L0_attn_in = {k: v for k, v in _L0_attn_all.items() if k in ('W_q', 'W_k', 'W_v', 'W_o', 'beta_param')}
    del _L0_attn_all

    def _L0_xattn_setup():
        import jax, jax.numpy as jnp
        import numpy as np
        B, TQ, TKV, D, H = (4, 256, 2048, 512, 8)
        HEAD_DIM = D // H

        def _split_heads(x, h):
            b, t, c = x.shape
            return x.reshape(b, t, h, c // h).transpose(0, 2, 1, 3)
        key = jax.random.key(seed)
        ks = jax.random.split(key, 8)
        s = 0.02
        inputs_q = jax.random.normal(ks[0], (B, TQ, D), jnp.float32)
        inputs_kv = jax.random.normal(ks[1], (B, TKV, D), jnp.float32)
        attention_mask = jax.random.randint(ks[2], (B, TQ, TKV), 0, 2).astype(bool)
        Wq = jax.random.normal(ks[3], (D, D), jnp.float32) * s
        Wk = jax.random.normal(ks[4], (D, D), jnp.float32) * s
        Wv = jax.random.normal(ks[5], (D, D), jnp.float32) * s
        Wo = jax.random.normal(ks[6], (D, D), jnp.float32) * s
        zb = jnp.zeros((D,), jnp.float32)
        return {'inputs_q': inputs_q, 'inputs_kv': inputs_kv, 'attention_mask': attention_mask, 'Wq': Wq, 'bq': zb, 'Wk': Wk, 'bk': zb, 'Wv': Wv, 'bv': zb, 'Wo': Wo, 'bo': zb}
    _L0_xattn_all = _L0_xattn_setup()
    _L0_xattn_in = {k: v for k, v in _L0_xattn_all.items() if k in ('Wq', 'bq', 'Wk', 'bk', 'Wv', 'bv', 'Wo', 'bo')}
    del _L0_xattn_all

    def _L0_ffn_setup():
        import jax, jax.numpy as jnp
        import numpy as np
        BLOCK = 32
        W_BITS = 4
        ACT_BITS = 16

        def act_qdq(x):
            qmax = 2.0 ** (ACT_BITS - 1) - 1.0
            scale = jnp.maximum(jnp.max(jnp.abs(x)) / qmax, 1e-12)
            return jnp.clip(jnp.round(x / scale), -qmax - 1.0, qmax) * scale

        def fixed_qdq_u16(x):
            scale = 1.0 / 65536.0
            return jnp.clip(jnp.round(x / scale), 0.0, 65535.0) * scale

        def lpbq_dequant(w):
            O, I = w.shape
            qmax = 2.0 ** (W_BITS - 1) - 1.0
            wb = w.reshape(O, I // BLOCK, BLOCK)
            s = jnp.maximum(jnp.max(jnp.abs(wb), axis=-1, keepdims=True) / qmax, 1e-12)
            wq = jnp.clip(jnp.round(wb / s), -qmax - 1.0, qmax) * s
            return wq.reshape(O, I)
        key = jax.random.key(seed)
        k1, k2, k3, k4 = jax.random.split(key, 4)
        B, S, H, I = (2, 2048, 512, 1536)
        x = jax.random.normal(k1, (B, S, H), jnp.float32)
        w_gate = jax.random.normal(k2, (I, H), jnp.float32) * 0.02
        w_up = jax.random.normal(k3, (I, H), jnp.float32) * 0.02
        w_down = jax.random.normal(k4, (H, I), jnp.float32) * 0.02
        return {'x': x, 'w_gate': w_gate, 'w_up': w_up, 'w_down': w_down}
    _L0_ffn_all = _L0_ffn_setup()
    _L0_ffn_in = {k: v for k, v in _L0_ffn_all.items() if k in ('w_gate', 'w_up', 'w_down')}
    del _L0_ffn_all
    return {'x': x, 'ctx_1024': ctx_1024, 'mask_BxSxS2_bk0': mask_BxSxS2_bk0, 'L0_attn_W_q': _L0_attn_in['W_q'], 'L0_attn_W_k': _L0_attn_in['W_k'], 'L0_attn_W_v': _L0_attn_in['W_v'], 'L0_attn_W_o': _L0_attn_in['W_o'], 'L0_attn_beta_param': _L0_attn_in['beta_param'], 'L0_xattn_Wq': _L0_xattn_in['Wq'], 'L0_xattn_bq': _L0_xattn_in['bq'], 'L0_xattn_Wk': _L0_xattn_in['Wk'], 'L0_xattn_bk': _L0_xattn_in['bk'], 'L0_xattn_Wv': _L0_xattn_in['Wv'], 'L0_xattn_bv': _L0_xattn_in['bv'], 'L0_xattn_Wo': _L0_xattn_in['Wo'], 'L0_xattn_bo': _L0_xattn_in['bo'], 'L0_ffn_w_gate': _L0_ffn_in['w_gate'], 'L0_ffn_w_up': _L0_ffn_in['w_up'], 'L0_ffn_w_down': _L0_ffn_in['w_down']}

def reference(x, ctx_1024, mask_BxSxS2_bk0, L0_attn_W_q, L0_attn_W_k, L0_attn_W_v, L0_attn_W_o, L0_attn_beta_param, L0_xattn_Wq, L0_xattn_bq, L0_xattn_Wk, L0_xattn_bk, L0_xattn_Wv, L0_xattn_bv, L0_xattn_Wo, L0_xattn_bo, L0_ffn_w_gate, L0_ffn_w_up, L0_ffn_w_down):
    import jax
    import jax.numpy as jnp

    def _L0_attn_ref(x, W_q, W_k, W_v, W_o, beta_param):
        import jax, jax.numpy as jnp
        import numpy as np
        N_HEADS = 16
        SEG = 64
        EPS = 1e-06

        def _sigma(x):
            return jax.nn.elu(x) + 1.0

        def _infini_attention(x, W_q, W_k, W_v, W_o, beta_param):
            B, T, D = x.shape
            H = N_HEADS
            dk = D // H
            assert T % SEG == 0
            S = T // SEG

            def proj(W):
                y = (x @ W.T).reshape(B, T, H, dk).transpose(0, 2, 1, 3)
                return y.reshape(B, H, S, SEG, dk).transpose(2, 0, 1, 3, 4)
            Qs, Ks, Vs = (proj(W_q), proj(W_k), proj(W_v))
            beta = jax.nn.sigmoid(beta_param).reshape(1, H, 1, 1)
            causal = jnp.triu(jnp.ones((SEG, SEG), dtype=bool), k=1)
            inv_sqrt_dk = 1.0 / jnp.sqrt(jnp.asarray(dk, x.dtype))
            M0 = jnp.zeros((B, H, dk, dk), dtype=x.dtype)
            z0 = jnp.zeros((B, H, dk), dtype=x.dtype)

            def step(carry, qkv):
                M, z = carry
                q, k, v = qkv
                sq = _sigma(q)
                denom_q = jnp.sum(sq * z[:, :, None, :], axis=-1, keepdims=True) + EPS
                A_mem = jnp.matmul(sq, M) / denom_q
                scores = jnp.matmul(q, jnp.swapaxes(k, -2, -1)) * inv_sqrt_dk
                scores = jnp.where(causal, -jnp.inf, scores)
                A_dot = jnp.matmul(jax.nn.softmax(scores, axis=-1), v)
                A_s = beta * A_mem + (1.0 - beta) * A_dot
                sk = _sigma(k)
                denom_k = jnp.sum(sk * z[:, :, None, :], axis=-1, keepdims=True) + EPS
                V_prev = jnp.matmul(sk, M) / denom_k
                M_new = M + jnp.einsum('bhtk,bhtv->bhkv', sk, v - V_prev)
                z_new = z + jnp.sum(sk, axis=-2)
                return ((M_new, z_new), A_s)
            (M, z), outs = jax.lax.scan(step, (M0, z0), (Qs, Ks, Vs))
            out = outs.transpose(1, 3, 0, 2, 4).reshape(B, S * SEG, H, dk)
            out = outs.transpose(1, 2, 0, 3, 4).reshape(B, H, T, dk)
            out = out.transpose(0, 2, 1, 3).reshape(B, T, D)
            out = out @ W_o.T
            return (out, M.mean(0), z.mean(0))

        def _reference_tuple_inner(x, W_q, W_k, W_v, W_o, beta_param):
            return _infini_attention(x, W_q, W_k, W_v, W_o, beta_param)
        return _reference_tuple_inner(x, W_q, W_k, W_v, W_o, beta_param)[0]

    def _L0_xattn_ref(inputs_q, inputs_kv, attention_mask, Wq, bq, Wk, bk, Wv, bv, Wo, bo):
        import jax, jax.numpy as jnp
        import numpy as np
        B, TQ, TKV, D, H = (4, 256, 2048, 512, 8)
        HEAD_DIM = D // H

        def _split_heads(x, h):
            b, t, c = x.shape
            return x.reshape(b, t, h, c // h).transpose(0, 2, 1, 3)
        q = _split_heads(inputs_q @ Wq + bq, H)
        k = _split_heads(inputs_kv @ Wk + bk, H)
        v = _split_heads(inputs_kv @ Wv + bv, H)
        scale = 1.0 / np.sqrt(HEAD_DIM).astype(np.float32)
        scores = jnp.einsum('bhtd,bhTd->bhtT', q, k) * scale
        large_k = jnp.asarray(1e+30, scores.dtype)
        scores = jnp.where(attention_mask[:, None, :, :], scores, -large_k)
        probs = jax.nn.softmax(scores, axis=-1)
        summed = jnp.einsum('bhtT,bhTd->bhtd', probs, v)
        b, h, t, d = summed.shape
        summed = summed.transpose(0, 2, 1, 3).reshape(b, t, h * d)
        wipe = jnp.all(~attention_mask, axis=-1, keepdims=True)
        summed = jnp.where(wipe, jnp.zeros_like(summed), summed)
        return summed @ Wo + bo

    def _L0_ffn_ref(x, w_gate, w_up, w_down):
        import jax, jax.numpy as jnp
        import numpy as np
        BLOCK = 32
        W_BITS = 4
        ACT_BITS = 16

        def act_qdq(x):
            qmax = 2.0 ** (ACT_BITS - 1) - 1.0
            scale = jnp.maximum(jnp.max(jnp.abs(x)) / qmax, 1e-12)
            return jnp.clip(jnp.round(x / scale), -qmax - 1.0, qmax) * scale

        def fixed_qdq_u16(x):
            scale = 1.0 / 65536.0
            return jnp.clip(jnp.round(x / scale), 0.0, 65535.0) * scale

        def lpbq_dequant(w):
            O, I = w.shape
            qmax = 2.0 ** (W_BITS - 1) - 1.0
            wb = w.reshape(O, I // BLOCK, BLOCK)
            s = jnp.maximum(jnp.max(jnp.abs(wb), axis=-1, keepdims=True) / qmax, 1e-12)
            wq = jnp.clip(jnp.round(wb / s), -qmax - 1.0, qmax) * s
            return wq.reshape(O, I)
        x = act_qdq(x)
        up = act_qdq(x @ lpbq_dequant(w_up).T)
        gate = act_qdq(x @ lpbq_dequant(w_gate).T)
        sig = fixed_qdq_u16(jax.nn.sigmoid(gate))
        gate = act_qdq(gate * sig)
        o = act_qdq(gate * up)
        return o @ lpbq_dequant(w_down).T
    x = _layernorm(x + _L0_attn_ref(x, L0_attn_W_q, L0_attn_W_k, L0_attn_W_v, L0_attn_W_o, L0_attn_beta_param), axis=-1)
    x = _layernorm(x + _L0_xattn_ref(x, ctx_1024, mask_BxSxS2_bk0, L0_xattn_Wq, L0_xattn_bq, L0_xattn_Wk, L0_xattn_bk, L0_xattn_Wv, L0_xattn_bv, L0_xattn_Wo, L0_xattn_bo), axis=-1)
    x = _layernorm(x + _L0_ffn_ref(x, L0_ffn_w_gate, L0_ffn_w_up, L0_ffn_w_down), axis=-1)
    return x

_drawn_inputs = setup_inputs


def setup_inputs(seed=0):
    import zlib

    import numpy as np

    out = dict(_drawn_inputs(seed))
    spreads = {'L0_attn_beta_param': (0.0, 0.8),
     'L0_xattn_bq': (0.0, 0.8),
     'L0_xattn_bk': (0.0, 0.8),
     'L0_xattn_bv': (0.0, 0.1),
     'L0_xattn_bo': (0.0, 0.1)}
    factors = {'L0_xattn_Wq': 4.95, 'L0_xattn_Wk': 4.816}
    for name, (base, spread) in spreads.items():
        noise = np.random.default_rng([zlib.crc32(name.encode()), seed]).standard_normal(out[name].shape)
        drawn = base * np.exp(spread * noise) if base else spread * noise
        out[name] = jnp.asarray(drawn.astype(out[name].dtype))
    for name, factor in factors.items():
        out[name] = (out[name] * factor).astype(out[name].dtype)
    return out
```

```python
from contextlib import ExitStack

import concourse.bass as bass
from concourse import mybir

F32 = mybir.dt.float32
F32R = mybir.dt.float32r
BF16 = mybir.dt.bfloat16
I16 = mybir.dt.int16
U16 = mybir.dt.uint16
U8 = mybir.dt.uint8
ALU = mybir.AluOpType
ACT = mybir.ActivationFunctionType
AX = mybir.AxisListType.X
RMAX = bass.bass_isa.ReduceOp.max

P = 128
D = 512
HID = 1536
TB = 512
QBLOCK = 32
QMAX = 32767.0
WQMAX = 7.0
SIG_ONE = 65536.0
LN_EPS = 1e-5
CTX = 77
MEM_EPS = 1e-6
POOL_CONSTS = 9
DVE_CONSTS = 9


def wait(eng, sem, value):
    if not isinstance(value, int) or value > 0:
        eng.wait_ge(sem, value)


def batches(eng, NB, emit):
    emit(0, 0, True, False)
    if NB > 2:
        with eng.Fori(0, (NB - 2) // 2) as i:
            emit(i * 2 + 1, 1, False, False)
            emit(i * 2 + 2, 0, False, False)
    emit(NB - 1, 1, False, True)


def split_weights_stage(nc, jobs, tag):
    with ExitStack() as ctx:
        def sem(name):
            return nc.alloc_semaphore(f"{tag}_{name}")

        raw = ctx.enter_context(nc.sbuf_tensor(f"{tag}_raw", [P, 2, D // P, D], F32))
        loaded = [sem("loaded0"), sem("loaded1")]
        hi_done, lo_done = sem("hi_done"), sem("lo_done")
        block = ctx.enter_context(nc.Block())

        @block.sync
        def _(sp):
            for n, (src, hi, lo) in enumerate(jobs):
                if n >= 2:
                    sp.wait_ge(lo_done, n - 1)
                sp.dma_start(raw[:, n % 2, :, :], src).then_inc(loaded[n % 2], 16)

        @block.scalar
        def _(act):
            for n, (src, hi, lo) in enumerate(jobs):
                act.wait_ge(loaded[n % 2], 16 * (n // 2 + 1))
                nc.scalar.activation(hi[:, :, :], raw[:, n % 2, :, :], ACT.Copy).then_inc(hi_done, 1)

        @block.vector
        def _(dve):
            for n, (src, hi, lo) in enumerate(jobs):
                dve.wait_ge(hi_done, n + 1)
                nc.vector.tensor_tensor(lo[:, :, :], raw[:, n % 2, :, :], hi[:, :, :], ALU.subtract).then_inc(lo_done, 1)




def self_phase(nc, ident, identb, x, x_t, x1, w, beta, NB):
    K = D // P
    H = 16
    HW = D // H
    HG = P // HW
    S = P // 2
    MW = HW + 1
    SCALE = HW ** -0.5
    with ExitStack() as ctx:
        def sb(name, shape, dt=F32):
            return ctx.enter_context(nc.sbuf_tensor("a_" + name, shape, dt))

        def ps(name, shape):
            return ctx.enter_context(nc.psum_tensor("a_" + name, shape, F32))

        def sem(name):
            return nc.alloc_semaphore("a_" + name)

        wq, wk, wv, wo = ((sb(f"w{n}_hi", [P, K, D], F32R), sb(f"w{n}_lo", [P, K, D], F32R)) for n in "qkvo")
        split_weights_stage(nc, [(src, hi, lo) for src, (hi, lo) in zip(w, (wq, wk, wv, wo))], "aw")
        x_in = sb("x_in", [P, K, TB])
        xt_hi, xt_lo = sb("xt_hi", [P, K, TB], F32R), sb("xt_lo", [P, K, TB], F32R)
        q_t = [sb(f"q_t{u}", [P, K, TB]) for u in range(2)]
        k_t = [sb(f"k_t{u}", [P, K, TB]) for u in range(2)]
        v_n = [sb(f"v_n{u}", [P, 4, H, MW]) for u in range(2)]
        q_pad = sb("q_pad", [P, K, 4 * S])
        k_diag = sb("k_diag", [P, K, 2, HG * S])
        feat = sb("feat", [P, 2, K, 4 * S])
        f_exp = sb("f_exp", [P, 2, K, 2 * S])
        sk_n = sb("sk_n", [P, D])
        state = sb("state", [P, K, HG * MW])
        m_rec = sb("m_rec", [P, 2, H])
        m_out = sb("m_out", [P, 2, H, HW])
        delta = sb("delta", [P, H, MW])
        gain = sb("gain", [P, 2, H])
        beta_b, one_m = sb("beta_b", [P, H]), sb("one_m", [P, H])
        tri = sb("tri", [P, P], BF16)
        causal = sb("causal", [P, S], BF16)
        top, a_rec = sb("top", [P, H]), sb("a_rec", [P, H])
        e_in = sb("e_in", [P, H, S])
        probs = sb("probs", [P, H, P])
        p_t = sb("p_t", [P, H, P])
        att = sb("att", [P, 2, D])
        o_hi, o_lo = sb("o_hi", [P, K, P], F32R), sb("o_lo", [P, K, P], F32R)
        y = sb("y", [P, 2, D])
        st, mv, var = sb("st", [P, 2, 6]), sb("mv", [P, 2, 2]), sb("var", [P, 2, 1])
        rstd, half = sb("rstd", [P, 2, 1]), sb("half", [P, 1])
        wide = ps("wide", [P, 2, 512])
        score = ps("score", [P, 2, 512])
        turn = ps("turn", [P, 2, 512])
        mem = ps("mem", [P, 2, 512])

        names = """beta_loaded pool_consts beta_exp consts_done x_loaded x_hi_done x_lo_done proj_mm proj_out padded f_exped f_floored feat_done
                   scored topped shifted exped p_turned p_moved mixed a_recd a_scaled a_done a_added
                   sk_turned sk_moved mem_read eps_added m_recd m_gained m_done delta_done mem_written m_updated m_reset
                   o_turned o_hi_done o_lo_done y_mm y_done stats aggr var_done powed normed stats_seen update_seen""".split()
        s = {n: sem(n) for n in names}
        r_loaded = [sem(f"r_loaded{u}") for u in range(2)]
        stored = [sem(f"stored{u}") for u in range(2)]
        N = 4 * NB
        ITEMS = [(kind, f) for f in range(2) for kind in "qk"] + [(kind, f) for f in (2, 3) for kind in "qk"] + [("v", t) for t in range(4)]
        NI = len(ITEMS)
        ITEM_BANK = [1, 0, 1, 0, 0, 1, 0, 1, 1, 0, 1, 0]
        ITEM_PREV = [0, 0, 1, 2, 4, 3, 5, 6, 8, 7, 9, 10]
        Y_BANK = [0, 1, 0, 1]
        block = ctx.enter_context(nc.Block())

        @block.sync
        def _(sp):
            sp.dma_start(beta_b[:, :], beta).then_inc(s["beta_loaded"], 16)

            def load_x(c):
                wait(sp, s["x_lo_done"], c * 4)
                sp.dma_start(x_in[:, :, :], x_t[bass.ds(c, 1), :, :, :].rearrange("b k p t -> p (b k) t")).then_inc(s["x_loaded"], 16)

            def load_residual(n, b, t):
                wait(sp, stored[t % 2], b * 32 + 16 * (t // 2))
                sp.dma_start(y[:, t % 2, :], x[bass.ds(b, 1), :, t, :].rearrange("b p d -> p (b d)")).then_inc(r_loaded[t % 2], 16)

            def store(n, b, t):
                sp.wait_ge(s["normed"], n + 1)
                sp.dma_start(x1[bass.ds(b, 1), :, t, :].rearrange("b p d -> p (b d)"), y[:, t % 2, :]).then_inc(stored[t % 2], 16)

            load_x(0)

            def emit(b, u, first, last):
                for t in range(4):
                    if t == 0 and not last:
                        load_x(b + 1)
                    if t >= 2:
                        store(b * 4 + t - 2, b, t - 2)
                    elif not first:
                        store(b * 4 + t - 2, b - 1, t + 2)
                    load_residual(b * 4 + t, b, t)

            batches(sp, NB, emit)
            store(N - 2, NB - 1, 2)
            store(N - 1, NB - 1, 3)
            for u in range(2):
                sp.wait_ge(stored[u], 16 * 2 * NB)

        @block.tensor
        def _(pe):
            def project(c, i, steady):
                kind, f = ITEMS[i]
                if i == 0:
                    pe.wait_ge(s["x_lo_done"], c * 4 + 4)
                    if steady:
                        wait(pe, s["y_done"], c * 4 - 5)
                elif i in (1, 5, 9) and steady:
                    wait(pe, s["y_done"], c * 4 - 4 + i // 4)
                wait(pe, s["proj_out"], c * NI + ITEM_PREV[i])
                out = wide[:, ITEM_BANK[i], :]
                for k in range(K):
                    if kind == "v":
                        cols = slice(f * P, (f + 1) * P)
                        parts = ((xt_hi[:, k, cols], wv[0][:, k, :]), (xt_lo[:, k, cols], wv[0][:, k, :]), (xt_hi[:, k, cols], wv[1][:, k, :]))
                    else:
                        hi, lo = wq if kind == "q" else wk
                        cols = slice(f * P, (f + 1) * P)
                        parts = ((hi[:, k, cols], xt_hi[:, k, :]), (hi[:, k, cols], xt_lo[:, k, :]), (lo[:, k, cols], xt_hi[:, k, :]))
                    for m, (a, r) in enumerate(parts):
                        mm = nc.tensor.matmul(out, a, r, start=(k == 0 and m == 0), stop=(k == K - 1 and m == 2))
                mm.then_inc(s["proj_mm"], 1)

            def read_memory(n, g, c, t):
                if g == 0:
                    pe.wait_ge(s["feat_done"], n * 2 + 2)
                    if t == 0:
                        pe.wait_ge(s["m_reset"], c + 1)
                wait(pe, s["m_updated"], n * 2 + g)
                cols = slice(2 * S, 4 * S) if g == 0 else slice(0, 2 * S)
                for f in range(K):
                    mm = nc.tensor.matmul(mem[:, f // 2, (f % 2) * HG * MW:(f % 2 + 1) * HG * MW], feat[:, t % 2, f, cols],
                                          state[:, f, :], start=(f % 2 == 0), stop=(f % 2 == 1), skip_group_check=True)
                mm.then_inc(s["mem_read"], 1)

            def write_memory(n, g, t):
                pe.wait_ge(s["delta_done"], n * 2 + g + 1)
                if g == 0:
                    pe.wait_ge(s["sk_moved"], n + 1)
                rows = slice(S, P) if g == 0 else slice(0, S)
                for f in range(K):
                    mm = nc.tensor.matmul(mem[:, f // 2, (f % 2) * HG * MW:(f % 2 + 1) * HG * MW], sk_n[rows, f * P:(f + 1) * P],
                                          delta[rows, f * HG:(f + 1) * HG, :].rearrange("p h w -> p (h w)"),
                                          start=(f % 2 == 0), stop=(f % 2 == 1), skip_group_check=True)
                mm.then_inc(s["mem_written"], 1)

            def turn_p(n, g):
                if g == 0:
                    pe.wait_ge(s["exped"], n * 2 + 2)
                    pe.wait_ge(s["sk_moved"], n + 1)
                elif g == 1:
                    wait(pe, s["o_lo_done"], n - 1)
                else:
                    pe.wait_ge(s["p_moved"], n * 4 + g - 1)
                for j in range(4):
                    mm = nc.tensor.transpose(turn[:, g % 2, j * P:(j + 1) * P], probs[:, 4 * g + j, :], ident[:, :])
                mm.then_inc(s["p_turned"], 1)

            def attend(n, c, u, t):
                pe.wait_ge(s["p_moved"], n * 4 + 4)
                pe.wait_ge(s["proj_out"], c * NI + NI)
                for h in range(H):
                    mm = nc.tensor.matmul(score[:, h // 8, (h % 8) * MW:(h % 8 + 1) * MW], p_t[:, h, :], v_n[u][:, t, h, :],
                                          start=(h % 8 == 0), stop=(h % 8 == 7), skip_group_check=True)
                mm.then_inc(s["mixed"], 1)

            def turn_sk(n, r, first):
                pe.wait_ge(s["feat_done"], n * 2 + 2)
                if not first:
                    pe.wait_ge(s["p_moved"], n * 4 - 1)
                for f in range(K):
                    for g in range(2):
                        mm = nc.tensor.matmul(turn[g * S:(g + 1) * S, 0, f * P:(f + 1) * P], feat[:, r, f, 3 * S * g:3 * S * g + S], ident[:, :],
                                              start=True, stop=True, skip_group_check=True)
                mm.then_inc(s["sk_turned"], 1)

            def turn_o(n, r, final):
                pe.wait_ge(s["a_added"], n * 2 + 2)
                pe.wait_ge(s["p_moved"], n * 4 + (4 if final else 8))
                wait(pe, s["o_lo_done"], n)
                for k in range(K):
                    mm = nc.tensor.transpose(turn[:, 1, k * P:(k + 1) * P], att[:, r, k * P:(k + 1) * P], ident[:, :])
                mm.then_inc(s["o_turned"], 1)

            def scores(n, r):
                pe.wait_ge(s["padded"], n + 1)
                wait(pe, s["a_done"], n)
                for g in range(2):
                    nc.tensor.matmul(score[:, g, :], identb[:, :], causal[:, :].unsqueeze(1).broadcast_to([P, 8, S]), start=True, stop=False, skip_group_check=True)
                for f in range(K):
                    for g in range(2):
                        mm = nc.tensor.matmul(score[:, f // 2, (f % 2) * HG * S:(f % 2 + 1) * HG * S], q_pad[:, f, 2 * S * g:2 * S * (g + 1)],
                                              k_diag[:, f, g, :], start=False, stop=(f % 2 == 1 and g == 1), skip_group_check=True)
                mm.then_inc(s["scored"], 1)

            def project_o(n, bank, items):
                pe.wait_ge(s["o_lo_done"], n + 1)
                wait(pe, s["y_done"], n - 1)
                if items is not None:
                    wait(pe, s["proj_out"], items)
                for k in range(K):
                    for m, (o, a) in enumerate(((o_hi, wo[0]), (o_lo, wo[0]), (o_hi, wo[1]))):
                        mm = nc.tensor.matmul(wide[:, bank, :], o[:, k, :], a[:, k, :], start=(k == 0 and m == 0), stop=(k == K - 1 and m == 2))
                mm.then_inc(s["y_mm"], 1)

            pe.wait_ge(s["pool_consts"], POOL_CONSTS)
            pe.wait_ge(s["consts_done"], DVE_CONSTS)
            for i in range(NI):
                project(0, i, False)
            turn_sk(0, 0, True)
            scores(0, 0)

            def emit(b, u, first, last):
                for t in range(4):
                    n = b * 4 + t
                    r = t % 2
                    items = [] if last or t == 0 else [4 * t - 4 + j for j in range(4)]

                    def item(j):
                        if items:
                            project(b + 1, items[j], True)

                    read_memory(n, 0, b, t)
                    turn_p(n, 0)
                    turn_p(n, 1)
                    item(0)
                    write_memory(n, 0, t)
                    turn_p(n, 2)
                    turn_p(n, 3)
                    item(1)
                    read_memory(n, 1, b, t)
                    attend(n, b, u, t)
                    item(2)
                    write_memory(n, 1, t)
                    if not (last and t == 3):
                        turn_sk(n + 1, 1 - r, False)
                    if not (first and t == 0):
                        turn_o(n - 1, 1 - r, False)
                    if not (last and t == 3):
                        scores(n + 1, 1 - r)
                    item(3)
                    if not (first and t == 0):
                        project_o(n - 1, Y_BANK[t], None if last and t else b * NI + NI if t == 0 else (b + 1) * NI + 4 * t - 1)

            batches(pe, NB, emit)
            turn_o(N - 1, 1, True)
            project_o(N - 1, 0, None)

        @block.scalar
        def _(act):
            act.wait_ge(s["beta_loaded"], 16)
            nc.scalar.activation(beta_b[:, :], beta_b[:, :], ACT.Exp, scale=-1.0).then_inc(s["beta_exp"], 1)
            act.wait_ge(s["pool_consts"], POOL_CONSTS)

            def x_high(c):
                act.wait_ge(s["x_loaded"], c * 16 + 16)
                wait(act, s["proj_mm"], c * NI)
                for k in range(K):
                    nc.scalar.activation(xt_hi[:, k, :], x_in[:, k, :], ACT.Copy).then_inc(s["x_hi_done"], 1)

            def item_out(c, u, i):
                kind, f = ITEMS[i]
                act.wait_ge(s["proj_mm"], c * NI + i + 1)
                src = wide[:, ITEM_BANK[i], :]
                if kind == "v":
                    ins = nc.scalar.activation(v_n[u][:, f, :, 0:HW], src.rearrange("p (h w) -> p h w", h=H), ACT.Copy)
                else:
                    ins = nc.scalar.activation((q_t if kind == "q" else k_t)[u][:, f, :], src, ACT.Copy)
                ins.then_inc(s["proj_out"], 1)

            def feat_exp(n, c, u, t):
                if t == 0:
                    act.wait_ge(s["proj_out"], c * NI + 8)
                for j, src in enumerate((q_t[u], k_t[u])):
                    wait(act, s["feat_done"], n * 2 - 1 + j)
                    nc.scalar.activation(f_exp[:, j, :, :], src[:, :, t * P:(t + 1) * P], ACT.Exp).then_inc(s["f_exped"], 1)

            def exp(n):
                act.wait_ge(s["shifted"], n + 1)
                wait(act, s["p_turned"], n * 4)
                nc.scalar.activation(probs[0:S, :, S:P], e_in[0:S, :, :], ACT.Exp, scale=SCALE).then_inc(s["exped"], 1)
                nc.scalar.activation(probs[S:P, :, 0:S], e_in[S:P, :, :], ACT.Exp, scale=SCALE).then_inc(s["exped"], 1)

            def p_out(n, g):
                if g == 0:
                    wait(act, s["mixed"], n)
                act.wait_ge(s["p_turned"], n * 4 + g + 1)
                nc.scalar.activation(p_t[:, 4 * g:4 * g + 4, :], turn[:, g % 2, :].rearrange("p (h q) -> p h q", h=4), ACT.Copy).then_inc(s["p_moved"], 1)

            def sk_out(n, r):
                act.wait_ge(s["sk_turned"], n + 1)
                wait(act, s["mem_written"], n * 2)
                nc.scalar.activation(sk_n[:, :], turn[:, 0, :], ACT.Copy).then_inc(s["sk_moved"], 1)

            def o_high(n):
                act.wait_ge(s["o_turned"], n + 1)
                wait(act, s["y_mm"], n)
                nc.scalar.activation(o_hi[:, :, :], turn[:, 1, :].rearrange("p (k m) -> p k m", k=K), ACT.Copy).then_inc(s["o_hi_done"], 1)

            x_high(0)
            for i in range(NI):
                item_out(0, 0, i)
            feat_exp(0, 0, 0, 0)
            sk_out(0, 0)
            exp(0)

            def emit(b, u, first, last):
                for t in range(4):
                    n = b * 4 + t
                    r = t % 2
                    items = [] if last or t == 0 else [4 * t - 4 + j for j in range(4)]

                    def item(j):
                        if items:
                            item_out(b + 1, 1 - u, items[j])

                    p_out(n, 0)
                    p_out(n, 1)
                    item(0)
                    p_out(n, 2)
                    p_out(n, 3)
                    item(1)
                    if t < 3:
                        feat_exp(n + 1, b, u, t + 1)
                    elif not last:
                        feat_exp(n + 1, b + 1, 1 - u, 0)
                    item(2)
                    if not (last and t == 3):
                        sk_out(n + 1, 1 - r)
                    if not (first and t == 0):
                        o_high(n - 1)
                    item(3)
                    if not (last and t == 3):
                        exp(n + 1)
                    if t == 0 and not last:
                        x_high(b + 1)

            batches(act, NB, emit)
            o_high(N - 1)

        @block.gpsimd
        def _(pool):
            nc.gpsimd.memset(tri[:, :], 0.0).then_inc(s["pool_consts"], 1)
            pool.wait_ge(s["pool_consts"], 1)
            nc.gpsimd.affine_select(out=tri[:, :], in_=tri[:, :], compare_op=ALU.is_ge, fill=-1e30, base=0,
                                    pattern=[[-1, P]], channel_multiplier=1).then_inc(s["pool_consts"], 1)
            for tile in (q_pad, k_diag, probs):
                nc.gpsimd.memset(tile[:], 0.0).then_inc(s["pool_consts"], 1)
            for tile in v_n:
                nc.gpsimd.memset(tile[:, :, :, HW:MW], 1.0).then_inc(s["pool_consts"], 1)
            nc.gpsimd.memset(delta[:, :, HW:MW], 1.0).then_inc(s["pool_consts"], 1)
            nc.gpsimd.memset(half[:, :], -0.5).then_inc(s["pool_consts"], 1)

            def reset(b):
                wait(pool, s["m_updated"], b * 8)
                pool.sem_inc(s["update_seen"], 1)
                nc.gpsimd.memset(state[:, :, :], 0.0).then_inc(s["m_reset"], 1)

            def add_memory(n, r):
                for g in range(2):
                    rows = slice(0, S) if g == 0 else slice(S, P)
                    if g == 0:
                        pool.wait_ge(s["a_done"], n + 1)
                        wait(pool, s["powed"], n - 1)
                    else:
                        pool.wait_ge(s["a_added"], n * 2 + 1)
                    pool.wait_ge(s["m_done"], n * 2 + g + 1)
                    nc.gpsimd.tensor_tensor(att[rows, r, :], att[rows, r, :], m_out[rows, g, :, :].rearrange("p h w -> p (h w)"), ALU.add).then_inc(s["a_added"], 1)

            def power(n, r, added):
                pool.wait_ge(s["var_done"], n + 1)
                pool.wait_ge(s["a_added"], added)
                nc.gpsimd.tensor_tensor(rstd[:, r, :], var[:, r, :], half[:, :], ALU.pow).then_inc(s["powed"], 1)

            def emit(b, u, first, last):
                for t in range(4):
                    n = b * 4 + t
                    if t == 0:
                        reset(b)
                    add_memory(n, t % 2)
                    if not (first and t == 0):
                        power(n - 1, 1 - t % 2, n * 2 + 2)

            batches(pool, NB, emit)
            power(N - 1, 1, N * 2)

        @block.vector
        def _(dve):
            dve.wait_ge(s["pool_consts"], POOL_CONSTS)
            dve.wait_ge(s["beta_exp"], 1)
            nc.vector.tensor_scalar(beta_b[:, :], beta_b[:, :], 1.0, None, ALU.add).then_inc(s["consts_done"], 1)
            dve.wait_ge(s["consts_done"], 1)
            nc.vector.reciprocal(beta_b[:, :], beta_b[:, :]).then_inc(s["consts_done"], 1)
            dve.wait_ge(s["consts_done"], 2)
            nc.vector.tensor_scalar(one_m[:, :], beta_b[:, :], -1.0, 1.0, ALU.mult, ALU.add).then_inc(s["consts_done"], 1)
            nc.vector.tensor_copy(gain[0:S, 0, :], beta_b[0:S, :]).then_inc(s["consts_done"], 1)
            nc.vector.tensor_copy(gain[S:P, 1, :], beta_b[S:P, :]).then_inc(s["consts_done"], 1)
            nc.vector.memset(gain[S:P, 0, :], 1.0).then_inc(s["consts_done"], 1)
            nc.vector.memset(gain[0:S, 1, :], 1.0).then_inc(s["consts_done"], 1)
            nc.vector.tensor_copy(causal[0:S, :], tri[0:S, 0:S]).then_inc(s["consts_done"], 1)
            nc.vector.tensor_copy(causal[S:P, :], tri[S:P, S:P]).then_inc(s["consts_done"], 1)
            dve.wait_ge(s["consts_done"], DVE_CONSTS)

            def x_low(c):
                for k in range(K):
                    dve.wait_ge(s["x_hi_done"], c * 4 + k + 1)
                    nc.vector.tensor_tensor(xt_lo[:, k, :], x_in[:, k, :], xt_hi[:, k, :], ALU.subtract).then_inc(s["x_lo_done"], 1)

            def pad(n, c, u, t, r):
                if t == 0:
                    dve.wait_ge(s["proj_out"], c * NI + 8)
                wait(dve, s["scored"], n)
                cols = slice(t * P, (t + 1) * P)
                nc.vector.tensor_copy(q_pad[:, :, S:3 * S], q_t[u][:, :, cols])
                for h in range(HG):
                    rows = slice(h * HW, (h + 1) * HW)
                    ins = nc.vector.tensor_copy(k_diag[rows, :, :, h * S:(h + 1) * S], k_t[u][rows, :, cols].rearrange("p f (g e) -> p f g e", g=2))
                ins.then_inc(s["padded"], 1)

            def features(n, u, t, r):
                cols = slice(t * P, (t + 1) * P)
                for j, src in enumerate((q_t[u], k_t[u])):
                    dve.wait_ge(s["f_exped"], n * 2 + j + 1)
                    nc.vector.tensor_scalar(f_exp[:, j, :, :], f_exp[:, j, :, :], 1.0, None, ALU.min).then_inc(s["f_floored"], 1)
                for j, src in enumerate((q_t[u], k_t[u])):
                    dve.wait_ge(s["f_floored"], n * 2 + j + 1)
                    if j == 0:
                        nc.vector.scalar_tensor_tensor(feat[:, r, :, S:3 * S], src[:, :, cols], 0.0, f_exp[:, 0, :, :], ALU.max, ALU.add).then_inc(s["feat_done"], 1)
                    else:
                        for g in range(2):
                            ins = nc.vector.scalar_tensor_tensor(feat[:, r, :, 3 * S * g:3 * S * g + S], src[:, :, t * P + g * S:t * P + (g + 1) * S], 0.0,
                                                                 f_exp[:, 1, :, g * S:(g + 1) * S], ALU.max, ALU.add)
                        ins.then_inc(s["feat_done"], 1)

            def shift(n):
                dve.wait_ge(s["scored"], n + 1)
                heads = score[:, :, :].rearrange("p g (h e) -> p (g h) e", e=S)
                nc.vector.tensor_reduce(top[:, :], heads, AX, ALU.max).then_inc(s["topped"], 1)
                wait(dve, s["exped"], n * 2)
                dve.wait_ge(s["topped"], n + 1)
                nc.vector.tensor_tensor(e_in[:, :, :], heads, top[:, :].unsqueeze(2).broadcast_to([P, H, S]), ALU.subtract).then_inc(s["shifted"], 1)

            mem_h = mem[:, :, 0:8 * MW].rearrange("p b (h w) -> p b h w", w=MW)
            mix_h = score[:, :, 0:8 * MW].rearrange("p b (h w) -> p b h w", w=MW)

            def recall(n, g, u, t):
                i = n * 2 + g
                dve.wait_ge(s["mem_read"], i + 1)
                nc.vector.tensor_scalar(m_rec[:, g, :].rearrange("p (b h) -> p b h", b=2), mem_h[:, :, :, HW], MEM_EPS, None, ALU.add).then_inc(s["eps_added"], 1)
                dve.wait_ge(s["eps_added"], i + 1)
                nc.vector.reciprocal(m_rec[:, g, :], m_rec[:, g, :]).then_inc(s["m_recd"], 1)
                dve.wait_ge(s["m_recd"], i + 1)
                nc.vector.tensor_tensor(m_rec[:, g, :], m_rec[:, g, :], gain[:, g, :], ALU.mult).then_inc(s["m_gained"], 1)
                dve.wait_ge(s["m_gained"], i + 1)
                wait(dve, s["a_added"], i - 1)
                nc.vector.tensor_tensor(m_out[:, g, :, :].rearrange("p (b h) w -> p b h w", b=2), mem_h[:, :, :, 0:HW],
                                        m_rec[:, g, :].rearrange("p (b h) -> p b h", b=2).unsqueeze(3).broadcast_to([P, 2, 8, HW]), ALU.mult).then_inc(s["m_done"], 1)
                dve.wait_ge(s["m_done"], i + 1)
                rows = slice(S, P) if g == 0 else slice(0, S)
                nc.vector.tensor_tensor(delta[rows, :, 0:HW], v_n[u][rows, t, :, 0:HW], m_out[rows, g, :, :], ALU.subtract).then_inc(s["delta_done"], 1)

            def update(n, g):
                dve.wait_ge(s["mem_written"], n * 2 + g + 1)
                for h in range(HG):
                    rows = slice(h * HW, (h + 1) * HW)
                    new = mem[rows, :, 0:8 * MW].rearrange("p b (f w) -> p b f w", f=2)[:, :, :, h * MW:(h + 1) * MW]
                    old = state[rows, :, h * MW:(h + 1) * MW].rearrange("p (b f) w -> p b f w", b=2)
                    ins = nc.vector.tensor_tensor(old, new, old, ALU.add)
                ins.then_inc(s["m_updated"], 1)

            def attended(n, r):
                dve.wait_ge(s["mixed"], n + 1)
                nc.vector.reciprocal(a_rec[:, :].rearrange("p (b h) -> p b h", b=2), mix_h[:, :, :, HW]).then_inc(s["a_recd"], 1)
                dve.wait_ge(s["a_recd"], n + 1)
                nc.vector.tensor_tensor(a_rec[:, :], a_rec[:, :], one_m[:, :], ALU.mult).then_inc(s["a_scaled"], 1)
                dve.wait_ge(s["a_scaled"], n + 1)
                wait(dve, s["o_turned"], n - 1)
                nc.vector.tensor_tensor(att[:, r, :].rearrange("p (b h w) -> p b h w", b=2, h=8), mix_h[:, :, :, 0:HW],
                                        a_rec[:, :].rearrange("p (b h) -> p b h", b=2).unsqueeze(3).broadcast_to([P, 2, 8, HW]), ALU.mult).then_inc(s["a_done"], 1)

            def o_low(n):
                dve.wait_ge(s["o_hi_done"], n + 1)
                nc.vector.tensor_tensor(o_lo[:, :, :], turn[:, 1, :].rearrange("p (k m) -> p k m", k=K), o_hi[:, :, :], ALU.subtract).then_inc(s["o_lo_done"], 1)

            def add(n, r, bank, residuals):
                dve.wait_ge(s["y_mm"], n + 1)
                dve.wait_ge(r_loaded[r], residuals)
                nc.vector.tensor_tensor(y[:, r, :], wide[:, bank, :], y[:, r, :], ALU.add).then_inc(s["y_done"], 1)
                dve.wait_ge(s["y_done"], n + 1)
                nc.vector.bn_stats(st[:, r, :], y[:, r, :]).then_inc(s["stats"], 1)
                dve.wait_ge(s["stats"], n + 1)
                dve.sem_inc(s["stats_seen"], 1)
                nc.vector.bn_aggr(mv[:, r, :], st[:, r, :]).then_inc(s["aggr"], 1)
                dve.wait_ge(s["aggr"], n + 1)
                wait(dve, s["powed"], n - 1)
                nc.vector.tensor_scalar(var[:, r, :], mv[:, r, 1:2], LN_EPS, None, ALU.add).then_inc(s["var_done"], 1)

            def norm(n, r):
                dve.wait_ge(s["powed"], n + 1)
                nc.vector.tensor_scalar(y[:, r, :], y[:, r, :], mv[:, r, 0:1], rstd[:, r, :], ALU.subtract, ALU.mult).then_inc(s["normed"], 1)

            x_low(0)
            pad(0, 0, 0, 0, 0)
            features(0, 0, 0, 0)
            shift(0)

            def emit(b, u, first, last):
                for t in range(4):
                    n = b * 4 + t
                    r = t % 2
                    recall(n, 0, u, t)
                    if not (first and t < 2):
                        norm(n - 2, r)
                    update(n, 0)
                    if not (last and t == 3):
                        c, cu, ct = (b, u, t + 1) if t < 3 else (b + 1, 1 - u, 0)
                        pad(n + 1, c, cu, ct, 1 - r)
                        features(n + 1, cu, ct, 1 - r)
                    recall(n, 1, u, t)
                    attended(n, r)
                    update(n, 1)
                    if not (first and t == 0):
                        o_low(n - 1)
                    if not (last and t == 3):
                        shift(n + 1)
                    if not (first and t == 0):
                        add(n - 1, 1 - r, Y_BANK[t], b * 32 + 16 * ((t + 1) // 2))
                    if t == 0 and not last:
                        x_low(b + 1)

            batches(dve, NB, emit)
            norm(N - 2, 0)
            o_low(N - 1)
            add(N - 1, 1, 0, 32 * NB)
            norm(N - 1, 1)


def cross_phase(nc, ident, identb, x1, x2, ctx_t, mask, w, bq, bk, bv, bo, x_top, NB):
    K = D // P
    XH = 8
    HD = D // XH
    C = CTX
    CP = C + 1
    SCALE = HD ** -0.5
    with ExitStack() as ctx:
        def sb(name, shape, dt=F32):
            return ctx.enter_context(nc.sbuf_tensor("x_" + name, shape, dt))

        def ps(name, shape):
            return ctx.enter_context(nc.psum_tensor("x_" + name, shape, F32))

        def sem(name):
            return nc.alloc_semaphore("x_" + name)

        wq, wk, wv, wo = ((sb(f"w{n}_hi", [P, K, D], F32R), sb(f"w{n}_lo", [P, K, D], F32R)) for n in "qkvo")
        split_weights_stage(nc, [(src, hi, lo) for src, (hi, lo) in zip(w, (wq, wk, wv, wo))], "xw")
        x_in = sb("x_in", [P, 4, D])
        x_res = sb("x_res", [P, 2, D])
        xt_hi, xt_lo = sb("xt_hi", [P, K, TB], F32R), sb("xt_lo", [P, K, TB], F32R)
        q_t = [sb(f"q_t{u}", [P, K, TB]) for u in range(2)]
        c_in = sb("c_in", [P, K, CP])
        c_hi, c_lo = sb("c_hi", [P, K, CP], F32R), sb("c_lo", [P, K, CP], F32R)
        k_t = [sb(f"k_t{u}", [P, K, CP]) for u in range(2)]
        v_n = [sb(f"v_n{u}", [C, XH, HD + 1]) for u in range(2)]
        m_in = sb("m_in", [P, 4, C], U8)
        m_neg = [sb(f"m_neg{u}", [P, 4, C], BF16) for u in range(2)]
        keep = sb("keep", [P, 2, 4])
        bq_c, bk_c = sb("bq_c", [P, K]), sb("bk_c", [P, K])
        bv_b, bo_b = sb("bv_b", [P, D]), sb("bo_b", [P, D])
        top = sb("top", [P, 2, XH])
        e_in = sb("e_in", [P, XH, C])
        probs = sb("probs", [P, 2, XH, C])
        p_t = [sb(f"p_t{u}", [C, XH, P]) for u in range(2)]
        rec = sb("rec", [P, 2, XH])
        att = sb("att", [P, 2, D])
        o_hi, o_lo = sb("o_hi", [P, K, P], F32R), sb("o_lo", [P, K, P], F32R)
        y = sb("y", [P, 3, D])
        st, mv, var = sb("st", [P, 2, 6]), sb("mv", [P, 2, 2]), sb("var", [P, 2, 1])
        rstd, half = sb("rstd", [P, 2, 1]), sb("half", [P, 1])
        x_out = sb("x_out", [P, 2, D])
        wide = ps("wide", [P, 2, D])
        score = ps("score", [P, 2, 512])
        turn = ps("turn", [P, 2, 512])
        mix = ps("mix", [P, 2, 512])

        names = """consts_loaded pool_consts bias_scaled x_loaded x_turned xt_hi_done xt_lo_done q_mm q_done c_loaded c_hi_done c_lo_done
                   k_mm k_done v_mm v_done m_loaded m_done keep_done x_biased scored topped shifted exped
                   p_turned p_moved mixed recd kept att_done o_turned o_hi_done o_lo_done y_mm y_done stats aggr
                   var_done powed normed absmaxed stats_seen""".split()
        s = {n: sem(n) for n in names}
        r_loaded = [sem(f"r_loaded{u}") for u in range(2)]
        stored = [sem(f"stored{u}") for u in range(2)]
        N = 4 * NB
        block = ctx.enter_context(nc.Block())

        @block.sync
        def _(sp):
            sp.dma_start(bq_c[:, :], bq).then_inc(s["consts_loaded"], 16)
            sp.dma_start(bk_c[:, :], bk).then_inc(s["consts_loaded"], 16)
            sp.dma_start(bv_b[:, :], bv).then_inc(s["consts_loaded"], 16)
            sp.dma_start(bo_b[:, :], bo).then_inc(s["consts_loaded"], 16)

            def load_x(b):
                wait(sp, s["x_turned"], b * 4)
                sp.dma_start(x_in[:, :, :], x1[bass.ds(b, 1), :, :, :].rearrange("b p t d -> p (b t) d")).then_inc(s["x_loaded"], 16)

            def load_residual(n, b, t):
                wait(sp, s["y_done"], n - 1)
                sp.dma_start(x_res[:, t % 2, :], x1[bass.ds(b, 1), :, t, :].rearrange("b p d -> p (b d)")).then_inc(r_loaded[t % 2], 16)

            def load_c(b):
                wait(sp, s["c_lo_done"], b)
                sp.dma_start(c_in[:, :, 0:C], ctx_t[bass.ds(b, 1), :, :, :].rearrange("b k p c -> p (b k) c")).then_inc(s["c_loaded"], 16)
                wait(sp, s["m_done"], b)
                wait(sp, s["keep_done"], b)
                sp.dma_start(m_in[:, :, :], mask[bass.ds(b, 1), :, :, :].rearrange("b t p c -> p (b t) c")).then_inc(s["m_loaded"], 16)

            def store(n, b, t):
                sp.wait_ge(s["normed"], n + 1)
                sp.dma_start(x2[bass.ds(b, 1), :, t, :].rearrange("b p d -> p (b d)"), x_out[:, t % 2, :]).then_inc(stored[t % 2], 16)

            sp.wait_ge(s["pool_consts"], 1)
            load_x(0)
            load_c(0)

            def emit(b, u, first, last):
                for t in range(4):
                    load_residual(b * 4 + t, b, t)
                    if t == 0 and not last:
                        load_x(b + 1)
                        load_c(b + 1)
                    if t >= 2:
                        store(b * 4 + t - 2, b, t - 2)
                    elif not first:
                        store(b * 4 + t - 2, b - 1, t + 2)

            batches(sp, NB, emit)
            store(N - 2, NB - 1, 2)
            store(N - 1, NB - 1, 3)
            for u in range(2):
                sp.wait_ge(stored[u], 16 * 2 * NB)

        @block.tensor
        def _(pe):
            def turn_x(c, k):
                if k == 0:
                    pe.wait_ge(s["x_loaded"], c * 16 + 16)
                    wait(pe, s["k_done"], c)
                elif k == 1:
                    wait(pe, s["v_done"], c)
                else:
                    wait(pe, s["xt_lo_done"], c * 4 + k - 1)
                for t in range(4):
                    mm = nc.tensor.transpose(wide[:, k % 2, t * P:(t + 1) * P], x_in[:, t, k * P:(k + 1) * P], ident[:, :])
                mm.then_inc(s["x_turned"], 1)

            def project_q(c, f):
                if f < 2:
                    pe.wait_ge(s["xt_lo_done"], c * 4 + 4)
                else:
                    pe.wait_ge(s["q_done"], c * 4 + f - 1)
                for k in range(K):
                    for n, (a, x) in enumerate(((wq[0], xt_hi), (wq[0], xt_lo), (wq[1], xt_hi))):
                        mm = nc.tensor.matmul(wide[:, f % 2, :], a[:, k, f * P:(f + 1) * P], x[:, k, :],
                                              start=(k == 0 and n == 0), stop=(k == K - 1 and n == 2))
                mm.then_inc(s["q_mm"], 1)

            def project_k(c):
                pe.wait_ge(s["q_done"], c * 4 + 3)
                pe.wait_ge(s["c_lo_done"], c + 1)
                for f in range(K):
                    for k in range(K):
                        for n, (a, x) in enumerate(((wk[0], c_hi), (wk[0], c_lo), (wk[1], c_hi))):
                            mm = nc.tensor.matmul(wide[:, 0, f * CP:(f + 1) * CP], a[:, k, f * P:(f + 1) * P], x[:, k, :],
                                                  start=(f == 0 and k == 0 and n == 0), stop=(k == K - 1 and n == 2), skip_group_check=True)
                mm.then_inc(s["k_mm"], 1)

            def project_v(c):
                pe.wait_ge(s["q_done"], c * 4 + 4)
                for k in range(K):
                    for n, (x, a) in enumerate(((c_hi, wv[0]), (c_lo, wv[0]), (c_hi, wv[1]))):
                        mm = nc.tensor.matmul(wide[0:C, 1, :], x[:, k, 0:C], a[:, k, :],
                                              start=(k == 0 and n == 0), stop=(k == K - 1 and n == 2))
                mm.then_inc(s["v_mm"], 1)

            def scores(n, c, u, t):
                if t == 0:
                    pe.wait_ge(s["q_done"], c * 4 + 4)
                    pe.wait_ge(s["k_done"], c + 1)
                    pe.wait_ge(s["m_done"], c + 1)
                wait(pe, s["shifted"], n * 2)
                for g in range(2):
                    nc.tensor.matmul(score[:, g, 0:4 * C], identb[:, :],
                                     m_neg[u][:, t, :].unsqueeze(1).broadcast_to([P, 4, C]), start=True, stop=False, skip_group_check=True)
                for f in range(4):
                    for g in range(2):
                        mm = nc.tensor.matmul(score[:, g, f * C:(f + 1) * C], q_t[u][g * HD:(g + 1) * HD, f, t * P:(t + 1) * P],
                                              k_t[u][g * HD:(g + 1) * HD, f, 0:C], start=False, stop=(f == 3), skip_group_check=True)
                mm.then_inc(s["scored"], 1)

            def turn_p(n, r):
                pe.wait_ge(s["exped"], n + 1)
                wait(pe, s["o_lo_done"], n - 1)
                for g in range(2):
                    for f in range(4):
                        mm = nc.tensor.transpose(turn[0:C, g, f * P:(f + 1) * P], probs[:, r, 2 * f + g, :], ident[:, :])
                    mm.then_inc(s["p_turned"], 1)

            def attend(n, r, c, u):
                pe.wait_ge(s["p_moved"], n * 2 + 2)
                pe.wait_ge(s["v_done"], c + 1)
                wait(pe, s["att_done"], n * 2)
                wait(pe, s["y_done"], n - 1)
                for g in range(2):
                    for f in range(4):
                        mm = nc.tensor.matmul(mix[:, g, f * (HD + 1):(f + 1) * (HD + 1)], p_t[r][:, 2 * f + g, :],
                                              v_n[u][:, 2 * f + g, :], start=(f == 0), stop=(f == 3), skip_group_check=True)
                    mm.then_inc(s["mixed"], 1)

            def turn_o(n, r):
                pe.wait_ge(s["att_done"], n * 2 + 2)
                for k in range(K):
                    mm = nc.tensor.transpose(turn[:, 0, k * P:(k + 1) * P], att[:, r, k * P:(k + 1) * P], ident[:, :])
                mm.then_inc(s["o_turned"], 1)

            def project_o(n, final):
                pe.wait_ge(s["o_lo_done"], n + 1)
                pe.wait_ge(s["att_done"], n * 2 + (2 if final else 3))
                for k in range(K):
                    for m, (o, a) in enumerate(((o_hi, wo[0]), (o_lo, wo[0]), (o_hi, wo[1]))):
                        mm = nc.tensor.matmul(mix[:, 0, :], o[:, k, :], a[:, k, :], start=(k == 0 and m == 0), stop=(k == K - 1 and m == 2))
                mm.then_inc(s["y_mm"], 1)

            pe.wait_ge(s["pool_consts"], 4)
            for k in range(K):
                turn_x(0, k)
            for f in range(K):
                project_q(0, f)
            project_k(0)
            project_v(0)
            scores(0, 0, 0, 0)

            def emit(b, u, first, last):
                for t in range(4):
                    n = b * 4 + t
                    r = t % 2
                    turn_p(n, r)
                    if not last:
                        if t == 1:
                            turn_x(b + 1, 2)
                            turn_x(b + 1, 3)
                        elif t == 2:
                            project_q(b + 1, 1)
                            project_q(b + 1, 2)
                        elif t == 3:
                            project_v(b + 1)
                    attend(n, r, b, u)
                    if not (first and t == 0):
                        turn_o(n - 1, 1 - r)
                    if t < 3:
                        scores(n + 1, b, u, t + 1)
                    elif not last:
                        scores(n + 1, b + 1, 1 - u, 0)
                    if not last:
                        if t == 0:
                            turn_x(b + 1, 0)
                            turn_x(b + 1, 1)
                        elif t == 1:
                            project_q(b + 1, 0)
                        elif t == 2:
                            project_q(b + 1, 3)
                            project_k(b + 1)
                    if not (first and t == 0):
                        project_o(n - 1, False)

            batches(pe, NB, emit)
            turn_o(N - 1, 1)
            project_o(N - 1, True)

        @block.scalar
        def _(act):
            def x_high(c, k):
                act.wait_ge(s["x_turned"], c * 4 + k + 1)
                wait(act, s["q_mm"], c * 4)
                nc.scalar.activation(xt_hi[:, k, :], wide[:, k % 2, :], ACT.Copy).then_inc(s["xt_hi_done"], 1)

            def q_out(c, u, f):
                act.wait_ge(s["q_mm"], c * 4 + f + 1)
                nc.scalar.activation(q_t[u][:, f, :], wide[:, f % 2, :], ACT.Identity, bias=bq_c[:, f:f + 1], scale=SCALE).then_inc(s["q_done"], 1)

            def c_high(c):
                act.wait_ge(s["c_loaded"], c * 16 + 16)
                wait(act, s["v_mm"], c)
                nc.scalar.activation(c_hi[:, :, :], c_in[:, :, :], ACT.Copy).then_inc(s["c_hi_done"], 1)

            def exp(n, r):
                act.wait_ge(s["shifted"], n * 2 + 2)
                wait(act, s["p_turned"], n * 2 - 2)
                nc.scalar.activation(probs[:, r, :, :], e_in[:, :, :], ACT.Exp).then_inc(s["exped"], 1)

            def p_out(n, r):
                wait(act, s["mixed"], n * 2 - 2)
                for g in range(2):
                    act.wait_ge(s["p_turned"], n * 2 + g + 1)
                    nc.scalar.activation(p_t[r][:, g::2, :], turn[0:C, g, :].rearrange("c (f p) -> c f p", f=4), ACT.Copy).then_inc(s["p_moved"], 1)

            def o_high(n):
                act.wait_ge(s["o_turned"], n + 1)
                wait(act, s["y_mm"], n)
                nc.scalar.activation(o_hi[:, :, :], turn[:, 0, :].rearrange("p (k m) -> p k m", k=K), ACT.Copy).then_inc(s["o_hi_done"], 1)

            act.wait_ge(s["bias_scaled"], 1)
            for k in range(K):
                x_high(0, k)
            c_high(0)
            for f in range(K):
                q_out(0, 0, f)

            def k_out(c, u):
                act.wait_ge(s["k_mm"], c + 1)
                for f in range(K):
                    ins = nc.scalar.activation(k_t[u][:, f, :], wide[:, 0, f * CP:(f + 1) * CP], ACT.Identity, bias=bk_c[:, f:f + 1])
                ins.then_inc(s["k_done"], 1)

            k_out(0, 0)
            exp(0, 0)

            def emit(b, u, first, last):
                for t in range(4):
                    n = b * 4 + t
                    p_out(n, t % 2)
                    if not last:
                        if t == 1:
                            x_high(b + 1, 2)
                            x_high(b + 1, 3)
                        elif t == 2:
                            q_out(b + 1, 1 - u, 1)
                            q_out(b + 1, 1 - u, 2)
                    if not (first and t == 0):
                        o_high(n - 1)
                    if not (last and t == 3):
                        exp(n + 1, 1 - t % 2)
                    if not last:
                        if t == 0:
                            x_high(b + 1, 0)
                            x_high(b + 1, 1)
                            c_high(b + 1)
                        elif t == 1:
                            q_out(b + 1, 1 - u, 0)
                        elif t == 2:
                            q_out(b + 1, 1 - u, 3)
                            k_out(b + 1, 1 - u)

            batches(act, NB, emit)
            o_high(N - 1)

        @block.gpsimd
        def _(pool):
            nc.gpsimd.memset(c_in[:, :, C:CP], 0.0).then_inc(s["pool_consts"], 1)
            for u in range(2):
                nc.gpsimd.memset(v_n[u][:, :, HD:HD + 1], 1.0).then_inc(s["pool_consts"], 1)
            nc.gpsimd.memset(half[:, :], -0.5).then_inc(s["pool_consts"], 1)

            def bias_x(b, t):
                pool.wait_ge(r_loaded[t % 2], b * 32 + (t // 2) * 16 + 16)
                nc.gpsimd.tensor_tensor(x_res[:, t % 2, :], x_res[:, t % 2, :], bo_b[:, :], ALU.add).then_inc(s["x_biased"], 1)

            def power(n, r):
                pool.wait_ge(s["var_done"], n + 1)
                nc.gpsimd.tensor_tensor(rstd[:, r, :], var[:, r, :], half[:, :], ALU.pow).then_inc(s["powed"], 1)

            pool.wait_ge(s["consts_loaded"], 64)

            def emit(b, u, first, last):
                for t in range(4):
                    bias_x(b, t)
                    if not (first and t == 0):
                        power(b * 4 + t - 1, 1 - t % 2)

            batches(pool, NB, emit)
            power(N - 1, 1)

        @block.vector
        def _(dve):
            def x_low(c, k):
                dve.wait_ge(s["xt_hi_done"], c * 4 + k + 1)
                nc.vector.tensor_tensor(xt_lo[:, k, :], wide[:, k % 2, :], xt_hi[:, k, :], ALU.subtract).then_inc(s["xt_lo_done"], 1)

            def c_low(c):
                dve.wait_ge(s["c_hi_done"], c + 1)
                nc.vector.tensor_tensor(c_lo[:, :, :], c_in[:, :, :], c_hi[:, :, :], ALU.subtract).then_inc(s["c_lo_done"], 1)

            def v_out(c, u):
                dve.wait_ge(s["v_mm"], c + 1)
                nc.vector.tensor_tensor(v_n[u][:, :, 0:HD], wide[0:C, 1, :].rearrange("c (h d) -> c h d", h=XH),
                                        bv_b[0:C, :].rearrange("c (h d) -> c h d", h=XH), ALU.add).then_inc(s["v_done"], 1)

            def mask_out(c, u):
                dve.wait_ge(s["m_loaded"], c * 16 + 16)
                nc.vector.tensor_scalar(m_neg[u][:, :, :], m_in[:, :, :], 1.0, 1e30, ALU.subtract, ALU.mult).then_inc(s["m_done"], 1)
                nc.vector.tensor_reduce(keep[:, u, :], m_in[:, :, :], AX, ALU.max).then_inc(s["keep_done"], 1)

            def shift(n, r):
                dve.wait_ge(s["scored"], n + 1)
                for g in range(2):
                    nc.vector.tensor_reduce(top[:, r, g::2], score[:, g, 0:4 * C].rearrange("p (f c) -> p f c", f=4), AX, ALU.max).then_inc(s["topped"], 1)
                wait(dve, s["exped"], n)
                for g in range(2):
                    dve.wait_ge(s["topped"], n * 2 + g + 1)
                    nc.vector.tensor_tensor(e_in[:, g::2, :], score[:, g, 0:4 * C].rearrange("p (f c) -> p f c", f=4),
                                            top[:, r, g::2].unsqueeze(2).broadcast_to([P, 4, C]), ALU.subtract).then_inc(s["shifted"], 1)

            def attended(n, r, c, u, t):
                for g in range(2):
                    dve.wait_ge(s["mixed"], n * 2 + g + 1)
                    nc.vector.reciprocal(rec[:, r, g::2], mix[:, g, 0:4 * (HD + 1)].rearrange("p (f c) -> p f c", f=4)[:, :, HD]).then_inc(s["recd"], 1)
                for g in range(2):
                    dve.wait_ge(s["recd"], n * 2 + g + 1)
                    if g == 0:
                        dve.wait_ge(s["recd"], n * 2 + 2)
                        dve.wait_ge(s["keep_done"], c + 1)
                        nc.vector.tensor_scalar(rec[:, r, :], rec[:, r, :], keep[:, u, t:t + 1], None, ALU.mult).then_inc(s["kept"], 1)
                        dve.wait_ge(s["kept"], n + 1)
                        wait(dve, s["o_turned"], n - 1)
                    nc.vector.tensor_tensor(att[:, r, :].rearrange("p (f g d) -> p g f d", g=2, f=4)[:, g],
                                            mix[:, g, 0:4 * (HD + 1)].rearrange("p (f c) -> p f c", f=4)[:, :, 0:HD],
                                            rec[:, r, g::2].unsqueeze(2).broadcast_to([P, 4, HD]), ALU.mult).then_inc(s["att_done"], 1)

            def o_low(n):
                dve.wait_ge(s["o_hi_done"], n + 1)
                nc.vector.tensor_tensor(o_lo[:, :, :], turn[:, 0, :].rearrange("p (k m) -> p k m", k=K), o_hi[:, :, :], ALU.subtract).then_inc(s["o_lo_done"], 1)

            def add(n, r):
                dve.wait_ge(s["y_mm"], n + 1)
                dve.wait_ge(s["x_biased"], n + 1)
                nc.vector.tensor_tensor(y[:, r, :], mix[:, 0, :], x_res[:, r, :], ALU.add).then_inc(s["y_done"], 1)
                dve.wait_ge(s["y_done"], n + 1)
                nc.vector.bn_stats(st[:, r, :], y[:, r, :]).then_inc(s["stats"], 1)
                dve.wait_ge(s["stats"], n + 1)
                dve.sem_inc(s["stats_seen"], 1)
                nc.vector.bn_aggr(mv[:, r, :], st[:, r, :]).then_inc(s["aggr"], 1)
                dve.wait_ge(s["aggr"], n + 1)
                wait(dve, s["powed"], n - 1)
                nc.vector.tensor_scalar(var[:, r, :], mv[:, r, 1:2], LN_EPS, None, ALU.add).then_inc(s["var_done"], 1)

            def norm(n, r, slot_uses):
                dve.wait_ge(s["powed"], n + 1)
                wait(dve, s["absmaxed"], n - 1)
                wait(dve, stored[r], slot_uses)
                nc.vector.tensor_scalar(x_out[:, r, :], y[:, r, :], mv[:, r, 0:1], rstd[:, r, :], ALU.subtract, ALU.mult).then_inc(s["normed"], 1)
                dve.wait_ge(s["normed"], n + 1)
                nc.vector.tensor_reduce(x_top[:, bass.ds(n, 1)], x_out[:, r, :], AX, ALU.max, apply_absolute_value=True).then_inc(s["absmaxed"], 1)

            dve.wait_ge(s["consts_loaded"], 64)
            nc.vector.tensor_scalar(bq_c[:, :], bq_c[:, :], SCALE, None, ALU.mult).then_inc(s["bias_scaled"], 1)
            mask_out(0, 0)
            for k in range(K):
                x_low(0, k)
            c_low(0)
            v_out(0, 0)
            shift(0, 0)

            def emit(b, u, first, last):
                for t in range(4):
                    n = b * 4 + t
                    r = t % 2
                    if not last:
                        if t == 1:
                            x_low(b + 1, 2)
                            x_low(b + 1, 3)
                        elif t == 3:
                            v_out(b + 1, 1 - u)
                    attended(n, r, b, u, t)
                    if not (first and t == 0):
                        o_low(n - 1)
                    if t == 2 and not last:
                        mask_out(b + 1, 1 - u)
                    if not (last and t == 3):
                        shift(n + 1, 1 - r)
                    if not last and t == 0:
                        x_low(b + 1, 0)
                        x_low(b + 1, 1)
                        c_low(b + 1)
                    if not (first and t < 2):
                        norm(n - 2, r, b * 32 - 16 if t < 2 else b * 32)
                    if not (first and t == 0):
                        add(n - 1, 1 - r)

            batches(dve, NB, emit)
            o_low(N - 1)
            norm(N - 2, 0, 32 * NB - 16)
            add(N - 1, 1)
            norm(N - 1, 1, 32 * NB - 16)


def ffn_weights_stage(nc, ident, jobs, tag):
    steps = [(src, hi, lo, r, c) for src, hi, lo in jobs
             for r in range(src.shape[0]) for c in range(src.shape[2] // D)]
    G = D // QBLOCK
    with ExitStack() as ctx:
        def sb(name, shape, dt=F32):
            return ctx.enter_context(nc.sbuf_tensor(f"{tag}_{name}", shape, dt))

        def sem(name):
            return nc.alloc_semaphore(f"{tag}_{name}")

        w_in = sb("w_in", [P, 2, D])
        w_int = sb("w_int", [P, 2, D], I16)
        w_deq = sb("w_deq", [P, 2, D])
        w_top = sb("w_top", [P, 2, G])
        w_scale = sb("w_scale", [P, 2, G])
        w_inv = sb("w_inv", [P, 2, G])
        w_psum = ctx.enter_context(nc.psum_tensor(f"{tag}_w_psum", [P, 2, D], F32))
        loaded = [sem("w_loaded0"), sem("w_loaded1")]
        topped, scaled, floored, inverted = sem("w_topped"), sem("w_scaled"), sem("w_floored"), sem("w_inverted")
        rounded, dequant, turned = sem("w_rounded"), sem("w_dequant"), sem("w_turned")
        hi_done, lo_done = sem("w_hi_done"), sem("w_lo_done")
        block = ctx.enter_context(nc.Block())

        @block.sync
        def _(sp):
            for n, (src, hi, lo, r, c) in enumerate(steps):
                if n >= 2:
                    sp.wait_ge(rounded, n - 1)
                sp.dma_start(w_in[:, n % 2, :], src[r, :, c * D:(c + 1) * D]).then_inc(loaded[n % 2], 16)

        @block.vector
        def _(dve):
            def finish(n):
                src, hi, lo, r, c = steps[n]
                dve.wait_ge(hi_done, n + 1)
                K = D // P
                nc.vector.tensor_tensor(lo[:, c * K:(c + 1) * K, r * P:(r + 1) * P],
                                        w_psum[:, n % 2, :].rearrange("p (k m) -> p k m", k=K),
                                        hi[:, c * K:(c + 1) * K, r * P:(r + 1) * P], ALU.subtract).then_inc(lo_done, 1)

            for n, (src, hi, lo, r, c) in enumerate(steps):
                s = n % 2
                blocks = w_in[:, s, :].rearrange("p (g e) -> p g e", e=QBLOCK)
                dve.wait_ge(loaded[s], 16 * (n // 2 + 1))
                nc.vector.tensor_reduce(w_top[:, s, :], blocks, AX, ALU.max, apply_absolute_value=True).then_inc(topped, 1)
                dve.wait_ge(topped, n + 1)
                nc.vector.tensor_scalar(w_scale[:, s, :], w_top[:, s, :], 1.0 / WQMAX, 1e-12, ALU.mult, ALU.max).then_inc(scaled, 1)
                dve.wait_ge(scaled, n + 1)
                nc.vector.reciprocal(w_inv[:, s, :], w_scale[:, s, :]).then_inc(inverted, 1)
                dve.wait_ge(inverted, n + 1)
                nc.vector.tensor_tensor(w_int[:, s, :].rearrange("p (g e) -> p g e", e=QBLOCK), blocks,
                                        w_inv[:, s, :].unsqueeze(2).broadcast_to([P, G, QBLOCK]), ALU.mult).then_inc(rounded, 1)
                dve.wait_ge(rounded, n + 1)
                if n >= 2:
                    dve.wait_ge(turned, n - 1)
                nc.vector.tensor_tensor(w_deq[:, s, :].rearrange("p (g e) -> p g e", e=QBLOCK),
                                        w_int[:, s, :].rearrange("p (g e) -> p g e", e=QBLOCK),
                                        w_scale[:, s, :].unsqueeze(2).broadcast_to([P, G, QBLOCK]), ALU.mult).then_inc(dequant, 1)
                if n >= 1:
                    finish(n - 1)
            finish(len(steps) - 1)

        @block.tensor
        def _(pe):
            for n in range(len(steps)):
                pe.wait_ge(dequant, n + 1)
                if n >= 2:
                    pe.wait_ge(lo_done, n - 1)
                for k in range(D // P):
                    last = nc.tensor.transpose(w_psum[:, n % 2, k * P:(k + 1) * P], w_deq[:, n % 2, k * P:(k + 1) * P], ident[:, :])
                last.then_inc(turned, 1)

        @block.scalar
        def _(act):
            for n, (src, hi, lo, r, c) in enumerate(steps):
                K = D // P
                act.wait_ge(turned, n + 1)
                nc.scalar.activation(hi[:, c * K:(c + 1) * K, r * P:(r + 1) * P],
                                     w_psum[:, n % 2, :].rearrange("p (k m) -> p k m", k=K), ACT.Copy).then_inc(hi_done, 1)


def scale_stage(nc, jobs, tag, extra=None):
    with ExitStack() as ctx:
        def sem(name):
            return nc.alloc_semaphore(f"{tag}_{name}")

        part = ctx.enter_context(nc.sbuf_tensor(f"{tag}_part", [P, len(jobs)], F32))
        total = ctx.enter_context(nc.sbuf_tensor(f"{tag}_total", [P, len(jobs)], F32))
        reduced, everywhere, step = sem("reduced"), sem("everywhere"), sem("step")
        block = ctx.enter_context(nc.Block())

        @block.vector
        def _(dve):
            for n, (maxima, result) in enumerate(jobs):
                nc.vector.tensor_reduce(part[:, n:n + 1], maxima, AX, ALU.max).then_inc(reduced, 1)
            dve.wait_ge(everywhere, 1)
            count = 0
            for n, (maxima, result) in enumerate(jobs):
                nc.vector.tensor_copy(result[:, 0:1], total[:, n:n + 1]).then_inc(step, 1)
                nc.vector.tensor_scalar(result[:, 1:2], total[:, n:n + 1], 1.0 / QMAX, 1e-12, ALU.mult, ALU.max).then_inc(step, 1)
                count += 2
                dve.wait_ge(step, count)
                nc.vector.reciprocal(result[:, 2:3], result[:, 1:2]).then_inc(step, 1)
                count += 1
            dve.wait_ge(step, count)
            if extra is not None:
                extra(dve, step, count)

        @block.gpsimd
        def _(pool):
            pool.wait_ge(reduced, len(jobs))
            nc.gpsimd.partition_all_reduce(total[:, :], part[:, :], P, RMAX).then_inc(everywhere, 1)


def gate_up_stage(nc, ident, x2, gu, wg_hi, wg_lo, wu_hi, wu_lo, xs, gu_top, NBLK):
    K = D // P
    J = 2 * HID // P
    NG = J // 4
    with ExitStack() as ctx:
        def sb(name, shape, dt=F32):
            return ctx.enter_context(nc.sbuf_tensor("gu_" + name, shape, dt))

        def sem(name):
            return nc.alloc_semaphore("gu_" + name)

        x_in = sb("x_in", [P, 4, D])
        x_int = sb("x_int", [P, 4, D], I16)
        x_q = sb("x_q", [P, 4, D])
        xt_hi = [sb(f"xt_hi{u}", [P, K, TB], F32R) for u in range(2)]
        xt_lo = [sb(f"xt_lo{u}", [P, K, TB], F32R) for u in range(2)]
        stage = sb("stage", [P, 4, 4, TB])
        acc = ctx.enter_context(nc.psum_tensor("gu_acc", [P, 4, TB], F32))
        turn = ctx.enter_context(nc.psum_tensor("gu_turn", [P, 2, TB], F32))
        x_loaded, x_rounded, x_ready = sem("x_loaded"), sem("x_rounded"), sem("x_ready")
        turned, hi_done, lo_done = sem("turned"), sem("hi_done"), sem("lo_done")
        products, evacuated, topped = sem("products"), sem("evacuated"), sem("topped")
        stored = [sem(f"stored{s}") for s in range(4)]
        block = ctx.enter_context(nc.Block())
        NPAIR = NBLK // 2

        def pairs(eng, body):
            if NPAIR > 1:
                with eng.Fori(0, NPAIR - 1) as i:
                    for u in range(2):
                        body(i, i * 2 + u, u, False)
            for u in range(2):
                body(NPAIR - 1, (NPAIR - 1) * 2 + u, u, u == 1)

        @block.sync
        def _(sp):
            def load(b):
                sp.dma_start(x_in[:, :, :], x2[bass.ds(b, 1), :, :, :].rearrange("b p t d -> p (b t) d")).then_inc(x_loaded, 16)

            for s in range(4):
                sp.sem_inc(stored[s], 16)
            load(0)

            def body(i, b, u, last):
                if not last:
                    sp.wait_ge(x_rounded, b + 1)
                    load(b + 1)
                for g in range(NG):
                    sp.wait_ge(topped, b * J + 4 * g + 4)
                    s = (u * NG + g) % 4
                    sp.dma_start(gu[bass.ds(b, 1), :, 4 * g:4 * g + 4, :].rearrange("b p j t -> p (b j) t"),
                                 stage[:, s, :, :]).then_inc(stored[s], 16)

            pairs(sp, body)
            for s in range(4):
                sp.wait_ge(stored[s], 16 + 16 * NBLK * NG // 4)

        @block.tensor
        def _(pe):
            def transposes(b, k, first):
                if k == 0:
                    pe.wait_ge(x_ready, b + 1)
                if not first or k >= 2:
                    pe.wait_ge(lo_done, b * K + k - 1)
                for t in range(4):
                    last = nc.tensor.transpose(turn[:, k % 2, t * P:(t + 1) * P], x_q[:, t, k * P:(k + 1) * P], ident[:, :])
                last.then_inc(turned, 1)

            for k in range(K):
                transposes(0, k, True)

            def body(i, b, u, last):
                pe.wait_ge(lo_done, b * K + K)
                pe.wait_ge(hi_done, b * K + K)
                for j in range(J):
                    pe.wait_ge(evacuated, b * J + j + 1)
                    whi, wlo = (wg_hi, wg_lo) if j < J // 2 else (wu_hi, wu_lo)
                    c = j % (J // 2)
                    for k in range(K):
                        for n, (w, x) in enumerate(((whi, xt_hi[u]), (whi, xt_lo[u]), (wlo, xt_hi[u]))):
                            mm = nc.tensor.matmul(acc[:, j % 4, :], w[:, k, c * P:(c + 1) * P], x[:, k, :],
                                                    start=(k == 0 and n == 0), stop=(k == K - 1 and n == 2))
                    mm.then_inc(products, 1)
                    if j in (12, 14, 16, 18) and not last:
                        transposes(b + 1, (j - 12) // 2, False)

            pairs(pe, body)

        @block.scalar
        def _(act):
            def round_x(b):
                act.wait_ge(x_loaded, b * 16 + 16)
                if not isinstance(b, int) or b > 0:
                    act.wait_ge(x_ready, b)
                nc.scalar.activation(x_int[:, :, :], x_in[:, :, :], ACT.Copy, scale=xs[:, 2:3]).then_inc(x_rounded, 1)

            def high(b, k, u):
                act.wait_ge(turned, b * K + k + 1)
                nc.scalar.activation(xt_hi[u][:, k, :], turn[:, k % 2, :], ACT.Copy).then_inc(hi_done, 1)

            act.sem_inc(evacuated, 4)
            round_x(0)
            for k in range(K):
                high(0, k, 0)

            def body(i, b, u, last):
                if not last:
                    round_x(b + 1)
                for j in range(J):
                    act.wait_ge(products, b * J + j + 1)
                    g = u * NG + j // 4
                    if j % 4 == 0:
                        act.wait_ge(stored[g % 4], (i * (2 * NG // 4) + g // 4) * 16 + 16)
                    nc.scalar.activation(stage[:, g % 4, j % 4, :], acc[:, j % 4, :], ACT.Copy, scale=xs[:, 1:2]).then_inc(evacuated, 1)
                    if j in (13, 15, 17, 19) and not last:
                        high(b + 1, (j - 13) // 2, 1 - u)

            pairs(act, body)

        @block.vector
        def _(dve):
            def float_x(b):
                dve.wait_ge(x_rounded, b + 1)
                if not isinstance(b, int) or b > 0:
                    dve.wait_ge(turned, b * K)
                nc.vector.tensor_copy(x_q[:, :, :], x_int[:, :, :]).then_inc(x_ready, 1)

            def low(b, k, u):
                dve.wait_ge(hi_done, b * K + k + 1)
                nc.vector.tensor_tensor(xt_lo[u][:, k, :], turn[:, k % 2, :], xt_hi[u][:, k, :], ALU.subtract).then_inc(lo_done, 1)

            float_x(0)
            for k in range(K):
                low(0, k, 0)

            def body(i, b, u, last):
                if not last:
                    float_x(b + 1)
                for j in range(J):
                    g = u * NG + j // 4
                    dve.wait_ge(evacuated, b * J + j + 5)
                    nc.vector.tensor_reduce(gu_top[:, j // (J // 2), bass.ds(b * (J // 2) + j % (J // 2), 1)],
                                            stage[:, g % 4, j % 4, :], AX, ALU.max,
                                            apply_absolute_value=True).then_inc(topped, 1)
                    if j in (13, 15, 17, 19) and not last:
                        low(b + 1, (j - 13) // 2, 1 - u)

            pairs(dve, body)


def product_stage(nc, gu, prod, xs, ms, prod_top, NBLK):
    J = HID // P
    NG = J // 4
    F = 4 * TB
    with ExitStack() as ctx:
        def sb(name, dt=F32):
            return ctx.enter_context(nc.sbuf_tensor("pr_" + name, [P, NG, F], dt))

        def sem(name):
            return nc.alloc_semaphore("pr_" + name)

        g_in, u_in, sig, prd = sb("g_in"), sb("u_in"), sb("sig"), sb("prd")
        g_int, s_int, h_int, u_int = sb("g_int", I16), sb("s_int", U16), sb("h_int", I16), sb("u_int", I16)
        loaded_g = [sem(f"loaded_g{s}") for s in range(NG)]
        loaded_u = [sem(f"loaded_u{s}") for s in range(NG)]
        stored = [sem(f"stored{s}") for s in range(NG)]
        u_seen = sem("u_seen")
        g_rounded, sig_done, s_rounded, silu_done = sem("g_rounded"), sem("sig_done"), sem("s_rounded"), sem("silu_done")
        h_rounded, u_rounded, prod_done, topped = sem("h_rounded"), sem("u_rounded"), sem("prod_done"), sem("topped")
        block = ctx.enter_context(nc.Block())

        @block.sync
        def _(sp):
            def load(b, s):
                sp.dma_start(g_in[:, s, :], gu[bass.ds(b, 1), :, 4 * s:4 * s + 4, :].rearrange("b p j t -> p (b j t)")).then_inc(loaded_g[s], 16)
                sp.dma_start(u_in[:, s, :], gu[bass.ds(b, 1), :, J + 4 * s:J + 4 * s + 4, :].rearrange("b p j t -> p (b j t)")).then_inc(loaded_u[s], 16)

            for s in range(NG):
                load(0, s)
            if NBLK > 1:
                with sp.Fori(0, NBLK - 1) as b:
                    for s in range(NG):
                        sp.wait_ge(g_rounded, b * NG + s + 1)
                        sp.wait_ge(u_rounded, b * NG + s + 1)
                        load(b + 1, s)

        @block.scalar
        def _(act):
            def store(b, s):
                act.wait_ge(topped, b * NG + s + 1)
                act.dma_start(prod[bass.ds(b, 1), :, 4 * s:4 * s + 4, :].rearrange("b p j t -> p (b j t)"), prd[:, s, :]).then_inc(stored[s], 16)

            for s in range(NG):
                act.sem_inc(stored[s], 16)
            with act.Fori(0, NBLK) as b:
                for s in range(NG):
                    act.wait_ge(loaded_g[s], b * 16 + 16)
                    nc.scalar.activation(g_int[:, s, :], g_in[:, s, :], ACT.Copy, scale=ms[:, 0:1]).then_inc(g_rounded, 1)
                    act.wait_ge(g_rounded, b * NG + s + 1)
                    nc.scalar.activation(sig[:, s, :], g_int[:, s, :], ACT.Sigmoid, scale=ms[:, 1:2]).then_inc(sig_done, 1)
                for s in range(NG):
                    act.wait_ge(silu_done, b * NG + s + 1)
                    nc.scalar.activation(h_int[:, s, :], sig[:, s, :], ACT.Copy, scale=ms[:, 2:3]).then_inc(h_rounded, 1)
                for s in range(NG):
                    store(b, s)
            for s in range(NG):
                act.wait_ge(stored[s], 16 + NBLK * 16)

        @block.gpsimd
        def _(pool):
            with pool.Fori(0, NBLK) as b:
                for s in range(NG):
                    pool.wait_ge(loaded_u[s], b * 16 + 16)
                    pool.wait_ge(prod_done, b * NG + s + 1)
                    pool.sem_inc(u_seen, 1)
                    nc.gpsimd.tensor_scalar(u_int[:, s, :], u_in[:, s, :], ms[:, 3:4], None, ALU.mult).then_inc(u_rounded, 1)

        @block.vector
        def _(dve):
            dve.sem_inc(prod_done, NG)
            with dve.Fori(0, NBLK) as b:
                for s in range(NG):
                    dve.wait_ge(sig_done, b * NG + s + 1)
                    nc.vector.tensor_scalar(s_int[:, s, :], sig[:, s, :], 65536.0, 65535.0, ALU.mult, ALU.min).then_inc(s_rounded, 1)
                    dve.wait_ge(s_rounded, b * NG + s + 1)
                    nc.vector.scalar_tensor_tensor(sig[:, s, :], g_int[:, s, :], ms[:, 1:2], s_int[:, s, :], ALU.mult, ALU.mult).then_inc(silu_done, 1)
                for s in range(NG):
                    dve.wait_ge(h_rounded, b * NG + s + 1)
                    dve.wait_ge(u_rounded, b * NG + s + 1)
                    dve.wait_ge(stored[s], b * 16 + 16)
                    nc.vector.tensor_tensor(prd[:, s, :], h_int[:, s, :], u_int[:, s, :], ALU.mult).then_inc(prod_done, 1)
                    dve.wait_ge(prod_done, b * NG + s + 1 + NG)
                    nc.vector.tensor_reduce(prod_top[:, bass.ds(b * NG + s, 1)], prd[:, s, :], AX, ALU.max,
                                            apply_absolute_value=True).then_inc(topped, 1)


def down_stage(nc, prod, x2, out, wd_hi, wd_lo, ms, NBLK):
    J = HID // P
    with ExitStack() as ctx:
        def sb(name, shape, dt=F32):
            return ctx.enter_context(nc.sbuf_tensor("dn_" + name, shape, dt))

        def sem(name):
            return nc.alloc_semaphore("dn_" + name)

        p_in = sb("p_in", [P, J, TB])
        p_int = sb("p_int", [P, J, TB], I16)
        o_hi, o_lo = sb("o_hi", [P, J, TB], F32R), sb("o_lo", [P, J, TB], F32R)
        x_in = sb("x_in", [P, 2, D])
        y = sb("y", [P, 2, D])
        st = sb("st", [P, 2, 6])
        mv = sb("mv", [P, 2, 2])
        sd = sb("sd", [P, 2, 1])
        rs = sb("rs", [P, 2, 1])
        eps = sb("eps", [P, 1])
        acc = ctx.enter_context(nc.psum_tensor("dn_acc", [P, 4, D], F32))
        loaded, rounded, hi_done, lo_done = sem("loaded"), sem("rounded"), sem("hi_done"), sem("lo_done")
        products, added, stats, aggr, root, inv, normed = sem("products"), sem("added"), sem("stats"), sem("aggr"), sem("root"), sem("inv"), sem("normed")
        eps_set, stats_seen = sem("eps_set"), sem("stats_seen")
        x_loaded = [sem(f"x_loaded{s}") for s in range(2)]
        stored = [sem(f"stored{s}") for s in range(2)]
        block = ctx.enter_context(nc.Block())

        @block.sync
        def _(sp):
            def load(b):
                sp.dma_start(p_in[:, :, :], prod[bass.ds(b, 1), :, :, :].rearrange("b p j t -> p (b j) t")).then_inc(loaded, 16)

            def load_x(b, t):
                sp.dma_start(x_in[:, t % 2, :], x2[bass.ds(b, 1), :, t, :].rearrange("b p d -> p (b d)")).then_inc(x_loaded[t % 2], 16)

            sp.sem_inc(stored[0], 16)
            sp.sem_inc(stored[1], 16)
            load(0)

            def body(b, last):
                for t in range(4):
                    sp.wait_ge(added, b * 4 + t + 1)
                    load_x(b, t)
                    if t == 0 and not last:
                        sp.wait_ge(rounded, b * 2 + 2)
                        load(b + 1)
                    if t > 0:
                        store(b, t - 1)
                store(b, 3)

            def store(b, t):
                sp.wait_ge(normed, b * 4 + t + 1)
                sp.dma_start(out[bass.ds(b, 1), :, t, :].rearrange("b p d -> p (b d)"), y[:, t % 2, :]).then_inc(stored[t % 2], 16)

            with sp.Fori(0, NBLK - 1) as b:
                body(b, False)
            body(NBLK - 1, True)
            for s in range(2):
                sp.wait_ge(stored[s], 16 + NBLK * 32)

        @block.scalar
        def _(act):
            act.wait_ge(eps_set, 1)
            with act.Fori(0, NBLK) as b:
                act.wait_ge(loaded, b * 16 + 16)
                for h in range(2):
                    act.wait_ge(lo_done, b * 2 + h + 1)
                    s = slice(h * J // 2, (h + 1) * J // 2)
                    nc.scalar.activation(p_int[:, s, :], p_in[:, s, :], ACT.Copy, scale=ms[:, 4:5]).then_inc(rounded, 1)
                for h in range(2):
                    s = slice(h * J // 2, (h + 1) * J // 2)
                    act.wait_ge(rounded, b * 2 + h + 1)
                    act.wait_ge(products, b * 4 + 4)
                    nc.scalar.activation(o_hi[:, s, :], p_int[:, s, :], ACT.Copy).then_inc(hi_done, 1)
                for t in range(4):
                    act.wait_ge(aggr, b * 4 + t + 1)
                    nc.scalar.activation(sd[:, t % 2, :], mv[:, t % 2, 1:2], ACT.Sqrt, bias=eps[:, :]).then_inc(root, 1)

        @block.tensor
        def _(pe):
            pe.sem_inc(products, 4)
            with pe.Fori(0, NBLK) as b:
                for t in range(4):
                    if t == 0:
                        pe.wait_ge(lo_done, b * 2 + 4)
                    pe.wait_ge(added, b * 4 + t + 1)
                    for j in range(J):
                        for n, (o, w) in enumerate(((o_hi, wd_hi), (o_hi, wd_lo), (o_lo, wd_hi))):
                            last = nc.tensor.matmul(acc[:, t, :], o[:, j, t * P:(t + 1) * P], w[:, j, :],
                                                    start=(j == 0 and n == 0), stop=(j == J - 1 and n == 2))
                    last.then_inc(products, 1)

        @block.vector
        def _(dve):
            nc.vector.memset(eps[:, :], LN_EPS).then_inc(eps_set, 1)
            dve.sem_inc(lo_done, 2)
            dve.sem_inc(added, 2)
            with dve.Fori(0, NBLK) as b:
                for h in range(2):
                    s = slice(h * J // 2, (h + 1) * J // 2)
                    dve.wait_ge(hi_done, b * 2 + h + 1)
                    nc.vector.tensor_tensor(o_lo[:, s, :], p_int[:, s, :], o_hi[:, s, :], ALU.subtract).then_inc(lo_done, 1)
                for t in range(4):
                    u = t % 2
                    dve.wait_ge(products, b * 4 + t + 5)
                    dve.wait_ge(x_loaded[u], b * 32 + (t // 2) * 16 + 16)
                    dve.wait_ge(stored[u], b * 32 + (t // 2) * 16 + 16)
                    nc.vector.scalar_tensor_tensor(y[:, u, :], acc[:, t, :], ms[:, 5:6], x_in[:, u, :], ALU.mult, ALU.add).then_inc(added, 1)
                    dve.wait_ge(added, b * 4 + t + 3)
                    nc.vector.bn_stats(st[:, u, :], y[:, u, :]).then_inc(stats, 1)
                    dve.wait_ge(stats, b * 4 + t + 1)
                    dve.sem_inc(stats_seen, 1)
                    nc.vector.bn_aggr(mv[:, u, :], st[:, u, :]).then_inc(aggr, 1)
                    dve.wait_ge(root, b * 4 + t + 1)
                    nc.vector.reciprocal(rs[:, u, :], sd[:, u, :]).then_inc(inv, 1)
                    dve.wait_ge(inv, b * 4 + t + 1)
                    nc.vector.tensor_scalar(y[:, u, :], y[:, u, :], mv[:, u, 0:1], rs[:, u, 0:1], ALU.subtract, ALU.mult).then_inc(normed, 1)


def ffn_phase(nc, ident, x2, gu, prod, out, w_gate, w_up, w_down, x_top, NBLK):
    J = HID // P
    with ExitStack() as ctx:
        def sb(name, shape, dt=F32):
            return ctx.enter_context(nc.sbuf_tensor("ffn_" + name, shape, dt))

        xs, gs, us, hs, ps = (sb(n, [P, 4]) for n in ("xs", "gs", "us", "hs", "ps"))
        ms = sb("ms", [P, 8])
        gu_top = sb("gu_top", [P, 2, NBLK * J])
        silu_top = sb("silu_top", [P, NBLK * J // 4])
        prod_top = sb("prod_top", [P, NBLK * J // 4])
        scale_stage(nc, [(x_top[:, :], xs)], "xs")
        with ExitStack() as c2:
            wg_hi, wg_lo, wu_hi, wu_lo = (c2.enter_context(nc.sbuf_tensor("ffn_" + n, [P, D // P, HID], F32R))
                                          for n in ("wg_hi", "wg_lo", "wu_hi", "wu_lo"))
            ffn_weights_stage(nc, ident, [(w_gate, wg_hi, wg_lo), (w_up, wu_hi, wu_lo)], "wgu")
            gate_up_stage(nc, ident, x2, gu, wg_hi, wg_lo, wu_hi, wu_lo, xs, gu_top, NBLK)
        scale_stage(nc, [(gu_top[:, 0, :], gs), (gu_top[:, 1, :], us)], "gus")
        gate_params_stage(nc, gs, us, ms)
        silu_top_stage(nc, gu, ms, silu_top, NBLK)
        scale_stage(nc, [(silu_top[:, :], hs)], "hs")
        silu_params_stage(nc, hs, us, ms)
        product_stage(nc, gu, prod, xs, ms, prod_top, NBLK)
        scale_stage(nc, [(prod_top[:, :], ps)], "ps")
        with ExitStack() as c2:
            wd_hi, wd_lo = (c2.enter_context(nc.sbuf_tensor("ffn_" + n, [P, J, D], F32R)) for n in ("wd_hi", "wd_lo"))
            ffn_weights_stage(nc, ident, [(w_down, wd_hi, wd_lo)], "wd")
            down_params_stage(nc, ps, ms)
            down_stage(nc, prod, x2, out, wd_hi, wd_lo, ms, NBLK)




def gate_params_stage(nc, gs, us, ms):
    with ExitStack() as ctx:
        block = ctx.enter_context(nc.Block())

        @block.vector
        def _(dve):
            nc.vector.tensor_copy(ms[:, 0:1], gs[:, 2:3])
            nc.vector.tensor_copy(ms[:, 1:2], gs[:, 1:2])
            nc.vector.tensor_copy(ms[:, 3:4], us[:, 2:3])


def silu_top_stage(nc, gu, ms, silu_top, NBLK):
    J = HID // P
    NG = J // 4
    F = 4 * TB
    with ExitStack() as ctx:
        def sb(name, dt=F32):
            return ctx.enter_context(nc.sbuf_tensor("st_" + name, [P, NG, F], dt))

        def sem(name):
            return nc.alloc_semaphore("st_" + name)

        g_in, sig = sb("g_in"), sb("sig")
        g_int, s_int = sb("g_int", I16), sb("s_int", U16)
        loaded = [sem(f"loaded{s}") for s in range(NG)]
        g_rounded, sig_done, s_rounded, silu_done, topped = sem("g_rounded"), sem("sig_done"), sem("s_rounded"), sem("silu_done"), sem("topped")
        block = ctx.enter_context(nc.Block())

        @block.sync
        def _(sp):
            def load(b, s):
                sp.dma_start(g_in[:, s, :], gu[bass.ds(b, 1), :, 4 * s:4 * s + 4, :].rearrange("b p j t -> p (b j t)")).then_inc(loaded[s], 16)

            for s in range(NG):
                load(0, s)
            with sp.Fori(0, NBLK - 1) as b:
                for s in range(NG):
                    sp.wait_ge(g_rounded, b * NG + s + 1)
                    load(b + 1, s)

        @block.scalar
        def _(act):
            with act.Fori(0, NBLK) as b:
                for s in range(NG):
                    act.wait_ge(loaded[s], b * 16 + 16)
                    act.wait_ge(topped, b * NG + s + 1)
                    nc.scalar.activation(g_int[:, s, :], g_in[:, s, :], ACT.Copy, scale=ms[:, 0:1]).then_inc(g_rounded, 1)
                    act.wait_ge(g_rounded, b * NG + s + 1)
                    nc.scalar.activation(sig[:, s, :], g_int[:, s, :], ACT.Sigmoid, scale=ms[:, 1:2]).then_inc(sig_done, 1)

        @block.vector
        def _(dve):
            dve.sem_inc(topped, NG)
            with dve.Fori(0, NBLK) as b:
                for s in range(NG):
                    dve.wait_ge(sig_done, b * NG + s + 1)
                    nc.vector.tensor_scalar(s_int[:, s, :], sig[:, s, :], SIG_ONE, SIG_ONE - 1.0, ALU.mult, ALU.min).then_inc(s_rounded, 1)
                    dve.wait_ge(s_rounded, b * NG + s + 1)
                    nc.vector.scalar_tensor_tensor(sig[:, s, :], g_int[:, s, :], ms[:, 1:2], s_int[:, s, :], ALU.mult, ALU.mult).then_inc(silu_done, 1)
                    dve.wait_ge(silu_done, b * NG + s + 1)
                    nc.vector.tensor_reduce(silu_top[:, bass.ds(b * NG + s, 1)], sig[:, s, :], AX, ALU.max,
                                            apply_absolute_value=True).then_inc(topped, 1)


def silu_params_stage(nc, hs, us, ms):
    with ExitStack() as ctx:
        step = nc.alloc_semaphore("sp_step")
        block = ctx.enter_context(nc.Block())

        @block.vector
        def _(dve):
            nc.vector.tensor_scalar(ms[:, 6:7], hs[:, 0:1], 1.0 / SIG_ONE / QMAX, 1e-12, ALU.mult, ALU.max).then_inc(step, 1)
            dve.wait_ge(step, 1)
            nc.vector.reciprocal(ms[:, 2:3], ms[:, 6:7]).then_inc(step, 1)
            dve.wait_ge(step, 2)
            nc.vector.tensor_scalar(ms[:, 2:3], ms[:, 2:3], 1.0 / SIG_ONE, None, ALU.mult).then_inc(step, 1)
            nc.vector.tensor_tensor(ms[:, 7:8], ms[:, 6:7], us[:, 1:2], ALU.mult).then_inc(step, 1)
            dve.wait_ge(step, 4)


def down_params_stage(nc, ps, ms):
    with ExitStack() as ctx:
        step = nc.alloc_semaphore("dp_step")
        block = ctx.enter_context(nc.Block())

        @block.vector
        def _(dve):
            nc.vector.tensor_tensor(ms[:, 5:6], ps[:, 0:1], ms[:, 7:8], ALU.mult).then_inc(step, 1)
            dve.wait_ge(step, 1)
            nc.vector.tensor_scalar(ms[:, 5:6], ms[:, 5:6], 1.0 / QMAX, 1e-12, ALU.mult, ALU.max).then_inc(step, 1)
            dve.wait_ge(step, 2)
            nc.vector.reciprocal(ms[:, 4:5], ms[:, 5:6]).then_inc(step, 1)
            dve.wait_ge(step, 3)
            nc.vector.tensor_tensor(ms[:, 4:5], ms[:, 4:5], ms[:, 7:8], ALU.mult).then_inc(step, 1)
            dve.wait_ge(step, 4)


def identity_stage(nc, tiles):
    with ExitStack() as ctx:
        zeroed, filled = nc.alloc_semaphore("id_zeroed"), nc.alloc_semaphore("id_filled")
        block = ctx.enter_context(nc.Block())

        @block.gpsimd
        def _(pool):
            for n, tile in enumerate(tiles):
                nc.gpsimd.memset(tile[:, :], 0.0).then_inc(zeroed, 1)
                pool.wait_ge(zeroed, n + 1)
                nc.gpsimd.affine_select(out=tile[:, :], in_=tile[:, :], compare_op=ALU.not_equal, fill=1.0, base=0,
                                        pattern=[[-1, P]], channel_multiplier=1).then_inc(filled, 1)
            pool.wait_ge(filled, len(tiles))


def bass_infini_decoder(nc, x, x_t, ctx_t, mask, aq, ak, av, ao, beta, xq, bq, xk, bk, xv, bv, xo, bo, w_gate, w_up, w_down, out):
    NB = x.shape[0] // TB
    scratch = {name: nc.dram_tensor(name, shape, F32, kind="Internal").ap() for name, shape in
               (("x1", list(x.shape)), ("x2", list(x.shape)), ("gate_up", [NB, P, 2 * HID // P, TB]), ("product", [NB, P, HID // P, TB]))}

    def tokens(a):
        return a.rearrange("(b t p) d -> b p t d", t=TB // P, p=P)

    def rows(a):
        return a.rearrange("(k p) n -> p k n", p=P)

    with ExitStack() as ctx:
        ident = ctx.enter_context(nc.sbuf_tensor("ident", [P, P], F32))
        identb = ctx.enter_context(nc.sbuf_tensor("identb", [P, P], BF16))
        x_top = ctx.enter_context(nc.sbuf_tensor("x2_top", [P, NB * TB // P], F32))
        identity_stage(nc, (ident, identb))
        with nc.cleanup_on_exit():
            self_phase(nc, ident, identb, tokens(x), x_t, tokens(scratch["x1"]), [rows(w) for w in (aq, ak, av, ao)],
                       beta.broadcast_to([P, beta.shape[1]]), NB)
        with nc.cleanup_on_exit():
            cross_phase(nc, ident, identb, tokens(scratch["x1"]), tokens(scratch["x2"]), ctx_t, mask, [rows(w) for w in (xq, xk, xv, xo)],
                        bq, bk, bv.broadcast_to([P, D]), bo.broadcast_to([P, D]), x_top, NB)
        with nc.cleanup_on_exit():
            ffn_phase(nc, ident, tokens(scratch["x2"]), scratch["gate_up"], scratch["product"], tokens(out),
                      *(w.rearrange("(r p) c -> r p c", p=P) for w in (w_gate, w_up, w_down)), x_top, NB)


def kernel(**inputs):
    import numpy as _np
    import concourse.bacc as _bacc
    from concourse import mybir as _mybir
    from concourse.bass_utils import run_bass_kernel_spmd as _run

    given = {name: _np.asarray(a) for name, a in inputs.items()}
    x = given["x"]
    B, T, width = x.shape
    K, SEG = width // 128, 64
    ctx = given["ctx_1024"]
    C = ctx.shape[1]

    def columns(bias):
        return bias.reshape(K, 128).T

    layouts = {
        "x": x.reshape(B * T, width),
        "x_t": x.reshape(B, T // 128, 2, SEG, width)[:, :, ::-1].reshape(B, T, K, 128).transpose(0, 2, 3, 1),
        "ctx_t": ctx.transpose(0, 2, 1).reshape(B, K, 128, C),
        "mask": given["mask_BxSxS2_bk0"].reshape(B, T // 128, 128, C),
        "aq": given["L0_attn_W_q"].T,
        "ak": given["L0_attn_W_k"].T,
        "av": given["L0_attn_W_v"].T,
        "ao": given["L0_attn_W_o"].T,
        "beta": given["L0_attn_beta_param"][None],
        "xq": given["L0_xattn_Wq"],
        "bq": columns(given["L0_xattn_bq"]),
        "xk": given["L0_xattn_Wk"],
        "bk": columns(given["L0_xattn_bk"]),
        "xv": given["L0_xattn_Wv"],
        "bv": given["L0_xattn_bv"][None],
        "xo": given["L0_xattn_Wo"],
        "bo": given["L0_xattn_bo"][None],
        "w_gate": given["L0_ffn_w_gate"],
        "w_up": given["L0_ffn_w_up"],
        "w_down": given["L0_ffn_w_down"],
    }
    nc = _bacc.Bacc("TRN2", target_bir_lowering=False, num_devices=1)
    arrays, args = {}, []
    for name, a in layouts.items():
        a = _np.ascontiguousarray(a)
        arrays["in_" + name] = a
        args.append(nc.dram_tensor("in_" + name, a.shape, _mybir.dt.from_np(a.dtype), kind="ExternalInput").ap())
    args.append(nc.dram_tensor("out_x", (B * T, width), _mybir.dt.float32, kind="ExternalOutput").ap())
    bass_infini_decoder(nc, *args)
    r = _run(nc, [arrays], core_ids=[0])
    return r.results[0]["out_x"].reshape(B, T, width)
```

```python
from contextlib import ExitStack

import concourse.bass as bass
from concourse import mybir

F32 = mybir.dt.float32
F32R = mybir.dt.float32r
BF16 = mybir.dt.bfloat16
I16 = mybir.dt.int16
U16 = mybir.dt.uint16
U8 = mybir.dt.uint8
I32 = mybir.dt.int32
ALU = mybir.AluOpType
ACT = mybir.ActivationFunctionType
AX = mybir.AxisListType.X
RMAX = bass.bass_isa.ReduceOp.max

P = 128
D = 512
HID = 1536
TB = 512
QBLOCK = 32
QMAX = 32767.0
WQMAX = 7.0
SIG_ONE = 65536.0
SILU_NEG = 0.29
LN_EPS = 1e-5
CTX = 77
MEM_EPS = 1e-6
POOL_CONSTS = 9
DVE_CONSTS = 9


def wait(eng, sem, value):
    if not isinstance(value, int) or value > 0:
        eng.wait_ge(sem, value)


def batches(eng, NB, emit):
    emit(0, 0, True, False)
    if NB > 2:
        with eng.Fori(0, (NB - 2) // 2) as i:
            emit(i * 2 + 1, 1, False, False)
            emit(i * 2 + 2, 0, False, False)
    emit(NB - 1, 1, False, True)


def split_weights_stage(nc, jobs, tag, prefetch):
    with ExitStack() as ctx:
        def sem(name):
            return nc.alloc_semaphore(f"{tag}_{name}")

        raw = ctx.enter_context(nc.sbuf_tensor(f"{tag}_raw", [P, 2, D // P, D], F32))
        loaded = [sem("loaded0"), sem("loaded1")]
        hi_done, lo_done = sem("hi_done"), sem("lo_done")
        block = ctx.enter_context(nc.Block())

        @block.sync
        def _(sp):
            for n, (src, hi, lo) in enumerate(jobs):
                if n >= 2:
                    sp.wait_ge(lo_done, n - 1)
                sp.dma_start(raw[:, n % 2, :, :], src).then_inc(loaded[n % 2], 16)
                if n == 1:
                    prefetch(sp)

        @block.scalar
        def _(act):
            for n, (src, hi, lo) in enumerate(jobs):
                act.wait_ge(loaded[n % 2], 16 * (n // 2 + 1))
                nc.scalar.activation(hi[:, :, :], raw[:, n % 2, :, :], ACT.Copy).then_inc(hi_done, 1)

        @block.vector
        def _(dve):
            for n, (src, hi, lo) in enumerate(jobs):
                dve.wait_ge(hi_done, n + 1)
                nc.vector.tensor_tensor(lo[:, :, :], raw[:, n % 2, :, :], hi[:, :, :], ALU.subtract).then_inc(lo_done, 1)




def self_phase(nc, ident, identb, x, x_t, x1, w, beta, NB):
    K = D // P
    H = 16
    HW = D // H
    HG = P // HW
    S = P // 2
    MW = HW + 1
    SCALE = HW ** -0.5
    with ExitStack() as ctx:
        def sb(name, shape, dt=F32):
            return ctx.enter_context(nc.sbuf_tensor("a_" + name, shape, dt))

        def ps(name, shape):
            return ctx.enter_context(nc.psum_tensor("a_" + name, shape, F32))

        def sem(name):
            return nc.alloc_semaphore("a_" + name)

        wq, wk, wv, wo = ((sb(f"w{n}_hi", [P, K, D], F32R), sb(f"w{n}_lo", [P, K, D], F32R)) for n in "qkvo")
        x_in = sb("x_in", [P, K, TB])
        x_loaded = sem("x_loaded")

        def fetch_x(sp, c):
            sp.dma_start(x_in[:, :, :], x_t[bass.ds(c, 1), :, :, :].rearrange("b k p t -> p (b k) t")).then_inc(x_loaded, 16)

        split_weights_stage(nc, [(src, hi, lo) for src, (hi, lo) in zip(w, (wq, wk, wv, wo))], "aw", lambda sp: fetch_x(sp, 0))
        xt_hi, xt_lo = sb("xt_hi", [P, K, TB], F32R), sb("xt_lo", [P, K, TB], F32R)
        q_t = [sb(f"q_t{u}", [P, K, TB]) for u in range(2)]
        k_t = [sb(f"k_t{u}", [P, K, TB]) for u in range(2)]
        v_n = [sb(f"v_n{u}", [P, 4, H, MW]) for u in range(2)]
        q_pad = sb("q_pad", [P, K, 4 * S])
        k_diag = sb("k_diag", [P, K, 2, HG * S])
        feat = sb("feat", [P, 2, K, 4 * S])
        f_exp = sb("f_exp", [P, 2, K, 2 * S])
        sk_n = sb("sk_n", [P, D])
        state = sb("state", [P, K, HG * MW])
        m_rec = sb("m_rec", [P, 2, H])
        m_out = sb("m_out", [P, 2, H, HW])
        delta = sb("delta", [P, H, MW])
        gain = sb("gain", [P, 2, H])
        beta_b, one_m = sb("beta_b", [P, H]), sb("one_m", [P, H])
        tri = sb("tri", [P, P], BF16)
        causal = sb("causal", [P, S], BF16)
        top, a_rec = sb("top", [P, H]), sb("a_rec", [P, H])
        e_in = sb("e_in", [P, H, S])
        probs = sb("probs", [P, H, P])
        p_t = sb("p_t", [P, H, P])
        att = sb("att", [P, 2, D])
        o_hi, o_lo = sb("o_hi", [P, K, P], F32R), sb("o_lo", [P, K, P], F32R)
        y = sb("y", [P, 2, D])
        st, mv, var = sb("st", [P, 2, 6]), sb("mv", [P, 2, 2]), sb("var", [P, 2, 1])
        rstd, half = sb("rstd", [P, 2, 1]), sb("half", [P, 1])
        wide = ps("wide", [P, 2, 512])
        score = ps("score", [P, 2, 512])
        turn = ps("turn", [P, 2, 512])
        mem = ps("mem", [P, 2, 512])

        names = """beta_loaded pool_consts beta_exp consts_done x_hi_done x_lo_done proj_mm proj_out padded f_exped f_floored feat_done
                   scored topped shifted exped p_turned p_moved mixed a_recd a_scaled a_done a_added
                   sk_turned sk_moved mem_read eps_added m_recd m_gained m_done delta_done mem_written m_updated m_reset
                   o_turned o_hi_done o_lo_done y_mm y_done stats aggr var_done powed normed stats_seen update_seen""".split()
        s = {n: sem(n) for n in names}
        r_loaded = [sem(f"r_loaded{u}") for u in range(2)]
        stored = [sem(f"stored{u}") for u in range(2)]
        N = 4 * NB
        ITEMS = [(kind, f) for f in range(2) for kind in "qk"] + [(kind, f) for f in (2, 3) for kind in "qk"] + [("v", t) for t in range(4)]
        NI = len(ITEMS)
        PLACES = [(None, None, 0, 1), (2, 3, 4, None), (5, 6, 7, None), (8, 9, 10, 11)]
        ITEM_BANK = [0, 1, 1, 0, 1, 1, 0, 1, 1, 0, 1, 0]
        Y_BANK = [0, 0, 0, 1]
        ITEM_OUTS = [0, None, 2, None, 3, 5, None, 6, 8, None, 9, 10]
        ITEM_YS = {1: -5, 3: -4, 6: -3, 9: -2}
        FIRST_OUTS = [0, 0, 2, 1, 3, 5, 4, 6, 8, 7, 9, 10]
        Y_OUTS = [1, 4, 7, 11]
        block = ctx.enter_context(nc.Block())

        @block.sync
        def _(sp):
            sp.dma_start(beta_b[:, :], beta).then_inc(s["beta_loaded"], 16)

            def load_x(c):
                wait(sp, s["x_lo_done"], c * 4)
                fetch_x(sp, c)

            def load_residual(n, b, t):
                wait(sp, stored[t % 2], b * 32 + 16 * (t // 2))
                sp.dma_start(y[:, t % 2, :], x[bass.ds(b, 1), :, t, :].rearrange("b p d -> p (b d)")).then_inc(r_loaded[t % 2], 16)

            def store(n, b, t):
                sp.wait_ge(s["normed"], n + 1)
                sp.dma_start(x1[bass.ds(b, 1), :, t, :].rearrange("b p d -> p (b d)"), y[:, t % 2, :]).then_inc(stored[t % 2], 16)

            def emit(b, u, first, last):
                for t in range(4):
                    if t == 0 and not last:
                        load_x(b + 1)
                    if t >= 2:
                        store(b * 4 + t - 2, b, t - 2)
                    elif not first:
                        store(b * 4 + t - 2, b - 1, t + 2)
                    load_residual(b * 4 + t, b, t)

            batches(sp, NB, emit)
            store(N - 2, NB - 1, 2)
            store(N - 1, NB - 1, 3)
            for u in range(2):
                sp.wait_ge(stored[u], 16 * 2 * NB)

        @block.tensor
        def _(pe):
            def project(c, i, steady):
                kind, f = ITEMS[i]
                if i == 0:
                    pe.wait_ge(s["x_lo_done"], c * 4 + 4)
                if not steady:
                    wait(pe, s["proj_out"], FIRST_OUTS[i])
                elif ITEM_OUTS[i] is None:
                    wait(pe, s["y_done"], c * 4 + ITEM_YS[i])
                else:
                    pe.wait_ge(s["proj_out"], c * NI + ITEM_OUTS[i])
                out = wide[:, ITEM_BANK[i], :]
                for k in range(K):
                    if kind == "v":
                        cols = slice(f * P, (f + 1) * P)
                        parts = ((xt_hi[:, k, cols], wv[0][:, k, :]), (xt_lo[:, k, cols], wv[0][:, k, :]), (xt_hi[:, k, cols], wv[1][:, k, :]))
                    else:
                        hi, lo = wq if kind == "q" else wk
                        cols = slice(f * P, (f + 1) * P)
                        parts = ((hi[:, k, cols], xt_hi[:, k, :]), (hi[:, k, cols], xt_lo[:, k, :]), (lo[:, k, cols], xt_hi[:, k, :]))
                    for m, (a, r) in enumerate(parts):
                        mm = nc.tensor.matmul(out, a, r, start=(k == 0 and m == 0), stop=(k == K - 1 and m == 2))
                mm.then_inc(s["proj_mm"], 1)

            def read_memory(n, g, c, t):
                if g == 0:
                    pe.wait_ge(s["feat_done"], n * 2 + 2)
                    if t == 0:
                        pe.wait_ge(s["m_reset"], c + 1)
                wait(pe, s["m_updated"], n * 2 + g)
                cols = slice(2 * S, 4 * S) if g == 0 else slice(0, 2 * S)
                for f in range(K):
                    mm = nc.tensor.matmul(mem[:, f // 2, (f % 2) * HG * MW:(f % 2 + 1) * HG * MW], feat[:, t % 2, f, cols],
                                          state[:, f, :], start=(f % 2 == 0), stop=(f % 2 == 1), skip_group_check=True)
                mm.then_inc(s["mem_read"], 1)

            def write_memory(n, g, t):
                pe.wait_ge(s["delta_done"], n * 2 + g + 1)
                if g == 0:
                    pe.wait_ge(s["sk_moved"], n + 1)
                rows = slice(S, P) if g == 0 else slice(0, S)
                for f in range(K):
                    mm = nc.tensor.matmul(mem[:, f // 2, (f % 2) * HG * MW:(f % 2 + 1) * HG * MW], sk_n[rows, f * P:(f + 1) * P],
                                          delta[rows, f * HG:(f + 1) * HG, :].rearrange("p h w -> p (h w)"),
                                          start=(f % 2 == 0), stop=(f % 2 == 1), skip_group_check=True)
                mm.then_inc(s["mem_written"], 1)

            def turn_p(n, g):
                if g == 0:
                    pe.wait_ge(s["exped"], n * 4 + 2)
                    pe.wait_ge(s["sk_moved"], n + 1)
                elif g == 1:
                    wait(pe, s["o_lo_done"], n - 1)
                else:
                    pe.wait_ge(s["p_moved"], n * 4 + g - 1)
                    pe.wait_ge(s["exped"], n * 4 + 4)
                for j in range(4):
                    mm = nc.tensor.transpose(turn[:, g % 2, j * P:(j + 1) * P], probs[:, 4 * g + j, :], ident[:, :])
                mm.then_inc(s["p_turned"], 1)

            def attend(n, c, u, t):
                pe.wait_ge(s["p_moved"], n * 4 + 4)
                pe.wait_ge(s["proj_out"], c * NI + NI)
                for h in range(H):
                    mm = nc.tensor.matmul(score[:, h // 8, (h % 8) * MW:(h % 8 + 1) * MW], p_t[:, h, :], v_n[u][:, t, h, :],
                                          start=(h % 8 == 0), stop=(h % 8 == 7), skip_group_check=True)
                mm.then_inc(s["mixed"], 1)

            def turn_sk(n, r, first):
                pe.wait_ge(s["feat_done"], n * 2 + 2)
                if not first:
                    pe.wait_ge(s["p_moved"], n * 4 - 1)
                for f in range(K):
                    for g in range(2):
                        mm = nc.tensor.matmul(turn[g * S:(g + 1) * S, 0, f * P:(f + 1) * P], feat[:, r, f, 3 * S * g:3 * S * g + S], ident[:, :],
                                              start=True, stop=True, skip_group_check=True)
                mm.then_inc(s["sk_turned"], 1)

            def turn_o(n, r, final):
                pe.wait_ge(s["a_added"], n * 2 + 2)
                pe.wait_ge(s["p_moved"], n * 4 + (4 if final else 8))
                wait(pe, s["o_lo_done"], n)
                for k in range(K):
                    mm = nc.tensor.transpose(turn[:, 1, k * P:(k + 1) * P], att[:, r, k * P:(k + 1) * P], ident[:, :])
                mm.then_inc(s["o_turned"], 1)

            def scores(n, r):
                pe.wait_ge(s["padded"], n + 1)
                wait(pe, s["a_done"], n)
                for g in range(2):
                    nc.tensor.matmul(score[:, g, :], identb[:, :], causal[:, :].unsqueeze(1).broadcast_to([P, 8, S]), start=True, stop=False, skip_group_check=True)
                for f in range(K):
                    for g in range(2):
                        mm = nc.tensor.matmul(score[:, f // 2, (f % 2) * HG * S:(f % 2 + 1) * HG * S], q_pad[:, f, 2 * S * g:2 * S * (g + 1)],
                                              k_diag[:, f, g, :], start=False, stop=(f % 2 == 1 and g == 1), skip_group_check=True)
                mm.then_inc(s["scored"], 1)

            def project_o(n, bank, items):
                pe.wait_ge(s["o_lo_done"], n + 1)
                if items is None:
                    pe.wait_ge(s["y_done"], n)
                else:
                    pe.wait_ge(s["proj_out"], items)
                for k in range(K):
                    for m, (o, a) in enumerate(((o_hi, wo[0]), (o_lo, wo[0]), (o_hi, wo[1]))):
                        mm = nc.tensor.matmul(wide[:, bank, :], o[:, k, :], a[:, k, :], start=(k == 0 and m == 0), stop=(k == K - 1 and m == 2))
                mm.then_inc(s["y_mm"], 1)

            for i in range(NI):
                project(0, i, False)
            pe.wait_ge(s["pool_consts"], POOL_CONSTS)
            pe.wait_ge(s["consts_done"], DVE_CONSTS)
            turn_sk(0, 0, True)
            scores(0, 0)

            def emit(b, u, first, last):
                for t in range(4):
                    n = b * 4 + t
                    r = t % 2

                    def item(place):
                        if not last and PLACES[t][place] is not None:
                            project(b + 1, PLACES[t][place], True)

                    read_memory(n, 0, b, t)
                    turn_p(n, 0)
                    turn_p(n, 1)
                    item(0)
                    write_memory(n, 0, t)
                    turn_p(n, 2)
                    turn_p(n, 3)
                    item(1)
                    read_memory(n, 1, b, t)
                    attend(n, b, u, t)
                    item(2)
                    write_memory(n, 1, t)
                    if not (last and t == 3):
                        turn_sk(n + 1, 1 - r, False)
                    if not (first and t == 0):
                        turn_o(n - 1, 1 - r, False)
                    if not (last and t == 3):
                        scores(n + 1, 1 - r)
                    item(3)
                    if not (first and t == 0):
                        project_o(n - 1, Y_BANK[t], None if last else (b + 1) * NI + Y_OUTS[t])

            batches(pe, NB, emit)
            turn_o(N - 1, 1, True)
            project_o(N - 1, 0, None)

        @block.scalar
        def _(act):
            act.wait_ge(s["beta_loaded"], 16)
            nc.scalar.activation(beta_b[:, :], beta_b[:, :], ACT.Exp, scale=-1.0).then_inc(s["beta_exp"], 1)

            def x_high(c):
                act.wait_ge(x_loaded, c * 16 + 16)
                wait(act, s["proj_mm"], c * NI)
                for k in range(K):
                    nc.scalar.activation(xt_hi[:, k, :], x_in[:, k, :], ACT.Copy).then_inc(s["x_hi_done"], 1)

            def item_out(c, u, i):
                kind, f = ITEMS[i]
                act.wait_ge(s["proj_mm"], c * NI + i + 1)
                src = wide[:, ITEM_BANK[i], :]
                if kind == "v":
                    ins = nc.scalar.activation(v_n[u][:, f, :, 0:HW], src.rearrange("p (h w) -> p h w", h=H), ACT.Copy)
                else:
                    ins = nc.scalar.activation((q_t if kind == "q" else k_t)[u][:, f, :], src, ACT.Copy)
                ins.then_inc(s["proj_out"], 1)

            def feat_exp(n, c, u, t):
                if t == 0:
                    act.wait_ge(s["proj_out"], c * NI + 8)
                for j, src in enumerate((q_t[u], k_t[u])):
                    wait(act, s["feat_done"], n * 2 - 1 + j)
                    nc.scalar.activation(f_exp[:, j, :, :], src[:, :, t * P:(t + 1) * P], ACT.Exp).then_inc(s["f_exped"], 1)

            def exp(n):
                for g in range(2):
                    act.wait_ge(s["shifted"], n * 2 + g + 1)
                    wait(act, s["p_turned"], n * 4 - 2 + 2 * g)
                    for rows, keys in ((slice(0, S), slice(S, P)), (slice(S, P), slice(0, S))):
                        nc.scalar.activation(probs[rows, 8 * g:8 * g + 8, keys], e_in[rows, 8 * g:8 * g + 8, :], ACT.Exp, scale=SCALE).then_inc(s["exped"], 1)

            def p_out(n, g):
                if g == 0:
                    wait(act, s["mixed"], n)
                act.wait_ge(s["p_turned"], n * 4 + g + 1)
                nc.scalar.activation(p_t[:, 4 * g:4 * g + 4, :], turn[:, g % 2, :].rearrange("p (h q) -> p h q", h=4), ACT.Copy).then_inc(s["p_moved"], 1)

            def sk_out(n, r):
                act.wait_ge(s["sk_turned"], n + 1)
                wait(act, s["mem_written"], n * 2)
                nc.scalar.activation(sk_n[:, :], turn[:, 0, :], ACT.Copy).then_inc(s["sk_moved"], 1)

            def o_high(n):
                act.wait_ge(s["o_turned"], n + 1)
                wait(act, s["y_mm"], n)
                nc.scalar.activation(o_hi[:, :, :], turn[:, 1, :].rearrange("p (k m) -> p k m", k=K), ACT.Copy).then_inc(s["o_hi_done"], 1)

            x_high(0)
            act.wait_ge(s["pool_consts"], POOL_CONSTS)
            for i in range(NI):
                item_out(0, 0, i)
            feat_exp(0, 0, 0, 0)
            sk_out(0, 0)
            exp(0)

            def emit(b, u, first, last):
                for t in range(4):
                    n = b * 4 + t
                    r = t % 2

                    def item(place):
                        if not last and PLACES[t][place] is not None:
                            item_out(b + 1, 1 - u, PLACES[t][place])

                    p_out(n, 0)
                    p_out(n, 1)
                    item(0)
                    p_out(n, 2)
                    p_out(n, 3)
                    item(1)
                    if t < 3:
                        feat_exp(n + 1, b, u, t + 1)
                    elif not last:
                        feat_exp(n + 1, b + 1, 1 - u, 0)
                    if t == 0 and not last:
                        x_high(b + 1)
                    item(2)
                    if not (last and t == 3):
                        sk_out(n + 1, 1 - r)
                    if not (first and t == 0):
                        o_high(n - 1)
                    item(3)
                    if not (last and t == 3):
                        exp(n + 1)

            batches(act, NB, emit)
            o_high(N - 1)

        @block.gpsimd
        def _(pool):
            nc.gpsimd.memset(tri[:, :], 0.0).then_inc(s["pool_consts"], 1)
            pool.wait_ge(s["pool_consts"], 1)
            nc.gpsimd.affine_select(out=tri[:, :], in_=tri[:, :], compare_op=ALU.is_ge, fill=-1e30, base=0,
                                    pattern=[[-1, P]], channel_multiplier=1).then_inc(s["pool_consts"], 1)
            for tile in (q_pad, k_diag, probs):
                nc.gpsimd.memset(tile[:], 0.0).then_inc(s["pool_consts"], 1)
            for tile in v_n:
                nc.gpsimd.memset(tile[:, :, :, HW:MW], 1.0).then_inc(s["pool_consts"], 1)
            nc.gpsimd.memset(delta[:, :, HW:MW], 1.0).then_inc(s["pool_consts"], 1)
            nc.gpsimd.memset(half[:, :], -0.5).then_inc(s["pool_consts"], 1)

            def reset(b):
                wait(pool, s["m_updated"], b * 8)
                wait(pool, s["a_added"], b * 8)
                pool.sem_inc(s["update_seen"], 1)
                nc.gpsimd.memset(state[:, :, :], 0.0).then_inc(s["m_reset"], 1)

            def add_memory(n, r):
                for g in range(2):
                    rows = slice(0, S) if g == 0 else slice(S, P)
                    if g == 0:
                        pool.wait_ge(s["a_done"], n + 1)
                        wait(pool, s["powed"], n - 1)
                    else:
                        pool.wait_ge(s["a_added"], n * 2 + 1)
                    pool.wait_ge(s["m_done"], n * 2 + g + 1)
                    nc.gpsimd.tensor_tensor(att[rows, r, :], att[rows, r, :], m_out[rows, g, :, :].rearrange("p h w -> p (h w)"), ALU.add).then_inc(s["a_added"], 1)

            def power(n, r, added, resets):
                pool.wait_ge(s["var_done"], n + 1)
                pool.wait_ge(s["a_added"], added)
                pool.wait_ge(s["m_reset"], resets)
                nc.gpsimd.tensor_tensor(rstd[:, r, :], var[:, r, :], half[:, :], ALU.pow).then_inc(s["powed"], 1)

            def emit(b, u, first, last):
                for t in range(4):
                    n = b * 4 + t
                    if not (first and t < 2):
                        power(n - 2, t % 2, n * 2, b + 1)
                    add_memory(n, t % 2)
                    if t == 3 and not last:
                        reset(b + 1)

            reset(0)
            batches(pool, NB, emit)
            power(N - 2, 0, N * 2, NB)
            power(N - 1, 1, N * 2, NB)

        @block.vector
        def _(dve):
            def x_low(c):
                for k in range(K):
                    dve.wait_ge(s["x_hi_done"], c * 4 + k + 1)
                    nc.vector.tensor_tensor(xt_lo[:, k, :], x_in[:, k, :], xt_hi[:, k, :], ALU.subtract).then_inc(s["x_lo_done"], 1)

            x_low(0)
            dve.wait_ge(s["pool_consts"], POOL_CONSTS)
            dve.wait_ge(s["beta_exp"], 1)
            nc.vector.tensor_scalar(beta_b[:, :], beta_b[:, :], 1.0, None, ALU.add).then_inc(s["consts_done"], 1)
            dve.wait_ge(s["consts_done"], 1)
            nc.vector.reciprocal(beta_b[:, :], beta_b[:, :]).then_inc(s["consts_done"], 1)
            dve.wait_ge(s["consts_done"], 2)
            nc.vector.tensor_scalar(one_m[:, :], beta_b[:, :], -1.0, 1.0, ALU.mult, ALU.add).then_inc(s["consts_done"], 1)
            nc.vector.tensor_copy(gain[0:S, 0, :], beta_b[0:S, :]).then_inc(s["consts_done"], 1)
            nc.vector.tensor_copy(gain[S:P, 1, :], beta_b[S:P, :]).then_inc(s["consts_done"], 1)
            nc.vector.memset(gain[S:P, 0, :], 1.0).then_inc(s["consts_done"], 1)
            nc.vector.memset(gain[0:S, 1, :], 1.0).then_inc(s["consts_done"], 1)
            nc.vector.tensor_copy(causal[0:S, :], tri[0:S, 0:S]).then_inc(s["consts_done"], 1)
            nc.vector.tensor_copy(causal[S:P, :], tri[S:P, S:P]).then_inc(s["consts_done"], 1)
            dve.wait_ge(s["consts_done"], DVE_CONSTS)

            def pad(n, c, u, t, r):
                if t == 0:
                    dve.wait_ge(s["proj_out"], c * NI + 8)
                wait(dve, s["scored"], n)
                cols = slice(t * P, (t + 1) * P)
                nc.vector.tensor_copy(q_pad[:, :, S:3 * S], q_t[u][:, :, cols])
                for h in range(HG):
                    rows = slice(h * HW, (h + 1) * HW)
                    ins = nc.vector.tensor_copy(k_diag[rows, :, :, h * S:(h + 1) * S], k_t[u][rows, :, cols].rearrange("p f (g e) -> p f g e", g=2))
                ins.then_inc(s["padded"], 1)

            def features(n, u, t, r):
                cols = slice(t * P, (t + 1) * P)
                for j, src in enumerate((q_t[u], k_t[u])):
                    dve.wait_ge(s["f_exped"], n * 2 + j + 1)
                    nc.vector.tensor_scalar(f_exp[:, j, :, :], f_exp[:, j, :, :], 1.0, None, ALU.min).then_inc(s["f_floored"], 1)
                for j, src in enumerate((q_t[u], k_t[u])):
                    dve.wait_ge(s["f_floored"], n * 2 + j + 1)
                    if j == 0:
                        nc.vector.scalar_tensor_tensor(feat[:, r, :, S:3 * S], src[:, :, cols], 0.0, f_exp[:, 0, :, :], ALU.max, ALU.add).then_inc(s["feat_done"], 1)
                    else:
                        for g in range(2):
                            ins = nc.vector.scalar_tensor_tensor(feat[:, r, :, 3 * S * g:3 * S * g + S], src[:, :, t * P + g * S:t * P + (g + 1) * S], 0.0,
                                                                 f_exp[:, 1, :, g * S:(g + 1) * S], ALU.max, ALU.add)
                        ins.then_inc(s["feat_done"], 1)

            def shift(n):
                dve.wait_ge(s["scored"], n + 1)
                heads = [score[:, g, :].rearrange("p (h e) -> p h e", e=S) for g in range(2)]
                for g in range(2):
                    nc.vector.tensor_reduce(top[:, 8 * g:8 * g + 8], heads[g], AX, ALU.max).then_inc(s["topped"], 1)
                for g in range(2):
                    wait(dve, s["exped"], n * 4 - 2 + 2 * g)
                    dve.wait_ge(s["topped"], n * 2 + g + 1)
                    nc.vector.tensor_tensor(e_in[:, 8 * g:8 * g + 8, :], heads[g], top[:, 8 * g:8 * g + 8].unsqueeze(2).broadcast_to([P, 8, S]), ALU.subtract).then_inc(s["shifted"], 1)

            mem_h = mem[:, :, 0:8 * MW].rearrange("p b (h w) -> p b h w", w=MW)
            mix_h = score[:, :, 0:8 * MW].rearrange("p b (h w) -> p b h w", w=MW)

            def recall(n, g, u, t):
                i = n * 2 + g
                dve.wait_ge(s["mem_read"], i + 1)
                nc.vector.tensor_scalar(m_rec[:, g, :].rearrange("p (b h) -> p b h", b=2), mem_h[:, :, :, HW], MEM_EPS, None, ALU.add).then_inc(s["eps_added"], 1)
                dve.wait_ge(s["eps_added"], i + 1)
                nc.vector.reciprocal(m_rec[:, g, :], m_rec[:, g, :]).then_inc(s["m_recd"], 1)
                dve.wait_ge(s["m_recd"], i + 1)
                nc.vector.tensor_tensor(m_rec[:, g, :], m_rec[:, g, :], gain[:, g, :], ALU.mult).then_inc(s["m_gained"], 1)
                dve.wait_ge(s["m_gained"], i + 1)
                wait(dve, s["a_added"], i - 1)
                nc.vector.tensor_tensor(m_out[:, g, :, :].rearrange("p (b h) w -> p b h w", b=2), mem_h[:, :, :, 0:HW],
                                        m_rec[:, g, :].rearrange("p (b h) -> p b h", b=2).unsqueeze(3).broadcast_to([P, 2, 8, HW]), ALU.mult).then_inc(s["m_done"], 1)
                dve.wait_ge(s["m_done"], i + 1)
                rows = slice(S, P) if g == 0 else slice(0, S)
                nc.vector.tensor_tensor(delta[rows, :, 0:HW], v_n[u][rows, t, :, 0:HW], m_out[rows, g, :, :], ALU.subtract).then_inc(s["delta_done"], 1)

            def update(n, g):
                dve.wait_ge(s["mem_written"], n * 2 + g + 1)
                for h in range(HG):
                    rows = slice(h * HW, (h + 1) * HW)
                    new = mem[rows, :, 0:8 * MW].rearrange("p b (f w) -> p b f w", f=2)[:, :, :, h * MW:(h + 1) * MW]
                    old = state[rows, :, h * MW:(h + 1) * MW].rearrange("p (b f) w -> p b f w", b=2)
                    ins = nc.vector.tensor_tensor(old, new, old, ALU.add)
                ins.then_inc(s["m_updated"], 1)

            def attended(n, r):
                dve.wait_ge(s["mixed"], n + 1)
                nc.vector.reciprocal(a_rec[:, :].rearrange("p (b h) -> p b h", b=2), mix_h[:, :, :, HW]).then_inc(s["a_recd"], 1)
                dve.wait_ge(s["a_recd"], n + 1)
                nc.vector.tensor_tensor(a_rec[:, :], a_rec[:, :], one_m[:, :], ALU.mult).then_inc(s["a_scaled"], 1)
                dve.wait_ge(s["a_scaled"], n + 1)
                wait(dve, s["o_turned"], n - 1)
                nc.vector.tensor_tensor(att[:, r, :].rearrange("p (b h w) -> p b h w", b=2, h=8), mix_h[:, :, :, 0:HW],
                                        a_rec[:, :].rearrange("p (b h) -> p b h", b=2).unsqueeze(3).broadcast_to([P, 2, 8, HW]), ALU.mult).then_inc(s["a_done"], 1)

            def o_low(n):
                dve.wait_ge(s["o_hi_done"], n + 1)
                nc.vector.tensor_tensor(o_lo[:, :, :], turn[:, 1, :].rearrange("p (k m) -> p k m", k=K), o_hi[:, :, :], ALU.subtract).then_inc(s["o_lo_done"], 1)

            def add(n, r, bank, residuals):
                dve.wait_ge(s["y_mm"], n + 1)
                dve.wait_ge(r_loaded[r], residuals)
                nc.vector.tensor_tensor(y[:, r, :], wide[:, bank, :], y[:, r, :], ALU.add).then_inc(s["y_done"], 1)

            def moments(n, r):
                dve.wait_ge(s["y_done"], n + 1)
                nc.vector.bn_stats(st[:, r, :], y[:, r, :]).then_inc(s["stats"], 1)
                dve.wait_ge(s["stats"], n + 1)
                dve.sem_inc(s["stats_seen"], 1)
                nc.vector.bn_aggr(mv[:, r, :], st[:, r, :]).then_inc(s["aggr"], 1)
                dve.wait_ge(s["aggr"], n + 1)
                wait(dve, s["powed"], n - 1)
                nc.vector.tensor_scalar(var[:, r, :], mv[:, r, 1:2], LN_EPS, None, ALU.add).then_inc(s["var_done"], 1)

            def norm(n, r):
                dve.wait_ge(s["powed"], n + 1)
                nc.vector.tensor_scalar(y[:, r, :], y[:, r, :], mv[:, r, 0:1], rstd[:, r, :], ALU.subtract, ALU.mult).then_inc(s["normed"], 1)

            pad(0, 0, 0, 0, 0)
            features(0, 0, 0, 0)
            shift(0)

            def emit(b, u, first, last):
                for t in range(4):
                    n = b * 4 + t
                    r = t % 2
                    recall(n, 0, u, t)
                    if not (first and t < 2):
                        moments(n - 2, r)
                    update(n, 0)
                    if not (last and t == 3):
                        c, cu, ct = (b, u, t + 1) if t < 3 else (b + 1, 1 - u, 0)
                        pad(n + 1, c, cu, ct, 1 - r)
                        features(n + 1, cu, ct, 1 - r)
                        if t == 0 and not last:
                            x_low(b + 1)
                    recall(n, 1, u, t)
                    if not (first and t < 2):
                        norm(n - 2, r)
                    attended(n, r)
                    update(n, 1)
                    if not (first and t == 0):
                        o_low(n - 1)
                    if not (last and t == 3):
                        shift(n + 1)
                    if not (first and t == 0):
                        add(n - 1, 1 - r, Y_BANK[t], b * 32 + 16 * ((t + 1) // 2))

            batches(dve, NB, emit)
            moments(N - 2, 0)
            o_low(N - 1)
            norm(N - 2, 0)
            add(N - 1, 1, 0, 32 * NB)
            moments(N - 1, 1)
            norm(N - 1, 1)


def cross_phase(nc, ident, identb, x1, x2, ctx_t, mask, w, bq, bk, bv, bo, x_top, NB):
    K = D // P
    XH = 8
    HD = D // XH
    C = CTX
    CP = C + 1
    SCALE = HD ** -0.5
    with ExitStack() as ctx:
        def sb(name, shape, dt=F32):
            return ctx.enter_context(nc.sbuf_tensor("x_" + name, shape, dt))

        def ps(name, shape):
            return ctx.enter_context(nc.psum_tensor("x_" + name, shape, F32))

        def sem(name):
            return nc.alloc_semaphore("x_" + name)

        wq, wk, wv, wo = ((sb(f"w{n}_hi", [P, K, D], F32R), sb(f"w{n}_lo", [P, K, D], F32R)) for n in "qkvo")
        x_in = sb("x_in", [P, 4, D])
        c_in = sb("c_in", [P, K, CP])
        m_in = sb("m_in", [P, 4, C], U8)
        x_loaded, c_loaded, m_loaded = sem("x_loaded"), sem("c_loaded"), sem("m_loaded")

        def fetch_x(sp, b):
            sp.dma_start(x_in[:, :, :], x1[bass.ds(b, 1), :, :, :].rearrange("b p t d -> p (b t) d")).then_inc(x_loaded, 16)

        def fetch_c(sp, b):
            sp.dma_start(c_in[:, :, 0:C], ctx_t[bass.ds(b, 1), :, :, :].rearrange("b k p c -> p (b k) c")).then_inc(c_loaded, 16)

        def fetch_m(sp, b):
            sp.dma_start(m_in[:, :, :], mask[bass.ds(b, 1), :, :, :].rearrange("b t p c -> p (b t) c")).then_inc(m_loaded, 16)

        def prefetch(sp):
            fetch_x(sp, 0)
            fetch_c(sp, 0)
            fetch_m(sp, 0)

        split_weights_stage(nc, [(src, hi, lo) for src, (hi, lo) in zip(w, (wq, wk, wv, wo))], "xw", prefetch)
        x_res = sb("x_res", [P, 2, D])
        xt_hi, xt_lo = sb("xt_hi", [P, K, TB], F32R), sb("xt_lo", [P, K, TB], F32R)
        q_t = [sb(f"q_t{u}", [P, K, TB]) for u in range(2)]
        c_hi, c_lo = sb("c_hi", [P, K, CP], F32R), sb("c_lo", [P, K, CP], F32R)
        k_t = [sb(f"k_t{u}", [P, K, C]) for u in range(2)]
        v_n = [sb(f"v_n{u}", [C, XH, HD]) for u in range(2)]
        m_neg = [sb(f"m_neg{u}", [P, 4, C], BF16) for u in range(2)]
        keep = sb("keep", [P, 2, 4])
        k_n = sb("k_n", [C, D])
        bq_c, bk_c = sb("bq_c", [P, K]), sb("bk_c", [P, K])
        bv_b, bo_b = sb("bv_b", [P, D]), sb("bo_b", [P, D])
        top = sb("top", [P, 2, XH])
        e_in = sb("e_in", [P, XH, C])
        probs = sb("probs", [P, 2, XH, C])
        p_t = [sb(f"p_t{u}", [C, XH, P]) for u in range(2)]
        total, rec = sb("total", [P, 2, XH]), sb("rec", [P, 2, XH])
        o_hi, o_lo = sb("o_hi", [P, K, P], F32R), sb("o_lo", [P, K, P], F32R)
        y = sb("y", [P, 3, D])
        st, mv, var = sb("st", [P, 2, 6]), sb("mv", [P, 2, 2]), sb("var", [P, 2, 1])
        rstd, half = sb("rstd", [P, 2, 1]), sb("half", [P, 1])
        x_out = sb("x_out", [P, 2, D])
        wide = ps("wide", [P, 2, D])
        score = ps("score", [P, 2, 512])
        turn = ps("turn", [P, 2, 512])
        mix = ps("mix", [P, 2, 512])

        names = """consts_loaded pool_consts bias_scaled x_turned xt_hi_done xt_lo_done q_mm q_done c_hi_done c_lo_done
                   k_mm k_moved k_turned k_done v_mm v_done m_done keep_done x_biased scored topped shifted exped summed
                   p_turned p_moved mixed recd kept p_normed o_hi_done o_lo_done y_mm y_done stats aggr
                   var_done powed normed absmaxed stats_seen""".split()
        s = {n: sem(n) for n in names}
        r_loaded = [sem(f"r_loaded{u}") for u in range(2)]
        stored = [sem(f"stored{u}") for u in range(2)]
        N = 4 * NB
        block = ctx.enter_context(nc.Block())

        @block.sync
        def _(sp):
            sp.dma_start(bq_c[:, :], bq).then_inc(s["consts_loaded"], 16)
            sp.dma_start(bk_c[:, :], bk).then_inc(s["consts_loaded"], 16)
            sp.dma_start(bv_b[:, :], bv).then_inc(s["consts_loaded"], 16)
            sp.dma_start(bo_b[:, :], bo).then_inc(s["consts_loaded"], 16)

            def load_x(b):
                wait(sp, s["x_turned"], b * 4)
                fetch_x(sp, b)

            def load_residual(n, b, t):
                wait(sp, s["y_done"], n - 1)
                sp.dma_start(x_res[:, t % 2, :], x1[bass.ds(b, 1), :, t, :].rearrange("b p d -> p (b d)")).then_inc(r_loaded[t % 2], 16)

            def load_c(b):
                wait(sp, s["c_lo_done"], b)
                fetch_c(sp, b)
                wait(sp, s["m_done"], b)
                wait(sp, s["keep_done"], b)
                fetch_m(sp, b)

            def store(n, b, t):
                sp.wait_ge(s["normed"], n + 1)
                sp.dma_start(x2[bass.ds(b, 1), :, t, :].rearrange("b p d -> p (b d)"), x_out[:, t % 2, :]).then_inc(stored[t % 2], 16)

            def emit(b, u, first, last):
                for t in range(4):
                    if t == 0 and not last:
                        load_x(b + 1)
                        load_c(b + 1)
                    load_residual(b * 4 + t, b, t)
                    if t >= 2:
                        store(b * 4 + t - 2, b, t - 2)
                    elif not first:
                        store(b * 4 + t - 2, b - 1, t + 2)

            batches(sp, NB, emit)
            store(N - 2, NB - 1, 2)
            store(N - 1, NB - 1, 3)
            for u in range(2):
                sp.wait_ge(stored[u], 16 * 2 * NB)

        @block.tensor
        def _(pe):
            def turn_x(c, k):
                if k == 0:
                    pe.wait_ge(x_loaded, c * 16 + 16)
                    wait(pe, s["v_done"], c)
                elif k == 1:
                    wait(pe, s["q_done"], c * 4)
                else:
                    pe.wait_ge(s["xt_lo_done"], c * 4 + k - 1)
                for t in range(4):
                    mm = nc.tensor.transpose(wide[:, k % 2, t * P:(t + 1) * P], x_in[:, t, k * P:(k + 1) * P], ident[:, :])
                mm.then_inc(s["x_turned"], 1)

            def project_q(c, f):
                if f == 0:
                    pe.wait_ge(s["xt_lo_done"], c * 4 + 4)
                elif f == 3:
                    pe.wait_ge(s["k_done"], c + 1)
                else:
                    pe.wait_ge(s["q_done"], c * 4 + f)
                for k in range(K):
                    for n, (a, x) in enumerate(((wq[0], xt_hi), (wq[0], xt_lo), (wq[1], xt_hi))):
                        mm = nc.tensor.matmul(wide[:, f // 3, :], a[:, k, f * P:(f + 1) * P], x[:, k, :],
                                              start=(k == 0 and n == 0), stop=(k == K - 1 and n == 2))
                mm.then_inc(s["q_mm"], 1)

            def project_c(c, bank, weights, done):
                for k in range(K):
                    for n, (x, a) in enumerate(((c_hi, weights[0]), (c_lo, weights[0]), (c_hi, weights[1]))):
                        mm = nc.tensor.matmul(wide[0:C, bank, :], x[:, k, 0:C], a[:, k, :],
                                              start=(k == 0 and n == 0), stop=(k == K - 1 and n == 2))
                mm.then_inc(done, 1)

            def project_k(c):
                pe.wait_ge(s["c_lo_done"], c + 1)
                project_c(c, 1, wk, s["k_mm"])

            def turn_k(c):
                pe.wait_ge(s["k_moved"], c + 1)
                for f in range(K):
                    mm = nc.tensor.transpose(wide[:, 1, f * C:(f + 1) * C], k_n[:, f * P:(f + 1) * P], ident[0:C, 0:C])
                mm.then_inc(s["k_turned"], 1)

            def project_v(c):
                pe.wait_ge(s["q_done"], c * 4 + 3)
                project_c(c, 0, wv, s["v_mm"])

            def prepare(c, t):
                if t == 0:
                    turn_x(c, 2)
                    turn_x(c, 3)
                elif t == 1:
                    project_q(c, 0)
                    project_k(c)
                elif t == 2:
                    project_q(c, 1)
                    turn_k(c)
                    project_q(c, 2)
                    project_q(c, 3)
                else:
                    project_v(c)

            def scores(n, c, u, t):
                if t == 0:
                    pe.wait_ge(s["q_done"], c * 4 + 4)
                    pe.wait_ge(s["k_done"], c + 1)
                    pe.wait_ge(s["m_done"], c + 1)
                wait(pe, s["shifted"], n * 2)
                for g in range(2):
                    nc.tensor.matmul(score[:, g, 0:4 * C], identb[:, :],
                                     m_neg[u][:, t, :].unsqueeze(1).broadcast_to([P, 4, C]), start=True, stop=False, skip_group_check=True)
                for f in range(4):
                    for g in range(2):
                        mm = nc.tensor.matmul(score[:, g, f * C:(f + 1) * C], q_t[u][g * HD:(g + 1) * HD, f, t * P:(t + 1) * P],
                                              k_t[u][g * HD:(g + 1) * HD, f, :], start=False, stop=(f == 3), skip_group_check=True)
                mm.then_inc(s["scored"], 1)

            def turn_p(n, r):
                pe.wait_ge(s["p_normed"], n + 1)
                wait(pe, s["p_moved"], n * 2)
                for g in range(2):
                    for f in range(4):
                        mm = nc.tensor.transpose(turn[0:C, g, f * P:(f + 1) * P], probs[:, r, 2 * f + g, :], ident[:, :])
                    mm.then_inc(s["p_turned"], 1)

            def attend(n, r, c, u):
                pe.wait_ge(s["p_moved"], n * 2 + 2)
                pe.wait_ge(s["v_done"], c + 1)
                wait(pe, s["o_lo_done"], n)
                for f in range(4):
                    for g in range(2):
                        mm = nc.tensor.matmul(mix[g * HD:(g + 1) * HD, 0, f * P:(f + 1) * P], v_n[u][:, 2 * f + g, :], p_t[r][:, 2 * f + g, :],
                                              start=True, stop=True, skip_group_check=True)
                mm.then_inc(s["mixed"], 1)

            def project_o(n):
                pe.wait_ge(s["o_lo_done"], n + 1)
                wait(pe, s["y_done"], n)
                for k in range(K):
                    for m, (o, a) in enumerate(((o_hi, wo[0]), (o_lo, wo[0]), (o_hi, wo[1]))):
                        mm = nc.tensor.matmul(mix[:, 1, :], o[:, k, :], a[:, k, :], start=(k == 0 and m == 0), stop=(k == K - 1 and m == 2))
                mm.then_inc(s["y_mm"], 1)

            pe.wait_ge(s["pool_consts"], 2)
            turn_x(0, 0)
            turn_x(0, 1)
            for t in range(4):
                prepare(0, t)
            scores(0, 0, 0, 0)

            def emit(b, u, first, last):
                for t in range(4):
                    n = b * 4 + t
                    r = t % 2
                    turn_p(n, r)
                    if t < 3:
                        scores(n + 1, b, u, t + 1)
                    elif not last:
                        scores(n + 1, b + 1, 1 - u, 0)
                    attend(n, r, b, u)
                    if t == 0 and not last:
                        turn_x(b + 1, 0)
                        turn_x(b + 1, 1)
                    if not (first and t == 0):
                        project_o(n - 1)
                    if not last:
                        prepare(b + 1, t)

            batches(pe, NB, emit)
            project_o(N - 1)

        @block.scalar
        def _(act):
            def x_high(c, k):
                act.wait_ge(s["x_turned"], c * 4 + k + 1)
                wait(act, s["q_mm"], c * 4)
                nc.scalar.activation(xt_hi[:, k, :], wide[:, k % 2, :], ACT.Copy).then_inc(s["xt_hi_done"], 1)

            def q_out(c, u, f):
                act.wait_ge(s["q_mm"], c * 4 + f + 1)
                nc.scalar.activation(q_t[u][:, f, :], wide[:, f // 3, :], ACT.Identity, bias=bq_c[:, f:f + 1], scale=SCALE).then_inc(s["q_done"], 1)

            def c_high(c):
                act.wait_ge(c_loaded, c * 16 + 16)
                wait(act, s["v_mm"], c)
                nc.scalar.activation(c_hi[:, :, :], c_in[:, :, :], ACT.Copy).then_inc(s["c_hi_done"], 1)

            def exp(n, r):
                act.wait_ge(s["shifted"], n * 2 + 2)
                wait(act, s["p_turned"], n * 2 - 2)
                nc.scalar.activation(probs[:, r, :, :], e_in[:, :, :], ACT.Exp).then_inc(s["exped"], 1)

            def p_out(n, r):
                wait(act, s["mixed"], n - 1)
                for g in range(2):
                    act.wait_ge(s["p_turned"], n * 2 + g + 1)
                    nc.scalar.activation(p_t[r][:, g::2, :], turn[0:C, g, :].rearrange("c (f p) -> c f p", f=4), ACT.Copy).then_inc(s["p_moved"], 1)

            def o_high(n):
                act.wait_ge(s["mixed"], n + 1)
                wait(act, s["y_mm"], n)
                nc.scalar.activation(o_hi[:, :, :], mix[:, 0, :].rearrange("p (k m) -> p k m", k=K), ACT.Copy).then_inc(s["o_hi_done"], 1)

            def k_out(c, u):
                act.wait_ge(s["k_turned"], c + 1)
                for f in range(K):
                    ins = nc.scalar.activation(k_t[u][:, f, :], wide[:, 1, f * C:(f + 1) * C], ACT.Identity, bias=bk_c[:, f:f + 1])
                ins.then_inc(s["k_done"], 1)

            def k_move(c):
                act.wait_ge(s["k_mm"], c + 1)
                nc.scalar.activation(k_n[:, :], wide[0:C, 1, :], ACT.Copy).then_inc(s["k_moved"], 1)

            def prepare(c, u, t):
                if t == 0:
                    x_high(c, 2)
                    x_high(c, 3)
                    c_high(c)
                elif t == 1:
                    q_out(c, u, 0)
                    k_move(c)
                elif t == 2:
                    q_out(c, u, 1)
                    k_out(c, u)
                    q_out(c, u, 2)
                    q_out(c, u, 3)

            x_high(0, 0)
            x_high(0, 1)
            prepare(0, 0, 0)
            act.wait_ge(s["bias_scaled"], 1)
            prepare(0, 0, 1)
            prepare(0, 0, 2)
            exp(0, 0)

            def emit(b, u, first, last):
                for t in range(4):
                    n = b * 4 + t
                    p_out(n, t % 2)
                    if not (last and t == 3):
                        exp(n + 1, 1 - t % 2)
                    if t == 0 and not last:
                        x_high(b + 1, 0)
                        x_high(b + 1, 1)
                    o_high(n)
                    if not last:
                        prepare(b + 1, 1 - u, t)

            batches(act, NB, emit)

        @block.gpsimd
        def _(pool):
            nc.gpsimd.memset(c_in[:, :, C:CP], 0.0).then_inc(s["pool_consts"], 1)
            nc.gpsimd.memset(half[:, :], -0.5).then_inc(s["pool_consts"], 1)

            def bias_x(b, t):
                pool.wait_ge(r_loaded[t % 2], b * 32 + (t // 2) * 16 + 16)
                nc.gpsimd.tensor_tensor(x_res[:, t % 2, :], x_res[:, t % 2, :], bo_b[:, :], ALU.add).then_inc(s["x_biased"], 1)

            def power(n, r):
                pool.wait_ge(s["var_done"], n + 1)
                nc.gpsimd.tensor_tensor(rstd[:, r, :], var[:, r, :], half[:, :], ALU.pow).then_inc(s["powed"], 1)

            pool.wait_ge(s["consts_loaded"], 64)

            def emit(b, u, first, last):
                for t in range(4):
                    bias_x(b, t)
                    if not (first and t == 0):
                        power(b * 4 + t - 1, 1 - t % 2)

            batches(pool, NB, emit)
            power(N - 1, 1)

        @block.vector
        def _(dve):
            def x_low(c, k):
                dve.wait_ge(s["xt_hi_done"], c * 4 + k + 1)
                nc.vector.tensor_tensor(xt_lo[:, k, :], wide[:, k % 2, :], xt_hi[:, k, :], ALU.subtract).then_inc(s["xt_lo_done"], 1)

            def c_low(c):
                dve.wait_ge(s["c_hi_done"], c + 1)
                nc.vector.tensor_tensor(c_lo[:, :, :], c_in[:, :, :], c_hi[:, :, :], ALU.subtract).then_inc(s["c_lo_done"], 1)

            def v_out(c, u):
                dve.wait_ge(s["v_mm"], c + 1)
                nc.vector.tensor_tensor(v_n[u][:, :, :], wide[0:C, 0, :].rearrange("c (h d) -> c h d", h=XH),
                                        bv_b[0:C, :].rearrange("c (h d) -> c h d", h=XH), ALU.add).then_inc(s["v_done"], 1)

            def mask_out(c, u):
                dve.wait_ge(m_loaded, c * 16 + 16)
                nc.vector.tensor_scalar(m_neg[u][:, :, :], m_in[:, :, :], 1.0, 1e30, ALU.subtract, ALU.mult).then_inc(s["m_done"], 1)
                nc.vector.tensor_reduce(keep[:, u, :], m_in[:, :, :], AX, ALU.max).then_inc(s["keep_done"], 1)

            def shift(n, r):
                dve.wait_ge(s["scored"], n + 1)
                for g in range(2):
                    nc.vector.tensor_reduce(top[:, r, g::2], score[:, g, 0:4 * C].rearrange("p (f c) -> p f c", f=4), AX, ALU.max).then_inc(s["topped"], 1)
                wait(dve, s["exped"], n)
                for g in range(2):
                    dve.wait_ge(s["topped"], n * 2 + g + 1)
                    nc.vector.tensor_tensor(e_in[:, g::2, :], score[:, g, 0:4 * C].rearrange("p (f c) -> p f c", f=4),
                                            top[:, r, g::2].unsqueeze(2).broadcast_to([P, 4, C]), ALU.subtract).then_inc(s["shifted"], 1)

            def normalise(n, r, c, u, t):
                dve.wait_ge(s["exped"], n + 1)
                nc.vector.tensor_reduce(total[:, r, :], probs[:, r, :, :], AX, ALU.add).then_inc(s["summed"], 1)
                dve.wait_ge(s["summed"], n + 1)
                nc.vector.reciprocal(rec[:, r, :], total[:, r, :]).then_inc(s["recd"], 1)
                dve.wait_ge(s["recd"], n + 1)
                dve.wait_ge(s["keep_done"], c + 1)
                nc.vector.tensor_scalar(rec[:, r, :], rec[:, r, :], keep[:, u, t:t + 1], None, ALU.mult).then_inc(s["kept"], 1)
                dve.wait_ge(s["kept"], n + 1)
                nc.vector.tensor_tensor(probs[:, r, :, :], probs[:, r, :, :], rec[:, r, :].unsqueeze(2).broadcast_to([P, XH, C]), ALU.mult).then_inc(s["p_normed"], 1)

            def o_low(n):
                dve.wait_ge(s["o_hi_done"], n + 1)
                nc.vector.tensor_tensor(o_lo[:, :, :], mix[:, 0, :].rearrange("p (k m) -> p k m", k=K), o_hi[:, :, :], ALU.subtract).then_inc(s["o_lo_done"], 1)

            def add(n, r):
                dve.wait_ge(s["y_mm"], n + 1)
                dve.wait_ge(s["x_biased"], n + 1)
                nc.vector.tensor_tensor(y[:, r, :], mix[:, 1, :], x_res[:, r, :], ALU.add).then_inc(s["y_done"], 1)
                dve.wait_ge(s["y_done"], n + 1)
                nc.vector.bn_stats(st[:, r, :], y[:, r, :]).then_inc(s["stats"], 1)
                dve.wait_ge(s["stats"], n + 1)
                dve.sem_inc(s["stats_seen"], 1)
                nc.vector.bn_aggr(mv[:, r, :], st[:, r, :]).then_inc(s["aggr"], 1)
                dve.wait_ge(s["aggr"], n + 1)
                wait(dve, s["powed"], n - 1)
                nc.vector.tensor_scalar(var[:, r, :], mv[:, r, 1:2], LN_EPS, None, ALU.add).then_inc(s["var_done"], 1)

            def norm(n, r, slot_uses):
                dve.wait_ge(s["powed"], n + 1)
                wait(dve, s["absmaxed"], n - 1)
                wait(dve, stored[r], slot_uses)
                nc.vector.tensor_scalar(x_out[:, r, :], y[:, r, :], mv[:, r, 0:1], rstd[:, r, :], ALU.subtract, ALU.mult).then_inc(s["normed"], 1)
                dve.wait_ge(s["normed"], n + 1)
                nc.vector.tensor_reduce(x_top[:, bass.ds(n, 1)], x_out[:, r, :], AX, ALU.max, apply_absolute_value=True).then_inc(s["absmaxed"], 1)

            for k in range(K):
                x_low(0, k)
            c_low(0)
            dve.wait_ge(s["consts_loaded"], 64)
            nc.vector.tensor_scalar(bq_c[:, :], bq_c[:, :], SCALE, None, ALU.mult).then_inc(s["bias_scaled"], 1)
            mask_out(0, 0)
            v_out(0, 0)
            shift(0, 0)
            normalise(0, 0, 0, 0, 0)

            def emit(b, u, first, last):
                for t in range(4):
                    n = b * 4 + t
                    r = t % 2
                    if not (last and t == 3):
                        shift(n + 1, 1 - r)
                    if not (first and t < 2):
                        norm(n - 2, r, b * 32 - 16 if t < 2 else b * 32)
                    if not (last and t == 3):
                        c, cu, ct = (b, u, t + 1) if t < 3 else (b + 1, 1 - u, 0)
                        normalise(n + 1, 1 - r, c, cu, ct)
                    if t == 0 and not last:
                        x_low(b + 1, 0)
                        x_low(b + 1, 1)
                    o_low(n)
                    if not (first and t == 0):
                        add(n - 1, 1 - r)
                    if not last:
                        if t == 0:
                            x_low(b + 1, 2)
                            x_low(b + 1, 3)
                            c_low(b + 1)
                        elif t == 2:
                            mask_out(b + 1, 1 - u)
                        elif t == 3:
                            v_out(b + 1, 1 - u)

            batches(dve, NB, emit)
            norm(N - 2, 0, 32 * NB - 16)
            add(N - 1, 1)
            norm(N - 1, 1, 32 * NB - 16)


def ffn_weights_stage(nc, ident, jobs, tag, prefetch):
    steps = [(src, hi, lo, r, c) for src, hi, lo in jobs
             for r in range(src.shape[0]) for c in range(src.shape[2] // D)]
    G = D // QBLOCK
    with ExitStack() as ctx:
        def sb(name, shape, dt=F32):
            return ctx.enter_context(nc.sbuf_tensor(f"{tag}_{name}", shape, dt))

        def sem(name):
            return nc.alloc_semaphore(f"{tag}_{name}")

        w_in = sb("w_in", [P, 4, D])
        w_int = sb("w_int", [P, 2, D], I16)
        w_deq = sb("w_deq", [P, 2, D])
        w_top = sb("w_top", [P, 2, G])
        w_scale = sb("w_scale", [P, 2, G])
        w_inv = sb("w_inv", [P, 2, G])
        w_psum = ctx.enter_context(nc.psum_tensor(f"{tag}_w_psum", [P, 2, D], F32))
        loaded = [sem(f"w_loaded{i}") for i in range(4)]
        topped, scaled, floored, inverted = sem("w_topped"), sem("w_scaled"), sem("w_floored"), sem("w_inverted")
        rounded, dequant, turned = sem("w_rounded"), sem("w_dequant"), sem("w_turned")
        hi_done, lo_done = sem("w_hi_done"), sem("w_lo_done")
        block = ctx.enter_context(nc.Block())

        @block.sync
        def _(sp):
            for n, (src, hi, lo, r, c) in enumerate(steps):
                if n >= 4:
                    sp.wait_ge(rounded, n - 3)
                sp.dma_start(w_in[:, n % 4, :], src[r, :, c * D:(c + 1) * D]).then_inc(loaded[n % 4], 16)
            prefetch(sp)

        @block.vector
        def _(dve):
            def finish(n):
                src, hi, lo, r, c = steps[n]
                dve.wait_ge(hi_done, n + 1)
                K = D // P
                nc.vector.tensor_tensor(lo[:, c * K:(c + 1) * K, r * P:(r + 1) * P],
                                        w_psum[:, n % 2, :].rearrange("p (k m) -> p k m", k=K),
                                        hi[:, c * K:(c + 1) * K, r * P:(r + 1) * P], ALU.subtract).then_inc(lo_done, 1)

            def grouped(tile):
                return tile.rearrange("p (g e) -> p g e", e=QBLOCK)

            def top(n):
                dve.wait_ge(loaded[n % 4], 16 * (n // 4 + 1))
                nc.vector.tensor_reduce(w_top[:, n % 2, :], grouped(w_in[:, n % 4, :]), AX, ALU.max, apply_absolute_value=True).then_inc(topped, 1)

            def scale(n):
                dve.wait_ge(topped, n + 1)
                if n >= 2:
                    dve.wait_ge(dequant, n - 1)
                nc.vector.tensor_scalar(w_scale[:, n % 2, :], w_top[:, n % 2, :], 1.0 / WQMAX, 1e-12, ALU.mult, ALU.max).then_inc(scaled, 1)

            def invert(n):
                dve.wait_ge(scaled, n + 1)
                nc.vector.reciprocal(w_inv[:, n % 2, :], w_scale[:, n % 2, :]).then_inc(inverted, 1)

            def quantise(n):
                dve.wait_ge(inverted, n + 1)
                nc.vector.tensor_tensor(grouped(w_int[:, n % 2, :]), grouped(w_in[:, n % 4, :]),
                                        w_inv[:, n % 2, :].unsqueeze(2).broadcast_to([P, G, QBLOCK]), ALU.mult).then_inc(rounded, 1)

            def dequantise(n):
                dve.wait_ge(rounded, n + 1)
                if n >= 2:
                    dve.wait_ge(turned, n - 1)
                nc.vector.tensor_tensor(grouped(w_deq[:, n % 2, :]), grouped(w_int[:, n % 2, :]),
                                        w_scale[:, n % 2, :].unsqueeze(2).broadcast_to([P, G, QBLOCK]), ALU.mult).then_inc(dequant, 1)

            top(0)
            scale(0)
            invert(0)
            for n in range(len(steps)):
                more = n + 1 < len(steps)
                if more:
                    top(n + 1)
                quantise(n)
                if more:
                    scale(n + 1)
                dequantise(n)
                if more:
                    invert(n + 1)
                if n >= 1:
                    finish(n - 1)
            finish(len(steps) - 1)

        @block.tensor
        def _(pe):
            for n in range(len(steps)):
                pe.wait_ge(dequant, n + 1)
                if n >= 2:
                    pe.wait_ge(lo_done, n - 1)
                for k in range(D // P):
                    last = nc.tensor.transpose(w_psum[:, n % 2, k * P:(k + 1) * P], w_deq[:, n % 2, k * P:(k + 1) * P], ident[:, :])
                last.then_inc(turned, 1)

        @block.scalar
        def _(act):
            for n, (src, hi, lo, r, c) in enumerate(steps):
                K = D // P
                act.wait_ge(turned, n + 1)
                nc.scalar.activation(hi[:, c * K:(c + 1) * K, r * P:(r + 1) * P],
                                     w_psum[:, n % 2, :].rearrange("p (k m) -> p k m", k=K), ACT.Copy).then_inc(hi_done, 1)


def scale_stage(nc, jobs, tag):
    with ExitStack() as ctx:
        def sem(name):
            return nc.alloc_semaphore(f"{tag}_{name}")

        part = ctx.enter_context(nc.sbuf_tensor(f"{tag}_part", [P, len(jobs)], F32))
        total = ctx.enter_context(nc.sbuf_tensor(f"{tag}_total", [P, len(jobs)], F32))
        reduced, everywhere, step = sem("reduced"), sem("everywhere"), sem("step")
        block = ctx.enter_context(nc.Block())

        @block.vector
        def _(dve):
            for n, (maxima, result) in enumerate(jobs):
                nc.vector.tensor_reduce(part[:, n:n + 1], maxima, AX, ALU.max).then_inc(reduced, 1)
            dve.wait_ge(everywhere, 1)
            count = 0
            for n, (maxima, result) in enumerate(jobs):
                nc.vector.tensor_copy(result[:, 0:1], total[:, n:n + 1]).then_inc(step, 1)
                nc.vector.tensor_scalar(result[:, 1:2], total[:, n:n + 1], 1.0 / QMAX, 1e-12, ALU.mult, ALU.max).then_inc(step, 1)
                count += 2
                dve.wait_ge(step, count)
                nc.vector.reciprocal(result[:, 2:3], result[:, 1:2]).then_inc(step, 1)
                count += 1
            dve.wait_ge(step, count)

        @block.gpsimd
        def _(pool):
            pool.wait_ge(reduced, len(jobs))
            nc.gpsimd.partition_all_reduce(total[:, :], part[:, :], P, RMAX).then_inc(everywhere, 1)


def gate_up_stage(nc, ident, x_in, x_loaded, x2, gu, wg_hi, wg_lo, wu_hi, wu_lo, xs, gu_top, gate_max, NBLK):
    K = D // P
    J = 2 * HID // P
    NG = J // 4
    with ExitStack() as ctx:
        def sb(name, shape, dt=F32):
            return ctx.enter_context(nc.sbuf_tensor("gu_" + name, shape, dt))

        def sem(name):
            return nc.alloc_semaphore("gu_" + name)

        x_int = sb("x_int", [P, 4, D], I16)
        x_q = sb("x_q", [P, 4, D])
        xt_hi = [sb(f"xt_hi{u}", [P, K, TB], F32R) for u in range(2)]
        xt_lo = [sb(f"xt_lo{u}", [P, K, TB], F32R) for u in range(2)]
        stage = sb("stage", [P, 4, 4, TB])
        acc = ctx.enter_context(nc.psum_tensor("gu_acc", [P, 4, TB], F32))
        turn = ctx.enter_context(nc.psum_tensor("gu_turn", [P, 2, TB], F32))
        x_rounded, x_ready = sem("x_rounded"), sem("x_ready")
        turned, hi_done, lo_done = sem("turned"), sem("hi_done"), sem("lo_done")
        products, evacuated, topped = sem("products"), sem("evacuated"), sem("topped")
        stored = [sem(f"stored{s}") for s in range(4)]
        block = ctx.enter_context(nc.Block())
        NPAIR = NBLK // 2

        def pairs(eng, body):
            if NPAIR > 1:
                with eng.Fori(0, NPAIR - 1) as i:
                    for u in range(2):
                        body(i, i * 2 + u, u, False)
            for u in range(2):
                body(NPAIR - 1, (NPAIR - 1) * 2 + u, u, u == 1)

        @block.sync
        def _(sp):
            def load(b):
                sp.dma_start(x_in[:, :, :], x2[bass.ds(b, 1), :, :, :].rearrange("b p t d -> p (b t) d")).then_inc(x_loaded, 16)

            for s in range(4):
                sp.sem_inc(stored[s], 16)

            def body(i, b, u, last):
                if not last:
                    sp.wait_ge(x_rounded, b + 1)
                    load(b + 1)
                for g in range(NG):
                    sp.wait_ge(topped, b * J + 4 * g + 4)
                    s = (u * NG + g) % 4
                    sp.dma_start(gu[bass.ds(b, 1), :, 4 * g:4 * g + 4, :].rearrange("b p j t -> p (b j) t"),
                                 stage[:, s, :, :]).then_inc(stored[s], 16)

            pairs(sp, body)
            for s in range(4):
                sp.wait_ge(stored[s], 16 + 16 * NBLK * NG // 4)

        @block.tensor
        def _(pe):
            def transposes(b, k, first):
                if k == 0:
                    pe.wait_ge(x_ready, b + 1)
                if not first or k >= 2:
                    pe.wait_ge(lo_done, b * K + k - 1)
                for t in range(4):
                    last = nc.tensor.transpose(turn[:, k % 2, t * P:(t + 1) * P], x_q[:, t, k * P:(k + 1) * P], ident[:, :])
                last.then_inc(turned, 1)

            for k in range(K):
                transposes(0, k, True)

            def body(i, b, u, last):
                pe.wait_ge(lo_done, b * K + K)
                pe.wait_ge(hi_done, b * K + K)
                for j in range(J):
                    pe.wait_ge(evacuated, b * J + j + 1)
                    whi, wlo = (wg_hi, wg_lo) if j < J // 2 else (wu_hi, wu_lo)
                    c = j % (J // 2)
                    for k in range(K):
                        for n, (w, x) in enumerate(((whi, xt_hi[u]), (whi, xt_lo[u]), (wlo, xt_hi[u]))):
                            mm = nc.tensor.matmul(acc[:, j % 4, :], w[:, k, c * P:(c + 1) * P], x[:, k, :],
                                                    start=(k == 0 and n == 0), stop=(k == K - 1 and n == 2))
                    mm.then_inc(products, 1)
                    if j in (12, 14, 16, 18) and not last:
                        transposes(b + 1, (j - 12) // 2, False)

            pairs(pe, body)

        @block.scalar
        def _(act):
            def round_x(b):
                act.wait_ge(x_loaded, b * 16 + 16)
                if not isinstance(b, int) or b > 0:
                    act.wait_ge(x_ready, b)
                nc.scalar.activation(x_int[:, :, :], x_in[:, :, :], ACT.Copy, scale=xs[:, 2:3]).then_inc(x_rounded, 1)

            def high(b, k, u):
                act.wait_ge(turned, b * K + k + 1)
                nc.scalar.activation(xt_hi[u][:, k, :], turn[:, k % 2, :], ACT.Copy).then_inc(hi_done, 1)

            act.sem_inc(evacuated, 4)
            round_x(0)
            for k in range(K):
                high(0, k, 0)

            def body(i, b, u, last):
                for j in range(J):
                    if j == 3 and not last:
                        round_x(b + 1)
                    act.wait_ge(products, b * J + j + 1)
                    g = u * NG + j // 4
                    if j % 4 == 0:
                        act.wait_ge(stored[g % 4], (i * (2 * NG // 4) + g // 4) * 16 + 16)
                    nc.scalar.activation(stage[:, g % 4, j % 4, :], acc[:, j % 4, :], ACT.Copy, scale=xs[:, 1:2]).then_inc(evacuated, 1)
                    if j in (13, 15, 17, 19) and not last:
                        high(b + 1, (j - 13) // 2, 1 - u)

            pairs(act, body)

        @block.vector
        def _(dve):
            def float_x(b):
                dve.wait_ge(x_rounded, b + 1)
                if not isinstance(b, int) or b > 0:
                    dve.wait_ge(turned, b * K)
                nc.vector.tensor_copy(x_q[:, :, :], x_int[:, :, :]).then_inc(x_ready, 1)

            def low(b, k, u):
                dve.wait_ge(hi_done, b * K + k + 1)
                nc.vector.tensor_tensor(xt_lo[u][:, k, :], turn[:, k % 2, :], xt_hi[u][:, k, :], ALU.subtract).then_inc(lo_done, 1)

            float_x(0)
            for k in range(K):
                low(0, k, 0)

            def body(i, b, u, last):
                for j in range(J):
                    if j == 4 and not last:
                        float_x(b + 1)
                    g = u * NG + j // 4
                    dve.wait_ge(evacuated, b * J + j + 5)
                    if j < J // 2:
                        nc.vector.tensor_reduce(gate_max[:, bass.ds(b * (J // 2) + j, 1)], stage[:, g % 4, j % 4, :], AX, ALU.max)
                    nc.vector.tensor_reduce(gu_top[:, j // (J // 2), bass.ds(b * (J // 2) + j % (J // 2), 1)],
                                            stage[:, g % 4, j % 4, :], AX, ALU.max,
                                            apply_absolute_value=True).then_inc(topped, 1)
                    if j in (13, 15, 17, 19) and not last:
                        low(b + 1, (j - 13) // 2, 1 - u)

            pairs(dve, body)


def product_stage(nc, gu, prod, ms, prod_top, kept, NBLK):
    J = HID // P
    NG = J // 4
    F = 4 * TB
    with ExitStack() as ctx:
        def sb(name, dt=F32):
            return ctx.enter_context(nc.sbuf_tensor("pr_" + name, [P, NG, F], dt))

        def sem(name):
            return nc.alloc_semaphore("pr_" + name)

        g_in, u_in, sig, prd = sb("g_in"), sb("u_in"), sb("sig"), sb("prd")
        g_int, s_int, h_int, u_int = sb("g_int", I16), sb("s_int", I32), sb("h_int", I16), sb("u_int", I16)
        loaded_g = [sem(f"loaded_g{s}") for s in range(NG)]
        loaded_u = [sem(f"loaded_u{s}") for s in range(NG)]
        stored = [sem(f"stored{s}") for s in range(NG)]
        g_seen, u_seen = sem("g_seen"), sem("u_seen")
        g_rounded, sig_done, s_rounded, silu_done = sem("g_rounded"), sem("sig_done"), sem("s_rounded"), sem("silu_done")
        h_rounded, u_rounded, prod_done, topped = sem("h_rounded"), sem("u_rounded"), sem("prod_done"), sem("topped")
        block = ctx.enter_context(nc.Block())

        @block.sync
        def _(sp):
            def load(b, s):
                sp.dma_start(g_in[:, s, :], gu[bass.ds(b, 1), :, 4 * s:4 * s + 4, :].rearrange("b p j t -> p (b j t)")).then_inc(loaded_g[s], 16)
                sp.dma_start(u_in[:, s, :], gu[bass.ds(b, 1), :, J + 4 * s:J + 4 * s + 4, :].rearrange("b p j t -> p (b j t)")).then_inc(loaded_u[s], 16)

            def store(b, s):
                sp.wait_ge(topped, b * NG + s + 1)
                sp.dma_start(prod[bass.ds(b, 1), :, 4 * s:4 * s + 4, :].rearrange("b p j t -> p (b j t)"), prd[:, s, :]).then_inc(stored[s], 16)

            for s in range(NG):
                load(0, s)
            for s in range(NG):
                sp.sem_inc(stored[s], 16)
            def reload(b):
                for s in range(NG):
                    sp.wait_ge(g_rounded, b * NG + s + 1)
                    sp.wait_ge(u_rounded, b * NG + s + 1)
                    load(b + 1, s)

            for b in range(len(kept)):
                reload(b)
            with sp.Fori(len(kept), NBLK - 1) as b:
                reload(b)
                for s in range(NG):
                    store(b, s)
            for s in range(NG):
                store(NBLK - 1, s)
            for s in range(NG):
                sp.wait_ge(stored[s], 16 + (NBLK - len(kept)) * 16)

        @block.scalar
        def _(act):
            act.sem_inc(h_rounded, NG)
            with act.Fori(0, NBLK) as b:
                for s in range(NG):
                    act.wait_ge(h_rounded, b * NG + s + 1)
                    act.wait_ge(g_rounded, b * NG + s + 1)
                    nc.scalar.activation(sig[:, s, :], g_int[:, s, :], ACT.Sigmoid, scale=ms[:, 1:2]).then_inc(sig_done, 1)
                    act.wait_ge(sig_done, b * NG + s + 1)
                    nc.scalar.activation(s_int[:, s, :], sig[:, s, :], ACT.Copy, scale=SIG_ONE).then_inc(s_rounded, 1)
                for s in range(NG):
                    act.wait_ge(silu_done, b * NG + s + 1 + NG)
                    nc.scalar.activation(h_int[:, s, :], sig[:, s, :], ACT.Copy, scale=ms[:, 2:3]).then_inc(h_rounded, 1)

        @block.gpsimd
        def _(pool):
            with pool.Fori(0, NBLK) as b:
                for s in range(NG):
                    pool.wait_ge(loaded_g[s], b * 16 + 16)
                    pool.wait_ge(silu_done, b * NG + s + 1)
                    pool.sem_inc(g_seen, 1)
                    nc.gpsimd.tensor_scalar(g_int[:, s, :], g_in[:, s, :], ms[:, 0:1], 1.0, ALU.mult, ALU.mult).then_inc(g_rounded, 1)
                for s in range(NG):
                    pool.wait_ge(loaded_u[s], b * 16 + 16)
                    pool.wait_ge(prod_done, b * NG + s + 1)
                    pool.sem_inc(u_seen, 1)
                    nc.gpsimd.tensor_scalar(u_int[:, s, :], u_in[:, s, :], ms[:, 3:4], 1.0, ALU.mult, ALU.mult).then_inc(u_rounded, 1)

        @block.vector
        def _(dve):
            dve.sem_inc(prod_done, NG)
            dve.sem_inc(silu_done, NG)

            def block_products(b, target):
                for s in range(NG):
                    dve.wait_ge(s_rounded, b * NG + s + 1)
                    nc.vector.scalar_tensor_tensor(sig[:, s, :], s_int[:, s, :], SIG_ONE - 1.0, g_int[:, s, :], ALU.min, ALU.mult).then_inc(silu_done, 1)
                for s in range(NG):
                    dve.wait_ge(h_rounded, b * NG + s + 1 + NG)
                    dve.wait_ge(u_rounded, b * NG + s + 1)
                    if target is prd:
                        dve.wait_ge(stored[s], (b - len(kept)) * 16 + 16)
                    nc.vector.tensor_tensor(target[:, s, :], h_int[:, s, :], u_int[:, s, :], ALU.mult).then_inc(prod_done, 1)
                    dve.wait_ge(prod_done, b * NG + s + 1 + NG)
                    nc.vector.tensor_reduce(prod_top[:, bass.ds(b * NG + s, 1)], target[:, s, :], AX, ALU.max,
                                            apply_absolute_value=True).then_inc(topped, 1)

            for b, tile in enumerate(kept):
                block_products(b, tile[:, :, :].rearrange("p (s j) t -> p s (j t)", s=NG))
            with dve.Fori(len(kept), NBLK) as b:
                block_products(b, prd)


def down_stage(nc, p_in, loaded, prod, x2, out, wd_hi, wd_lo, ms, NBLK):
    J = HID // P
    with ExitStack() as ctx:
        def sb(name, shape, dt=F32):
            return ctx.enter_context(nc.sbuf_tensor("dn_" + name, shape, dt))

        def sem(name):
            return nc.alloc_semaphore("dn_" + name)

        p_int = sb("p_int", [P, 2, J, P], I16)
        o_hi, o_lo = sb("o_hi", [P, 2, J, P], F32R), sb("o_lo", [P, 2, J, P], F32R)
        x_in = sb("x_in", [P, 2, D])
        y = sb("y", [P, 2, D])
        st, mv, var = sb("st", [P, 2, 6]), sb("mv", [P, 2, 2]), sb("var", [P, 2, 1])
        rstd, half = sb("rstd", [P, 2, 1]), sb("half", [P, 1])
        acc = ctx.enter_context(nc.psum_tensor("dn_acc", [P, 4, D], F32))
        s = {n: sem(n) for n in "half_set rounded hi_done lo_done products added stats stats_seen aggr var_done powed normed".split()}
        x_loaded = [sem(f"x_loaded{u}") for u in range(2)]
        stored = [sem(f"stored{u}") for u in range(2)]
        N = 4 * NBLK
        block = ctx.enter_context(nc.Block())

        @block.sync
        def _(sp):
            def load(b, u):
                sp.dma_start(p_in[u][:, :, :], prod[bass.ds(b, 1), :, :, :].rearrange("b p j t -> p (b j) t")).then_inc(loaded[u], 16)

            def load_x(n, b, t):
                wait(sp, s["added"], n - 1)
                sp.dma_start(x_in[:, t % 2, :], x2[bass.ds(b, 1), :, t, :].rearrange("b p d -> p (b d)")).then_inc(x_loaded[t % 2], 16)

            def store(n, b, t):
                sp.wait_ge(s["normed"], n + 1)
                sp.dma_start(out[bass.ds(b, 1), :, t, :].rearrange("b p d -> p (b d)"), y[:, t % 2, :]).then_inc(stored[t % 2], 16)

            def emit(b, u, first, last):
                for t in range(4):
                    load_x(b * 4 + t, b, t)
                    if t == 0 and not first and not last:
                        sp.wait_ge(s["rounded"], b * 4)
                        load(b + 1, 1 - u)
                    if t >= 2:
                        store(b * 4 + t - 2, b, t - 2)
                    elif not first:
                        store(b * 4 + t - 2, b - 1, t + 2)

            batches(sp, NBLK, emit)
            store(N - 2, NBLK - 1, 2)
            store(N - 1, NBLK - 1, 3)
            for u in range(2):
                sp.wait_ge(stored[u], NBLK * 32)

        @block.scalar
        def _(act):
            def emit(b, u, first, last):
                act.wait_ge(loaded[u], (b - u) * 8 + 16)
                for t in range(4):
                    n, r = b * 4 + t, t % 2
                    wait(act, s["lo_done"], n - 1)
                    nc.scalar.activation(p_int[:, r, :, :], p_in[u][:, :, t * P:(t + 1) * P], ACT.Copy, scale=ms[:, 4:5]).then_inc(s["rounded"], 1)
                    act.wait_ge(s["rounded"], n + 1)
                    wait(act, s["products"], n - 1)
                    nc.scalar.activation(o_hi[:, r, :, :], p_int[:, r, :, :], ACT.Copy).then_inc(s["hi_done"], 1)

            batches(act, NBLK, emit)

        @block.tensor
        def _(pe):
            def emit(b, u, first, last):
                for t in range(4):
                    n, r = b * 4 + t, t % 2
                    pe.wait_ge(s["lo_done"], n + 1)
                    wait(pe, s["added"], n - 3)
                    for j in range(J):
                        for m, (o, w) in enumerate(((o_hi, wd_hi), (o_hi, wd_lo), (o_lo, wd_hi))):
                            mm = nc.tensor.matmul(acc[:, t, :], o[:, r, j, :], w[:, j, :],
                                                  start=(j == 0 and m == 0), stop=(j == J - 1 and m == 2))
                    mm.then_inc(s["products"], 1)

            batches(pe, NBLK, emit)

        @block.gpsimd
        def _(pool):
            nc.gpsimd.memset(half[:, :], -0.5).then_inc(s["half_set"], 1)
            pool.wait_ge(s["half_set"], 1)

            def power(n, r):
                pool.wait_ge(s["var_done"], n + 1)
                nc.gpsimd.tensor_tensor(rstd[:, r, :], var[:, r, :], half[:, :], ALU.pow).then_inc(s["powed"], 1)

            def emit(b, u, first, last):
                for t in range(4):
                    power(b * 4 + t, t % 2)

            batches(pool, NBLK, emit)

        @block.vector
        def _(dve):
            def low(n, r):
                dve.wait_ge(s["hi_done"], n + 1)
                nc.vector.tensor_tensor(o_lo[:, r, :, :], p_int[:, r, :, :], o_hi[:, r, :, :], ALU.subtract).then_inc(s["lo_done"], 1)

            def add(n, r, t, residuals):
                dve.wait_ge(s["products"], n + 1)
                dve.wait_ge(x_loaded[r], residuals)
                wait(dve, stored[r], residuals - 16)
                nc.vector.scalar_tensor_tensor(y[:, r, :], acc[:, t, :], ms[:, 5:6], x_in[:, r, :], ALU.mult, ALU.add).then_inc(s["added"], 1)
                dve.wait_ge(s["added"], n + 1)
                nc.vector.bn_stats(st[:, r, :], y[:, r, :]).then_inc(s["stats"], 1)
                dve.wait_ge(s["stats"], n + 1)
                dve.sem_inc(s["stats_seen"], 1)
                nc.vector.bn_aggr(mv[:, r, :], st[:, r, :]).then_inc(s["aggr"], 1)
                dve.wait_ge(s["aggr"], n + 1)
                wait(dve, s["powed"], n - 1)
                nc.vector.tensor_scalar(var[:, r, :], mv[:, r, 1:2], LN_EPS, None, ALU.add).then_inc(s["var_done"], 1)

            def norm(n, r):
                dve.wait_ge(s["powed"], n + 1)
                nc.vector.tensor_scalar(y[:, r, :], y[:, r, :], mv[:, r, 0:1], rstd[:, r, :], ALU.subtract, ALU.mult).then_inc(s["normed"], 1)

            def emit(b, u, first, last):
                for t in range(4):
                    n, r = b * 4 + t, t % 2
                    low(n, r)
                    if not (first and t < 2):
                        norm(n - 2, r)
                    if not (first and t == 0):
                        add(n - 1, 1 - r, (t + 3) % 4, b * 32 + 16 * ((t + 1) // 2))

            batches(dve, NBLK, emit)
            norm(N - 2, 0)
            add(N - 1, 1, 3, 32 * NBLK)
            norm(N - 1, 1)


def ffn_phase(nc, ident, x2, gu, prod, out, w_gate, w_up, w_down, x_top, NBLK):
    J = HID // P
    with ExitStack() as ctx:
        def sb(name, shape, dt=F32):
            return ctx.enter_context(nc.sbuf_tensor("ffn_" + name, shape, dt))

        xs, gs, us, hs, ps = (sb(n, [P, 4]) for n in ("xs", "gs", "us", "hs", "ps"))
        ms = sb("ms", [P, 8])
        gu_top = sb("gu_top", [P, 2, NBLK * J])
        silu_top = sb("silu_top", [P, NBLK * J // 4])
        prod_top = sb("prod_top", [P, NBLK * J // 4])
        gate_max, gp = sb("gate_max", [P, NBLK * J]), sb("gp", [P, 4])
        scale_stage(nc, [(x_top[:, :], xs)], "xs")
        with ExitStack() as c2:
            wg_hi, wg_lo, wu_hi, wu_lo = (c2.enter_context(nc.sbuf_tensor("ffn_" + n, [P, D // P, HID], F32R))
                                          for n in ("wg_hi", "wg_lo", "wu_hi", "wu_lo"))
            x_in = c2.enter_context(nc.sbuf_tensor("ffn_x_in", [P, TB // P, D], F32))
            x_loaded = nc.alloc_semaphore("gu_x_loaded")

            def fetch_x(sp):
                sp.dma_start(x_in[:, :, :], x2[0]).then_inc(x_loaded, 16)

            ffn_weights_stage(nc, ident, [(w_gate, wg_hi, wg_lo), (w_up, wu_hi, wu_lo)], "wgu", fetch_x)
            gate_up_stage(nc, ident, x_in, x_loaded, x2, gu, wg_hi, wg_lo, wu_hi, wu_lo, xs, gu_top, gate_max, NBLK)
        scale_stage(nc, [(gu_top[:, 0, :], gs), (gu_top[:, 1, :], us), (gate_max[:, :], gp)], "gus")
        gate_params_stage(nc, gs, us, ms)
        silu_top_stage(nc, gu, ms, gp, silu_top, NBLK)
        scale_stage(nc, [(silu_top[:, :], hs)], "hs")
        silu_params_stage(nc, hs, us, ms)
        p_in = [sb(f"p_in{u}", [P, J, TB]) for u in range(2)]
        product_stage(nc, gu, prod, ms, prod_top, p_in, NBLK)
        scale_stage(nc, [(prod_top[:, :], ps)], "ps")
        with ExitStack() as c2:
            wd_hi, wd_lo = (c2.enter_context(nc.sbuf_tensor("ffn_" + n, [P, J, D], F32R)) for n in ("wd_hi", "wd_lo"))
            p_loaded = [nc.alloc_semaphore(f"dn_loaded{u}") for u in range(2)]

            def blocks_kept(sp):
                for u in range(2):
                    sp.sem_inc(p_loaded[u], 16)

            ffn_weights_stage(nc, ident, [(w_down, wd_hi, wd_lo)], "wd", blocks_kept)
            down_params_stage(nc, ps, ms)
            down_stage(nc, p_in, p_loaded, prod, x2, out, wd_hi, wd_lo, ms, NBLK)




def gate_params_stage(nc, gs, us, ms):
    with ExitStack() as ctx:
        block = ctx.enter_context(nc.Block())

        @block.vector
        def _(dve):
            nc.vector.tensor_copy(ms[:, 0:1], gs[:, 2:3])
            nc.vector.tensor_copy(ms[:, 1:2], gs[:, 1:2])
            nc.vector.tensor_copy(ms[:, 3:4], us[:, 2:3])


def silu_top_stage(nc, gu, ms, gp, silu_top, NBLK):
    J = HID // P
    NG = J // 4
    F = 4 * TB
    with ExitStack() as ctx:
        def sb(name, shape, dt=F32):
            return ctx.enter_context(nc.sbuf_tensor("st_" + name, shape, dt))

        def sem(name):
            return nc.alloc_semaphore("st_" + name)

        g_in, sig = sb("g_in", [P, NG, F]), sb("sig", [P, NG, F])
        g_int, s_int = sb("g_int", [P, NG, F], I16), sb("s_int", [P, NG, F], U16)
        peak_g, peak_s = sb("peak_g", [P, 1], I16), sb("peak_s", [P, 1], U16)
        peak_sig, peak, low = sb("peak_sig", [P, 1]), sb("peak", [P, 1]), sb("low", [P, 1], I32)
        loaded = [sem(f"loaded{s}") for s in range(NG)]
        g_rounded, sig_done, s_rounded, silu_done, topped = sem("g_rounded"), sem("sig_done"), sem("s_rounded"), sem("silu_done"), sem("topped")
        peak_g_done, peak_sig_done, peak_s_done, peak_done = sem("peak_g_done"), sem("peak_sig_done"), sem("peak_s_done"), sem("peak_done")
        top_set, low_done = sem("top_set"), sem("low_done")
        block = ctx.enter_context(nc.Block())

        @block.sync
        def _(sp):
            def load(b, s):
                sp.dma_start(g_in[:, s, :], gu[bass.ds(b, 1), :, 4 * s:4 * s + 4, :].rearrange("b p j t -> p (b j t)")).then_inc(loaded[s], 16)

            sp.wait_ge(low_done, 1)
            with sp.If(sp.value_load(low[0:1, 0:1], min_val=0, max_val=1) == 1):
                for s in range(NG):
                    load(0, s)
                with sp.Fori(0, NBLK - 1) as b:
                    for s in range(NG):
                        sp.wait_ge(g_rounded, b * NG + s + 1)
                        load(b + 1, s)

        @block.scalar
        def _(act):
            nc.scalar.activation(peak_g[:, :], gp[:, 0:1], ACT.Copy, scale=ms[:, 0:1]).then_inc(peak_g_done, 1)
            act.wait_ge(peak_g_done, 1)
            nc.scalar.activation(peak_sig[:, :], peak_g[:, :], ACT.Sigmoid, scale=ms[:, 1:2]).then_inc(peak_sig_done, 1)
            act.wait_ge(low_done, 1)
            with act.If(act.value_load(low[0:1, 0:1], min_val=0, max_val=1) == 1):
                with act.Fori(0, NBLK) as b:
                    for s in range(NG):
                        act.wait_ge(loaded[s], b * 16 + 16)
                        act.wait_ge(topped, b * NG + s + 1)
                        nc.scalar.activation(g_int[:, s, :], g_in[:, s, :], ACT.Copy, scale=ms[:, 0:1]).then_inc(g_rounded, 1)
                        act.wait_ge(g_rounded, b * NG + s + 1)
                        nc.scalar.activation(sig[:, s, :], g_int[:, s, :], ACT.Sigmoid, scale=ms[:, 1:2]).then_inc(sig_done, 1)

        @block.vector
        def _(dve):
            dve.wait_ge(peak_sig_done, 1)
            nc.vector.tensor_scalar(peak_s[:, :], peak_sig[:, :], SIG_ONE, SIG_ONE - 1.0, ALU.mult, ALU.min).then_inc(peak_s_done, 1)
            dve.wait_ge(peak_s_done, 1)
            nc.vector.scalar_tensor_tensor(peak[:, :], peak_g[:, :], ms[:, 1:2], peak_s[:, :], ALU.mult, ALU.mult).then_inc(peak_done, 1)
            dve.wait_ge(peak_done, 1)
            nc.vector.tensor_copy(silu_top[:, :], peak[:, 0:1].broadcast_to([P, silu_top.shape[1]])).then_inc(top_set, 1)
            nc.vector.tensor_scalar(low[:, :], peak[:, :], SILU_NEG * SIG_ONE, None, ALU.is_lt).then_inc(low_done, 1)
            dve.wait_ge(low_done, 1)
            dve.wait_ge(top_set, 1)
            with dve.If(dve.value_load(low[0:1, 0:1], min_val=0, max_val=1) == 1):
                dve.sem_inc(topped, NG)
                with dve.Fori(0, NBLK) as b:
                    for s in range(NG):
                        dve.wait_ge(sig_done, b * NG + s + 1)
                        nc.vector.tensor_scalar(s_int[:, s, :], sig[:, s, :], SIG_ONE, SIG_ONE - 1.0, ALU.mult, ALU.min).then_inc(s_rounded, 1)
                        dve.wait_ge(s_rounded, b * NG + s + 1)
                        nc.vector.scalar_tensor_tensor(sig[:, s, :], g_int[:, s, :], ms[:, 1:2], s_int[:, s, :], ALU.mult, ALU.mult).then_inc(silu_done, 1)
                        dve.wait_ge(silu_done, b * NG + s + 1)
                        nc.vector.tensor_reduce(silu_top[:, bass.ds(b * NG + s, 1)], sig[:, s, :], AX, ALU.max,
                                                apply_absolute_value=True).then_inc(topped, 1)


def silu_params_stage(nc, hs, us, ms):
    with ExitStack() as ctx:
        step = nc.alloc_semaphore("sp_step")
        block = ctx.enter_context(nc.Block())

        @block.vector
        def _(dve):
            nc.vector.tensor_scalar(ms[:, 6:7], hs[:, 0:1], 1.0 / SIG_ONE / QMAX, 1e-12, ALU.mult, ALU.max).then_inc(step, 1)
            dve.wait_ge(step, 1)
            nc.vector.reciprocal(ms[:, 2:3], ms[:, 6:7]).then_inc(step, 1)
            dve.wait_ge(step, 2)
            nc.vector.tensor_scalar(ms[:, 2:3], ms[:, 2:3], ms[:, 1:2], 1.0 / SIG_ONE, ALU.mult, ALU.mult).then_inc(step, 1)
            nc.vector.tensor_tensor(ms[:, 7:8], ms[:, 6:7], us[:, 1:2], ALU.mult).then_inc(step, 1)
            dve.wait_ge(step, 4)


def down_params_stage(nc, ps, ms):
    with ExitStack() as ctx:
        step = nc.alloc_semaphore("dp_step")
        block = ctx.enter_context(nc.Block())

        @block.vector
        def _(dve):
            nc.vector.tensor_tensor(ms[:, 5:6], ps[:, 0:1], ms[:, 7:8], ALU.mult).then_inc(step, 1)
            dve.wait_ge(step, 1)
            nc.vector.tensor_scalar(ms[:, 5:6], ms[:, 5:6], 1.0 / QMAX, 1e-12, ALU.mult, ALU.max).then_inc(step, 1)
            dve.wait_ge(step, 2)
            nc.vector.reciprocal(ms[:, 4:5], ms[:, 5:6]).then_inc(step, 1)
            dve.wait_ge(step, 3)
            nc.vector.tensor_tensor(ms[:, 4:5], ms[:, 4:5], ms[:, 7:8], ALU.mult).then_inc(step, 1)
            dve.wait_ge(step, 4)


def identity_stage(nc, tiles):
    with ExitStack() as ctx:
        zeroed, filled = nc.alloc_semaphore("id_zeroed"), nc.alloc_semaphore("id_filled")
        block = ctx.enter_context(nc.Block())

        @block.gpsimd
        def _(pool):
            for n, tile in enumerate(tiles):
                nc.gpsimd.memset(tile[:, :], 0.0).then_inc(zeroed, 1)
                pool.wait_ge(zeroed, n + 1)
                nc.gpsimd.affine_select(out=tile[:, :], in_=tile[:, :], compare_op=ALU.not_equal, fill=1.0, base=0,
                                        pattern=[[-1, P]], channel_multiplier=1).then_inc(filled, 1)
            pool.wait_ge(filled, len(tiles))


def bass_infini_decoder(nc, x, x_t, ctx_t, mask, aq, ak, av, ao, beta, xq, bq, xk, bk, xv, bv, xo, bo, w_gate, w_up, w_down, out):
    NB = x.shape[0] // TB
    scratch = {name: nc.dram_tensor(name, shape, F32, kind="Internal").ap() for name, shape in
               (("x1", list(x.shape)), ("x2", list(x.shape)), ("gate_up", [NB, P, 2 * HID // P, TB]), ("product", [NB, P, HID // P, TB]))}

    def tokens(a):
        return a.rearrange("(b t p) d -> b p t d", t=TB // P, p=P)

    def rows(a):
        return a.rearrange("(k p) n -> p k n", p=P)

    with ExitStack() as ctx:
        ident = ctx.enter_context(nc.sbuf_tensor("ident", [P, P], F32))
        identb = ctx.enter_context(nc.sbuf_tensor("identb", [P, P], BF16))
        x_top = ctx.enter_context(nc.sbuf_tensor("x2_top", [P, NB * TB // P], F32))
        identity_stage(nc, (ident, identb))
        with nc.cleanup_on_exit():
            self_phase(nc, ident, identb, tokens(x), x_t, tokens(scratch["x1"]), [rows(w) for w in (aq, ak, av, ao)],
                       beta.broadcast_to([P, beta.shape[1]]), NB)
        with nc.cleanup_on_exit():
            cross_phase(nc, ident, identb, tokens(scratch["x1"]), tokens(scratch["x2"]), ctx_t, mask, [rows(w) for w in (xq, xk, xv, xo)],
                        bq, bk, bv.broadcast_to([P, D]), bo.broadcast_to([P, D]), x_top, NB)
        with nc.cleanup_on_exit():
            ffn_phase(nc, ident, tokens(scratch["x2"]), scratch["gate_up"], scratch["product"], tokens(out),
                      *(w.rearrange("(r p) c -> r p c", p=P) for w in (w_gate, w_up, w_down)), x_top, NB)


def kernel(**inputs):
    import numpy as _np
    import concourse.bacc as _bacc
    from concourse import mybir as _mybir
    from concourse.bass_utils import run_bass_kernel_spmd as _run

    given = {name: _np.asarray(a) for name, a in inputs.items()}
    x = given["x"]
    B, T, width = x.shape
    K, SEG = width // 128, 64
    ctx = given["ctx_1024"]
    C = ctx.shape[1]

    def columns(bias):
        return bias.reshape(K, 128).T

    layouts = {
        "x": x.reshape(B * T, width),
        "x_t": x.reshape(B, T // 128, 2, SEG, width)[:, :, ::-1].reshape(B, T, K, 128).transpose(0, 2, 3, 1),
        "ctx_t": ctx.transpose(0, 2, 1).reshape(B, K, 128, C),
        "mask": given["mask_BxSxS2_bk0"].reshape(B, T // 128, 128, C),
        "aq": given["L0_attn_W_q"].T,
        "ak": given["L0_attn_W_k"].T,
        "av": given["L0_attn_W_v"].T,
        "ao": given["L0_attn_W_o"].T,
        "beta": given["L0_attn_beta_param"][None],
        "xq": given["L0_xattn_Wq"],
        "bq": columns(given["L0_xattn_bq"]),
        "xk": given["L0_xattn_Wk"],
        "bk": columns(given["L0_xattn_bk"]),
        "xv": given["L0_xattn_Wv"],
        "bv": given["L0_xattn_bv"][None],
        "xo": given["L0_xattn_Wo"],
        "bo": given["L0_xattn_bo"][None],
        "w_gate": given["L0_ffn_w_gate"],
        "w_up": given["L0_ffn_w_up"],
        "w_down": given["L0_ffn_w_down"],
    }
    nc = _bacc.Bacc("TRN2", target_bir_lowering=False, num_devices=1)
    arrays, args = {}, []
    for name, a in layouts.items():
        a = _np.ascontiguousarray(a)
        arrays["in_" + name] = a
        args.append(nc.dram_tensor("in_" + name, a.shape, _mybir.dt.from_np(a.dtype), kind="ExternalInput").ap())
    args.append(nc.dram_tensor("out_x", (B * T, width), _mybir.dt.float32, kind="ExternalOutput").ap())
    bass_infini_decoder(nc, *args)
    r = _run(nc, [arrays], core_ids=[0])
    return r.results[0]["out_x"].reshape(B, T, width)
```
